# Optimizing a Trainium2 kernel written in Bass

```python
import numpy as np
import jax
import jax.numpy as jnp

def _softmax(x, axis=-1):
    return jax.nn.softmax(x, axis=axis)

def _gelu(x):
    return jax.nn.gelu(x, approximate=True)

def _silu(x):
    return jax.nn.silu(x)

def _sigmoid(x):
    return jax.nn.sigmoid(x)

def _layernorm(x, axis=-1, eps=1e-05):
    m = jnp.mean(x, axis=axis, keepdims=True)
    v = jnp.var(x, axis=axis, keepdims=True)
    return (x - m) / jnp.sqrt(v + eps)

def _scatter_add(tgt, idx, src, axis=0):
    return tgt.at[idx].add(src)

def _segment_sum(src, seg, n):
    return jax.ops.segment_sum(src, seg, n)
kernel_name = 'mk_gnn_resnorm_d4_gnn_r32_dc1c43'

def setup_inputs(seed: int=0):
    np.random.seed(seed)
    _w = jnp.asarray

    def _rec_inputs():
        import jax
        import jax.numpy as jnp
        _gk = jax.random.key(seed)
        x = -0.0009044 + 1 * jax.random.normal(jax.random.fold_in(_gk, 1), (3125, 32), jnp.float32)
        _s = jax.random.randint(jax.random.fold_in(_gk, 2), (25000,), 0, 3125, jnp.int32)
        _d = jax.random.randint(jax.random.fold_in(_gk, 3), (25000,), 0, 3125, jnp.int32)
        _loop = jnp.arange(3125, dtype=jnp.int32)
        src = jnp.concatenate([_s, _d, _loop])
        dst = jnp.concatenate([_d, _s, _loop])
        _o = jnp.argsort(dst, stable=True)
        src = src[_o]
        dst = dst[_o]
        edge_attr_2 = -5.09086e-05 + 0.577461 * jax.random.normal(jax.random.fold_in(_gk, 12), (53125, 2), jnp.float32)
        return (x, src, dst, edge_attr_2)
    x, src, dst, edge_attr_2 = _rec_inputs()

    def _L0_gnn_setup():
        import jax, jax.numpy as jnp
        import numpy as np
        N_NODES = 50000
        N_EDGES = 25000
        IN_FEATS = 32
        OUT_FEATS = 32
        NUM_HEADS = 4
        key = jax.random.key(seed)
        ks = jax.random.split(key, 12)
        H, F, IN = (NUM_HEADS, OUT_FEATS, IN_FEATS)
        h = jax.random.normal(ks[0], (N_NODES, IN), dtype=jnp.float32)
        src = jax.random.randint(ks[1], (N_EDGES,), 0, N_NODES, dtype=jnp.int64)
        dst = jax.random.randint(ks[2], (N_EDGES,), 0, N_NODES, dtype=jnp.int64)
        s = 0.1
        W_gat = jax.random.normal(ks[3], (IN, H * F), dtype=jnp.float32) * s
        attn_l = jax.random.normal(ks[4], (H, F), dtype=jnp.float32) * s
        attn_r = jax.random.normal(ks[5], (H, F), dtype=jnp.float32) * s
        W_ih = jax.random.normal(ks[6], (3 * F, H * F), dtype=jnp.float32) * s
        W_hh = jax.random.normal(ks[7], (3 * F, F), dtype=jnp.float32) * s
        b_ih = jax.random.normal(ks[8], (3 * F,), dtype=jnp.float32) * s
        b_hh = jax.random.normal(ks[9], (3 * F,), dtype=jnp.float32) * s
        return {'h': h, 'W_gat': W_gat, 'attn_l': attn_l, 'attn_r': attn_r, 'W_ih': W_ih, 'W_hh': W_hh, 'b_ih': b_ih, 'b_hh': b_hh, 'src': src, 'dst': dst}
    _L0_gnn_all = _L0_gnn_setup()
    _L0_gnn_in = {k: v for k, v in _L0_gnn_all.items() if k in ('W_gat', 'attn_l', 'attn_r', 'W_ih', 'W_hh', 'b_ih', 'b_hh')}
    del _L0_gnn_all

    def _L1_gnn_setup():
        import jax, jax.numpy as jnp
        import numpy as np
        N_NODES = 3125
        N_EDGES = 50000
        D = 32
        K = 3
        NEG_SLOPE = 0.2
        key = jax.random.key(seed)
        ks = jax.random.split(key, 10)
        s = 1.0 / np.sqrt(D)
        return {'u': jax.random.normal(ks[0], (N_NODES, D), jnp.float32), 'lambda_max': jnp.full((1,), 2.0, jnp.float32), 'edge_src': jax.random.randint(ks[1], (N_EDGES,), 0, N_NODES, jnp.int32), 'edge_dst': jax.random.randint(ks[2], (N_EDGES,), 0, N_NODES, jnp.int32), 'cheb_W': jax.random.normal(ks[3], (K * D, D), jnp.float32) * s, 'cheb_b': jnp.zeros((D,), jnp.float32), 'src_W': jax.random.normal(ks[4], (D, D), jnp.float32) * s, 'src_b': jnp.zeros((D,), jnp.float32), 'dst_W': jax.random.normal(ks[5], (D, D), jnp.float32) * s, 'dst_b': jnp.zeros((D,), jnp.float32), 'attn': jax.random.normal(ks[6], (1, D), jnp.float32) * s}
    _L1_gnn_all = _L1_gnn_setup()
    _L1_gnn_in = {k: v for k, v in _L1_gnn_all.items() if k in ('lambda_max', 'cheb_W', 'cheb_b', 'src_W', 'src_b', 'dst_W', 'dst_b', 'attn')}
    del _L1_gnn_all

    def _L2_gnn_setup():
        import jax, jax.numpy as jnp
        import numpy as np
        N_NODES = 50000
        N_EDGES = 50000
        F_IN = 32
        F_OUT = 32
        BASIS = (4, 4)

        def _tent_basis(u, n):
            centers = jnp.linspace(-1.0, 1.0, n, dtype=u.dtype)
            h = 2.0 / (n - 1)
            return jnp.maximum(0.0, 1.0 - jnp.abs(u[:, None] - centers[None, :]) / h)
        key = jax.random.key(seed)
        k1, k2, k3, k4, k5 = jax.random.split(key, 5)
        x = jax.random.normal(k1, (N_NODES, F_IN), dtype=jnp.float32)
        edge_attr = jax.random.uniform(k2, (N_EDGES, 2), dtype=jnp.float32, minval=-1.0, maxval=1.0)
        weight = jax.random.uniform(k3, (*BASIS, F_IN, F_OUT), dtype=jnp.float32, minval=-0.05, maxval=0.05)
        src = jax.random.randint(k4, (N_EDGES,), 0, N_NODES)
        tgt = jax.random.randint(k5, (N_EDGES,), 0, N_NODES)
        edge_index = jnp.stack([tgt, src], axis=0).astype(jnp.int64)
        return {'x': x, 'edge_attr': edge_attr, 'weight': weight, 'edge_index': edge_index}
    _L2_gnn_all = _L2_gnn_setup()
    _L2_gnn_in = {k: v for k, v in _L2_gnn_all.items() if k in ('weight',)}
    del _L2_gnn_all

    def _L3_gnn_setup():
        import jax, jax.numpy as jnp
        import numpy as np
        EPS = 1e-12

        def _agnn_conv(x, edge_index, beta):
            N = x.shape[0]
            loops = jnp.arange(N, dtype=edge_index.dtype)
            src = jnp.concatenate([edge_index[0], loops])
            dst = jnp.concatenate([edge_index[1], loops])
            norm = jnp.sqrt(jnp.sum(x * x, axis=-1, keepdims=True))
            x_norm = x / jnp.maximum(norm, EPS)
            alpha = beta[0] * jnp.sum(x_norm[dst] * x_norm[src], axis=-1)
            amax = jax.ops.segment_max(alpha, dst, num_segments=N)
            ex = jnp.exp(alpha - amax[dst])
            denom = jax.ops.segment_sum(ex, dst, num_segments=N)
            w = ex / jnp.maximum(denom[dst], EPS)
            out = jax.ops.segment_sum(w[:, None] * x[src], dst, num_segments=N)
            return out
        key = jax.random.key(seed)
        k1, k2 = jax.random.split(key)
        N, D, E = (50000, 32, 50000)
        x = jax.random.normal(k1, (N, D), dtype=jnp.float32)
        edge_index = jax.random.randint(k2, (2, E), 0, N, dtype=jnp.int64)
        beta = jnp.ones((1,), dtype=jnp.float32)
        return {'x': x, 'edge_index': edge_index, 'beta': beta}
    _L3_gnn_all = _L3_gnn_setup()
    _L3_gnn_in = {k: v for k, v in _L3_gnn_all.items() if k in ('beta',)}
    del _L3_gnn_all
    return {'x': x, 'src': src, 'dst': dst, 'edge_attr_2': edge_attr_2, 'L0_gnn_W_gat': _L0_gnn_in['W_gat'], 'L0_gnn_attn_l': _L0_gnn_in['attn_l'], 'L0_gnn_attn_r': _L0_gnn_in['attn_r'], 'L0_gnn_W_ih': _L0_gnn_in['W_ih'], 'L0_gnn_W_hh': _L0_gnn_in['W_hh'], 'L0_gnn_b_ih': _L0_gnn_in['b_ih'], 'L0_gnn_b_hh': _L0_gnn_in['b_hh'], 'L1_gnn_lambda_max': _L1_gnn_in['lambda_max'], 'L1_gnn_cheb_W': _L1_gnn_in['cheb_W'], 'L1_gnn_cheb_b': _L1_gnn_in['cheb_b'], 'L1_gnn_src_W': _L1_gnn_in['src_W'], 'L1_gnn_src_b': _L1_gnn_in['src_b'], 'L1_gnn_dst_W': _L1_gnn_in['dst_W'], 'L1_gnn_dst_b': _L1_gnn_in['dst_b'], 'L1_gnn_attn': _L1_gnn_in['attn'], 'L2_gnn_weight': _L2_gnn_in['weight'], 'L3_gnn_beta': _L3_gnn_in['beta']}

def reference(x, src, dst, edge_attr_2, L0_gnn_W_gat, L0_gnn_attn_l, L0_gnn_attn_r, L0_gnn_W_ih, L0_gnn_W_hh, L0_gnn_b_ih, L0_gnn_b_hh, L1_gnn_lambda_max, L1_gnn_cheb_W, L1_gnn_cheb_b, L1_gnn_src_W, L1_gnn_src_b, L1_gnn_dst_W, L1_gnn_dst_b, L1_gnn_attn, L2_gnn_weight, L3_gnn_beta):
    import jax
    import jax.numpy as jnp

    def _L0_gnn_ref(h, W_gat, attn_l, attn_r, W_ih, W_hh, b_ih, b_hh, src, dst):
        import jax, jax.numpy as jnp
        import numpy as np
        N_NODES = 50000
        N_EDGES = 25000
        IN_FEATS = 32
        OUT_FEATS = 32
        NUM_HEADS = 4
        N = h.shape[0]
        H, F = attn_l.shape
        feat = (h @ W_gat).reshape(N, H, F)
        el = jnp.einsum('nhf,hf->nh', feat, attn_l)
        er = jnp.einsum('nhf,hf->nh', feat, attn_r)
        e = jax.nn.leaky_relu(el[src] + er[dst], 0.2)
        emax = jax.ops.segment_max(e, dst, num_segments=N)
        ee = jnp.exp(e - emax[dst])
        denom = jax.ops.segment_sum(ee, dst, num_segments=N)
        alpha = ee / denom[dst]
        msg = feat[src] * alpha[:, :, None]
        agg = jax.ops.segment_sum(msg, dst, num_segments=N)
        x = agg.reshape(N, H * F)
        gi = x @ W_ih.T + b_ih
        gh = h @ W_hh.T + b_hh
        i_r, i_z, i_n = jnp.split(gi, 3, axis=1)
        h_r, h_z, h_n = jnp.split(gh, 3, axis=1)
        r = jax.nn.sigmoid(i_r + h_r)
        z = jax.nn.sigmoid(i_z + h_z)
        n = jnp.tanh(i_n + r * h_n)
        h_new = (1.0 - z) * n + z * h
        return jax.nn.elu(h_new)

    def _L1_gnn_ref(u, lambda_max, edge_src, edge_dst, cheb_W, cheb_b, src_W, src_b, dst_W, dst_b, attn):
        import jax, jax.numpy as jnp
        import numpy as np
        N_NODES = 3125
        N_EDGES = 50000
        D = 32
        K = 3
        NEG_SLOPE = 0.2
        N = u.shape[0]
        deg = jnp.zeros((N,), u.dtype).at[edge_dst].add(1.0)
        Dinv = jnp.clip(deg, 1.0, None) ** (-0.5)

        def unnL(x):
            m = (x * Dinv[:, None])[edge_src]
            agg = jax.ops.segment_sum(m, edge_dst, num_segments=N)
            return agg * Dinv[:, None]
        re_norm = 2.0 / lambda_max
        X0 = u
        Xt = [X0]
        X1 = X0
        if K > 1:
            h = unnL(X0)
            X1 = -re_norm * h + X0 * (re_norm - 1.0)
            Xt.append(X1)
        for _ in range(2, K):
            h = unnL(X1)
            Xi = -2.0 * re_norm * h + X1 * (2.0 * (re_norm - 1.0)) - X0
            Xt.append(Xi)
            X0, X1 = (X1, Xi)
        Xcat = jnp.concatenate(Xt, axis=1)
        hc = jax.nn.relu(Xcat @ cheb_W + cheb_b)
        H = attn.shape[0]
        fsrc = (hc @ src_W + src_b).reshape(N, H, -1)
        fdst = (hc @ dst_W + dst_b).reshape(N, H, -1)
        e = jax.nn.leaky_relu(fsrc[edge_src] + fdst[edge_dst], NEG_SLOPE)
        logits = jnp.einsum('ehd,hd->eh', e, attn)
        mx = jax.ops.segment_max(logits, edge_dst, num_segments=N)
        mx = jnp.where(jnp.isfinite(mx), mx, 0.0)
        ex = jnp.exp(logits - mx[edge_dst])
        den = jax.ops.segment_sum(ex, edge_dst, num_segments=N)
        a = ex / jnp.where(den > 0, den, 1.0)[edge_dst]
        msg = fsrc[edge_src] * a[:, :, None]
        out = jax.ops.segment_sum(msg, edge_dst, num_segments=N)
        return out.squeeze(1)

    def _L2_gnn_ref(x, edge_attr, weight, edge_index):
        import jax, jax.numpy as jnp
        import numpy as np
        N_NODES = 50000
        N_EDGES = 50000
        F_IN = 32
        F_OUT = 32
        BASIS = (4, 4)

        def _tent_basis(u, n):
            centers = jnp.linspace(-1.0, 1.0, n, dtype=u.dtype)
            h = 2.0 / (n - 1)
            return jnp.maximum(0.0, 1.0 - jnp.abs(u[:, None] - centers[None, :]) / h)
        k1, k2, f_in, f_out = weight.shape
        n_nodes = x.shape[0]
        bu = _tent_basis(edge_attr[:, 0], k1)
        bv = _tent_basis(edge_attr[:, 1], k2)
        basis = (bu[:, :, None] * bv[:, None, :]).reshape(-1, k1 * k2)
        xj = x[edge_index[1]]
        w2 = weight.reshape(k1 * k2, f_in, f_out)
        msg = basis[:, 0:1] * (xj @ w2[0])
        for k in range(1, k1 * k2):
            msg = msg + basis[:, k:k + 1] * (xj @ w2[k])
        out = jax.ops.segment_sum(msg, edge_index[0], num_segments=n_nodes)
        return out

    def _L3_gnn_ref(x, edge_index, beta):
        import jax, jax.numpy as jnp
        import numpy as np
        EPS = 1e-12

        def _agnn_conv(x, edge_index, beta):
            N = x.shape[0]
            loops = jnp.arange(N, dtype=edge_index.dtype)
            src = jnp.concatenate([edge_index[0], loops])
            dst = jnp.concatenate([edge_index[1], loops])
            norm = jnp.sqrt(jnp.sum(x * x, axis=-1, keepdims=True))
            x_norm = x / jnp.maximum(norm, EPS)
            alpha = beta[0] * jnp.sum(x_norm[dst] * x_norm[src], axis=-1)
            amax = jax.ops.segment_max(alpha, dst, num_segments=N)
            ex = jnp.exp(alpha - amax[dst])
            denom = jax.ops.segment_sum(ex, dst, num_segments=N)
            w = ex / jnp.maximum(denom[dst], EPS)
            out = jax.ops.segment_sum(w[:, None] * x[src], dst, num_segments=N)
            return out
        return x + jax.nn.relu(_agnn_conv(x, edge_index, beta))
    edge_index = jnp.stack([src, dst])
    x = _layernorm(x + _L0_gnn_ref(x, L0_gnn_W_gat, L0_gnn_attn_l, L0_gnn_attn_r, L0_gnn_W_ih, L0_gnn_W_hh, L0_gnn_b_ih, L0_gnn_b_hh, src, dst), axis=-1)
    x = _layernorm(x + _L1_gnn_ref(x, L1_gnn_lambda_max, src, dst, L1_gnn_cheb_W, L1_gnn_cheb_b, L1_gnn_src_W, L1_gnn_src_b, L1_gnn_dst_W, L1_gnn_dst_b, L1_gnn_attn), axis=-1)
    x = _layernorm(x + _L2_gnn_ref(x, edge_attr_2, L2_gnn_weight, edge_index), axis=-1)
    x = _layernorm(x + _L3_gnn_ref(x, edge_index, L3_gnn_beta), axis=-1)
    return x

_drawn_inputs = setup_inputs


def setup_inputs(seed=0):
    import zlib

    import numpy as np

    out = dict(_drawn_inputs(seed))
    spreads = {'L1_gnn_cheb_b': (0.0, 0.1), 'L1_gnn_src_b': (0.0, 0.1), 'L1_gnn_dst_b': (0.0, 0.8)}
    factors = {'L0_gnn_attn_l': 3.702, 'L0_gnn_attn_r': 8.0, 'L0_gnn_b_hh': 3.199}
    for name, (base, spread) in spreads.items():
        noise = np.random.default_rng([zlib.crc32(name.encode()), seed]).standard_normal(out[name].shape)
        drawn = base * np.exp(spread * noise) if base else spread * noise
        out[name] = jnp.asarray(drawn.astype(out[name].dtype))
    for name, factor in factors.items():
        out[name] = (out[name] * factor).astype(out[name].dtype)
    return out
```

```python
from contextlib import ExitStack

import concourse.bass as bass
from concourse import mybir

F32 = mybir.dt.float32
I32 = mybir.dt.int32
BF16 = mybir.dt.bfloat16
F16 = mybir.dt.float16
ALU = mybir.AluOpType
ACT = mybir.ActivationFunctionType
X_AXIS = mybir.AxisListType.X

BIG = 1.0e30
TINY = 1.0e-30
SKIP = 1.0e6
LN_EPS = 1.0e-5
NORM_EPS = 1.0e-12


class Count:

    def __init__(self, n=0):
        self.n = n
        self.reg = None
        self.per = 0

    def up(self, k=1):
        self.n += k
        return self.at()

    def at(self, ahead=0):
        if self.reg is None:
            return self.n + ahead
        return self.reg * self.per + (self.n + ahead)

    def enter(self, reg, per):
        self.reg, self.per, self.first = reg, per, self.n

    def leave(self, turns):
        assert self.n - self.first == self.per, (self.n - self.first, self.per)
        self.n = self.first + self.per * turns
        self.reg = None


def gnn_kernel(nc, x, src, dst, edge_attr, W_gat, attn_l, attn_r, W_ih, W_hh, b_ih, b_hh,
               lambda_max, cheb_W, cheb_b, src_W, src_b, dst_W, dst_b, attn, weight, beta, out):
    N, D = x.shape
    E = src.shape[0]
    H = attn_l.shape[0]
    P = 128
    NP = 125
    J = N // NP
    T = E // NP
    L = 25
    CH = T // L
    TURNS = (CH - 3) // 2
    HG = D + 1
    C0 = H * HG + H
    C1 = HG + 1
    W0 = D + 2 * H
    KV, KU = weight.shape[1], weight.shape[0]
    K2 = KU * KV
    assert K2 * D == 512 and KU == KV == 4 and L == J and H * D == P
    assert N == NP * J and E == NP * T and T == CH * L and CH == 2 * TURNS + 3
    GT = 4
    GROUPS = [range(g, min(g + GT, J)) for g in range(0, J, GT)]
    MID = N // 2
    assert MID <= 2048
    BANK = 512
    SLOT = 16

    with ExitStack() as ctx:
        def sb(name, shape, dt=F32):
            return ctx.enter_context(nc.sbuf_tensor(name, shape, dt))

        def sem(name):
            return ctx.enter_context(nc.semaphore(name))

        def dram(name, shape, dt=F32):
            return nc.dram_tensor(name, shape, dt, kind="Internal").ap()

        tab0_dram = dram("tab0_dram", (N, W0))
        tab_cheb_dram = [dram("tab_cheb0_dram", (N, D)), dram("tab_cheb1_dram", (N, D))]
        tab_fsrc_dram = dram("tab_fsrc_dram", (N, D))
        tab_fdst_dram = dram("tab_fdst_dram", (N, D))
        tab_x2_dram = dram("tab_x2_dram", (N, D))
        tab_x3_dram = dram("tab_x3_dram", (N, HG))
        tab_xn_dram = dram("tab_xn_dram", (N, D))
        starts4_dram = dram("starts4_dram", (P * T, H))
        starts32_dram = dram("starts32_dram", (P * T, D))
        scan0_dram = dram("scan0_dram", (P * T, C0))
        scan1_dram = dram("scan1_dram", (P * T, C1))
        scanD_dram = dram("scanD_dram", (P * T, D))

        dst_i = sb("dst_i", [NP, T], I32)
        fence = sb("fence", [P, 2])
        same = sb("same", [NP, T])
        ident = sb("ident", [P, P])
        ones = sb("ones", [P, P])
        before_qp = sb("before_qp", [P, P])
        before_pq = sb("before_pq", [P, P])
        shift = sb("shift", [P, P])
        carry_qp = sb("carry_qp", [NP, NP])
        carry_pq = sb("carry_pq", [NP, NP])
        no_carry_pq = sb("no_carry_pq", [NP, NP])
        ends = sb("ends", [NP, 4])
        node_i = sb("node_i", [P, J], I32)
        node_f = sb("node_f", [NP, J])
        base_i = sb("base_i", [P, 1], I32)
        base_f = sb("base_f", [NP, 1])
        row_of = sb("row_of", [P, J], I32)
        first_i = sb("first_i", [P, 1], I32)
        end_i = sb("end_i", [P, J], I32)
        start_i = sb("start_i", [P, J], I32)
        mend_get_i = sb("mend_get_i", [P, 1], I32)
        mend_put_i = sb("mend_put_i", [P, 1], I32)
        nodew = sb("nodew", [NP, 13, J])
        idx = sb("idx", [P, 2, L], I32)
        rows = sb("rows", [P, 2, L * W0])
        scan = sb("scan", [P, 2, L * C0])
        edges_d = sb("edges_d", [P, T * D])
        samec = sb("samec", [NP, 2, L])
        brk = sb("brk", [NP, L])
        mrun = sb("mrun", [NP, 2, H, L + 1])
        logit = sb("logit", [NP, H, L])
        rw = sb("rw", [NP, 2, 2, H, L])
        prod = sb("prod", [NP, L, D])
        local = sb("local", [P, C0])
        mended = sb("mended", [P, C0])
        diag = sb("diag", [NP, H, NP])
        cross = sb("cross", [NP, H * NP + H])
        crossT = sb("crossT", [NP, H, NP])
        small = sb("small", [NP, 4, H])
        X = sb("X", [NP, J, D])
        agg = sb("agg", [P, J, C0])
        aggn = sb("aggn", [NP, J, P])
        bigT = sb("bigT", [P, J * NP])
        smallT = sb("smallT", [D + 1, J * NP])
        tab = sb("tab", [P, J, W0])
        scat = sb("scat", [P, J, D])
        work = sb("work", [NP, J, D])
        work2 = sb("work2", [NP, J, D])
        rden = sb("rden", [NP, J, H])
        first_row = sb("first_row", [P, W0])
        attr = sb("attr", [NP, T, 2])
        src_i = sb("src_i", [NP, T], I32)
        src_f = sb("src_f", [NP, T])
        srcc = sb("srcc", [NP, 2, L])
        nodes16 = sb("nodes16", [NP, N], F16)
        stack3 = sb("stack3", [3 * D, D])
        tent = sb("tent", [NP, 2, L, KU])
        basis = sb("basis", [NP, L, KU, KV])
        w_gat = sb("w_gat", [D, P])
        att_lr = sb("att_lr", [D, 2, P])
        w_lr = sb("w_lr", [D, 2 * H])
        w_ih = sb("w_ih", [3 * D, P])
        w_hh = sb("w_hh", [3 * D, D])
        w_ihT = sb("w_ihT", [P, 3 * D])
        w_gatBD = sb("w_gatBD", [P, P])
        w_agg = sb("w_agg", [P, P])
        w_x = sb("w_x", [D + 1, P])
        b_row = sb("b_row", [D + 1, 6 * D])
        w_cheb = sb("w_cheb", [3 * D + 1, D])
        w_sd = sb("w_sd", [D + 1, 2 * D])
        att1 = sb("att1", [NP, D])
        w_spl = sb("w_spl", [P, KU, D])
        scal = sb("scal", [NP, 8])
        ps = ctx.enter_context(nc.psum_tensor("ps", [P, 8, 512], F32))

        consts_made = sem("consts_made")
        scan_cleared = sem("scan_cleared")
        graph_loaded = sem("graph_loaded")
        x_loaded = sem("x_loaded")
        weights_loaded = sem("weights_loaded")
        starts_cleared = sem("starts_cleared")
        vec_done = sem("vec_done")
        vec_for_pe = sem("vec_for_pe")
        pe_for_vec = sem("pe_for_vec")
        group_in_psum = sem("group_in_psum")
        group_copied = sem("group_copied")
        vec_for_act = sem("vec_for_act")
        act_for_vec = sem("act_for_vec")
        vec_for_sync = sem("vec_for_sync")
        vec_for_pool = sem("vec_for_pool")
        table_stored = sem("table_stored")
        dst_rows_in = sem("dst_rows_in")
        scattered = sem("scattered")
        first_in = sem("first_in")
        edges_in = sem("edges_in")
        local_in = sem("local_in")
        agg_in = sem("agg_in")
        idx_in = [sem("idx_in0"), sem("idx_in1")]
        rows_in = [sem("rows_in0"), sem("rows_in1")]
        fence_done = sem("fence_done")
        rows_used = sem("rows_used")
        chunk_scanned = sem("chunk_scanned")
        scan_stored = [sem("scan_stored0"), sem("scan_stored1")]
        edges_filled = sem("edges_filled")
        rows_in_psum = sem("rows_in_psum")
        bx_ready = sem("bx_ready")
        bx_in_psum = sem("bx_in_psum")
        bx_turned = sem("bx_turned")
        msg_in_psum = sem("msg_in_psum")
        msg_moved = sem("msg_moved")
        parts_ready = sem("parts_ready")
        onehot_ready = sem("onehot_ready")
        onehot_used = sem("onehot_used")
        out_stored = sem("out_stored")

        src_grid = src.rearrange("(p t) -> p t", t=T)
        dst_grid = dst.rearrange("(p t) -> p t", t=T)

        def nodes(a):
            return a.rearrange("(p j) c -> p (j c)", j=J)

        PASSES = {
            "gat": (tab0_dram, W0, scan0_dram, C0, H),
            "cheb0": (tab_cheb_dram[0], D, scanD_dram, D, 0),
            "cheb1": (tab_cheb_dram[1], D, scanD_dram, D, 0),
            "gatv2": (tab_fsrc_dram, D, scan1_dram, C1, 1),
            "agnn": (tab_x3_dram, HG, scan1_dram, C1, 1),
        }
        ORDER = list(PASSES)

        def chunks(eng, counts, step):
            before = [c.n for c, per in counts]
            step(0, 0, 0)
            step(1, 1, L)
            counts = [(c, c.n - n if per is None else per) for (c, per), n in zip(counts, before)]
            with eng.Fori(0, TURNS) as turn:
                for c, per in counts:
                    c.enter(turn, per)
                step(2, 0, turn * (2 * L) + 2 * L)
                step(3, 1, turn * (2 * L) + 3 * L)
            for c, per in counts:
                c.leave(TURNS)
            step(CH - 1, 0, (CH - 1) * L)

        bx = aggn[:, :, :].rearrange("p j c -> p (j c)")[:, 0:2 * K2 * D].rearrange("p (s c) -> p s c", s=2)
        bxT = rows[:, 0, 0:2 * KU * NP].rearrange("p (s c) -> p s c", s=2)
        parts = agg[0:NP, :, :].rearrange("p j c -> p (j c)").bitcast(BF16)[:, 0:2 * L * 3 * D]\
            .rearrange("p (b t c) -> p b t c", b=2, t=L)

        def onehot(s):
            return scan[0:NP, s, :].bitcast(BF16)[:, 0:N]

        with nc.Block() as block:

            @block.sync
            def _(sp):
                vec_sync, scanned = Count(), Count()
                gathered = [Count(), Count()]

                sp.dma_start(dst_i[:, :], dst_grid).then_inc(graph_loaded, SLOT)
                sp.dma_start(src_i[:, :], src_grid).then_inc(weights_loaded, SLOT)
                sp.dma_start(X[:, :, :].rearrange("p j c -> p (j c)"), nodes(x)).then_inc(x_loaded, SLOT)
                for t, a in [
                    (w_gat[:, :], W_gat),
                    (att_lr[:, 0, :], attn_l.rearrange("h f -> (h f)").partition_broadcast(D)),
                    (att_lr[:, 1, :], attn_r.rearrange("h f -> (h f)").partition_broadcast(D)),
                    (w_ih[:, :], W_ih),
                    (w_hh[:, :], W_hh),
                    (b_row[D:D + 1, 0:3 * D], b_ih.rearrange("(a n) -> a n", a=1)),
                    (b_row[D:D + 1, 3 * D:6 * D], b_hh.rearrange("(a n) -> a n", a=1)),
                    (w_cheb[0:3 * D, :], cheb_W),
                    (w_cheb[3 * D:3 * D + 1, :], cheb_b.rearrange("(a n) -> a n", a=1)),
                    (w_sd[0:D, 0:D], src_W),
                    (w_sd[0:D, D:2 * D], dst_W),
                    (w_sd[D:D + 1, 0:D], src_b.rearrange("(a n) -> a n", a=1)),
                    (w_sd[D:D + 1, D:2 * D], dst_b.rearrange("(a n) -> a n", a=1)),
                    (att1[:, :], attn.rearrange("h f -> (h f)").partition_broadcast(NP)),
                    (scal[:, 0:1], lambda_max.partition_broadcast(NP)),
                    (scal[:, 1:2], beta.partition_broadcast(NP)),
                    (attr[:, :, :].rearrange("p t c -> p (t c)"), edge_attr.rearrange("(p t) c -> p (t c)", t=T)),
                ]:
                    sp.dma_start(t, a).then_inc(weights_loaded, SLOT)
                for u in range(KU):
                    sp.dma_start(w_spl[:, u, :], weight[u].rearrange("v f o -> (v f) o"))\
                        .then_inc(weights_loaded, SLOT)
                sp.wait_ge(scan_cleared, 1)
                sp.dma_start(starts4_dram.rearrange("(p t) c -> p (t c)", t=T), scan[:, 0, 0:T * H])\
                    .then_inc(starts_cleared, SLOT)
                whole = scan[:, :, :].rearrange("p b c -> p (b c)")
                flat = starts32_dram.rearrange("(p t) c -> p (t c)", t=T)
                for a in range(0, T * D, 2 * L * C0):
                    sp.dma_start(flat[:, a:a + 2 * L * C0], whole).then_inc(starts_cleared, SLOT)

                def store_table(a, t):
                    sp.wait_ge(vec_for_sync, vec_sync.up())
                    sp.dma_start(nodes(a), t).then_inc(table_stored, SLOT)

                def load_edges(a, width, lots):
                    sp.wait_ge(scattered, lots * SLOT)
                    sp.dma_start(edges_d[:, 0:T * width], a.rearrange("(p t) c -> p (t c)", t=T))\
                        .then_inc(edges_in, SLOT)

                def run_pass(name):
                    table, width, scan_dram, C, heads = PASSES[name]
                    grid = scan_dram.rearrange("(p t) c -> p (t c)", t=T)

                    def step(k, b, t0):
                        if gathered[b].n or k >= 2:
                            sp.wait_ge(rows_in[b], gathered[b].at())
                        sp.dma_start(idx[0:NP, b, :], src_grid[:, bass.ds(t0, L)]).then_inc(idx_in[b], SLOT)
                        gathered[b].up(SLOT * L)
                        if k >= 2:
                            store(b, t0 - 2 * L)

                    def store(b, t0):
                        sp.wait_ge(chunk_scanned, scanned.up())
                        sp.dma_start(grid[:, bass.ds(t0 * C, L * C)], scan[:, b, 0:L * C])\
                            .then_inc(scan_stored[b], SLOT)

                    chunks(sp, [(gathered[0], SLOT * L), (gathered[1], SLOT * L), (scanned, 2)], step)
                    store(1, (CH - 2) * L)
                    store(0, (CH - 1) * L)

                tabf = tab[:, :, :].rearrange("p j c -> p (j c)")
                scatf = scat[:, :, :].rearrange("p j c -> p (j c)")
                store_table(tab0_dram, tabf[0:NP, :])
                load_edges(starts4_dram, H, J)
                run_pass("gat")
                store_table(tab_cheb_dram[0], tabf[0:NP, 0:J * D])
                run_pass("cheb0")
                store_table(tab_cheb_dram[1], tabf[0:NP, 0:J * D])
                run_pass("cheb1")
                store_table(tab_fsrc_dram, tabf[0:NP, 0:J * D])
                store_table(tab_fdst_dram, scatf[0:NP, :])
                load_edges(starts32_dram, D, 2 * J + 3)
                run_pass("gatv2")
                store_table(tab_x2_dram, scatf[0:NP, :])
                load_edges(starts32_dram, D, 3 * J + 4)
                store_table(tab_x3_dram, tabf[0:NP, 0:J * HG])
                store_table(tab_xn_dram, scatf[0:NP, :])
                load_edges(starts32_dram, D, 4 * J + 4)
                run_pass("agnn")
                sp.wait_ge(vec_for_sync, vec_sync.up())
                sp.dma_start(nodes(out), X[:, :, :].rearrange("p j c -> p (j c)")).then_inc(out_stored, SLOT)
                sp.wait_ge(out_stored, SLOT)
                for b in range(2):
                    sp.wait_ge(scan_stored[b], len(ORDER) * SLOT * ((CH + 1 - b) // 2))
                sp.wait_ge(table_stored, 8 * SLOT)
                sp.wait_ge(scattered, (4 * J + len(ORDER)) * SLOT)

            @block.gpsimd
            def _(pool):
                vec_pool, used = Count(), Count()
                loaded = [Count(), Count()]
                put = Count()
                fences = Count()
                stored = [Count(), Count()]
                tables = Count()

                pool.memset(ones[:, :], 1.0).then_inc(consts_made, 1)
                pool.memset(row_of[:, :], 0).then_inc(consts_made, 1)
                pool.memset(first_i[:, :], 0).then_inc(consts_made, 1)
                pool.memset(end_i[:, :], 0).then_inc(consts_made, 1)
                pool.memset(start_i[:, :], int(SKIP)).then_inc(consts_made, 1)
                pool.memset(mend_get_i[:, :], 0).then_inc(consts_made, 1)
                pool.memset(mend_put_i[:, :], int(SKIP)).then_inc(consts_made, 1)
                pool.memset(idx[:, :, :], 0).then_inc(consts_made, 1)
                pool.iota(node_i[:, :], [[1, J]], base=0, channel_multiplier=J).then_inc(consts_made, 1)
                pool.iota(base_i[:, :], [[1, 1]], base=0, channel_multiplier=T).then_inc(consts_made, 1)
                pool.iota(nodes16[:, :], [[1, N]], base=-MID, channel_multiplier=0,
                          allow_small_or_imprecise_dtypes=True).then_inc(consts_made, 1)
                pool.wait_ge(consts_made, 11)
                for t, op, base, cm, st in [
                    (ident, ALU.is_equal, 0, 1, -1),
                    (before_qp, ALU.is_gt, 0, -1, 1),
                    (before_pq, ALU.is_gt, 0, 1, -1),
                    (shift, ALU.is_equal, 1, 1, -1),
                ]:
                    pool.affine_select(t[:, :], ones[:, :], [[st, P]], op, 0.0, base=base,
                                       channel_multiplier=cm).then_inc(consts_made, 1)

                def gather(o, table, index, s):
                    pool.indirect_dma_start(o, None, table, bass.IndirectOffsetOnAxis(index, 0)).then_inc(s, SLOT)

                def scatter(table, index, rows_, last):
                    pool.indirect_dma_start(table, bass.IndirectOffsetOnAxis(index, 0), rows_, None,
                                            bounds_check=last, oob_is_err=False).then_inc(scattered, SLOT)
                    put.up(SLOT)

                def scatter_starts(a, c):
                    for j in range(J):
                        scatter(a, start_i[:, j:j + 1], scat[:, j, 0:c], E - 1)

                def run_pass(name):
                    table, width, scan_dram, C, heads = PASSES[name]
                    n = ORDER.index(name)

                    if heads:
                        free, count = rows_used, used
                    else:
                        free, count = chunk_scanned, Count(n * CH)

                    def step(k, b, t0):
                        pool.wait_ge(idx_in[b], loaded[b].up(SLOT))
                        if k >= 2:
                            pool.wait_ge(free, count.up())
                        if fences.n:
                            pool.wait_ge(fence_done, fences.at())
                        pool.tensor_tensor(fence[:, b:b + 1], ones[:, 0:1], ones[:, 1:2], ALU.add)\
                            .then_inc(fence_done, 1)
                        fences.up()
                        for t in range(L):
                            gather(rows[:, b, t * width:(t + 1) * width], table, idx[:, b, t:t + 1], rows_in[b])

                    chunks(pool, [(loaded[0], SLOT), (loaded[1], SLOT), (count, 2), (fences, 2)], step)
                    count.up(2)
                    for b in range(2):
                        pool.wait_ge(scan_stored[b], stored[b].up(SLOT * ((CH + 1 - b) // 2)))
                    gather(local[:, 0:C], scan_dram, mend_get_i[:, 0:1], local_in)
                    pool.wait_ge(vec_for_pool, vec_pool.up())
                    scatter(scan_dram, mend_put_i[:, 0:1], mended[:, 0:C], E - 1)
                    pool.wait_ge(scattered, put.at())
                    for j in range(J):
                        gather(agg[:, j, 0:C], scan_dram, end_i[:, j:j + 1], agg_in)

                pool.wait_ge(vec_for_pool, vec_pool.up())
                for j in range(J):
                    gather(edges_d[:, j * T:(j + 1) * T].bitcast(I32), dst_grid, row_of[:, j:j + 1], dst_rows_in)
                pool.wait_ge(table_stored, tables.up(SLOT))
                gather(first_row[:, 0:W0], tab0_dram, first_i[:, 0:1], first_in)
                pool.wait_ge(vec_for_pool, vec_pool.up())
                pool.wait_ge(starts_cleared, SLOT * (1 + T * D // (2 * L * C0)))
                scatter_starts(starts4_dram, H)
                run_pass("gat")
                for name in ("cheb0", "cheb1"):
                    pool.wait_ge(table_stored, tables.up(SLOT))
                    run_pass(name)
                pool.wait_ge(vec_for_sync, 5)
                scatter_starts(starts32_dram, D)
                pool.wait_ge(table_stored, tables.up(2 * SLOT))
                gather(first_row[:, 0:D], tab_fdst_dram, first_i[:, 0:1], first_in)
                run_pass("gatv2")
                pool.wait_ge(vec_for_sync, 6)
                scatter_starts(starts32_dram, D)
                pool.wait_ge(table_stored, tables.up(SLOT))
                gather(first_row[:, 0:D], tab_x2_dram, first_i[:, 0:1], first_in)
                pool.wait_ge(vec_for_sync, 8)
                scatter_starts(starts32_dram, D)
                pool.wait_ge(table_stored, tables.up(2 * SLOT))
                gather(first_row[:, 0:D], tab_xn_dram, first_i[:, 0:1], first_in)
                run_pass("agnn")

            @block.tensor
            def _(pe):
                operand, group, copied = Count(), Count(), Count()

                def in_groups(product):
                    for tiles in GROUPS:
                        n = group.n
                        if n >= 2:
                            pe.wait_ge(group_copied, n - 1)
                        for a, j in enumerate(tiles):
                            ins = product(ps[:, n % 2, :], a, j)
                        ins.then_inc(group_in_psum, 1)
                        group.up()

                def all_copied():
                    pe.wait_ge(group_copied, group.n)

                def tile_T(t, j):
                    return t[:, j * NP:(j + 1) * NP]

                def mend(name):
                    table, width, scan_dram, C, heads = PASSES[name]
                    if heads == 0:
                        pe.wait_ge(chunk_scanned, (ORDER.index(name) + 1) * CH)
                        pe.matmul(ps[0:NP, 6, 0:C], carry_qp[:, :], scan[0:NP, 0, (L - 1) * C:L * C],
                                  start=True, stop=True).then_inc(pe_for_vec, 1)
                        return
                    pe.wait_ge(vec_for_pe, operand.up())
                    for h in range(heads):
                        ins = pe.matmul(ps[0:NP, 6, h * NP:(h + 1) * NP], ones[0:NP, 0:NP], diag[:, h, :],
                                        start=True, stop=True)
                    ins.then_inc(pe_for_vec, 1)
                    pe.wait_ge(vec_for_pe, operand.up())
                    for h in range(heads):
                        ins = pe.transpose(ps[0:NP, 7, h * NP:(h + 1) * NP], cross[:, h * NP:(h + 1) * NP],
                                           ident[0:NP, 0:NP])
                    ins.then_inc(pe_for_vec, 1)
                    pe.wait_ge(vec_for_pe, operand.up())
                    for h in range(heads):
                        at = (L - 1) * C + h * HG
                        ins = pe.matmul(ps[0:NP, 6, h * HG:(h + 1) * HG], crossT[:, h, :],
                                        scan[0:NP, 0, at:at + HG], start=True, stop=True)
                    ins.then_inc(pe_for_vec, 1)

                def spline_messages():
                    made, turned = Count(), Count()
                    moved = Count()

                    def messages(b, t):
                        s = (L * b + t) % 2
                        pe.wait_ge(bx_turned, turned.up())
                        bank, at = 4 + 2 * b + t // 16, (t % 16) * D
                        for u in range(KU):
                            ins = pe.matmul(ps[0:NP, bank, at:at + D], bxT[:, s, u * NP:(u + 1) * NP],
                                            w_spl[:, u, :], start=(u == 0), stop=(u == KU - 1))
                        ins.then_inc(msg_in_psum, 1)

                    def step(k, b, t0):
                        if k >= 2:
                            pe.wait_ge(msg_moved, moved.up())
                        for t in range(L):
                            s = (L * b + t) % 2
                            pe.wait_ge(bx_ready, made.up())
                            for u in range(KU):
                                ins = pe.transpose(ps[:, s, u * NP:(u + 1) * NP],
                                                   bx[:, s, u * KV * D:(u + 1) * KV * D], ident[0:NP, 0:NP])
                            ins.then_inc(bx_in_psum, 1)
                            if t >= 1:
                                messages(b, t - 1)
                        messages(b, L - 1)

                    chunks(pe, [(made, 2 * L), (turned, 2 * L), (moved, 2)], step)

                def sum_into_sources():
                    hot, part = Count(), Count()

                    def step(k, b, t0):
                        pe.wait_ge(parts_ready, part.up())
                        for t in range(L):
                            s = (L * b + t) % 2
                            pe.wait_ge(onehot_ready, hot.up())
                            for at in range(0, N, BANK):
                                n = min(BANK, N - at)
                                ins = pe.matmul(ps[0:3 * D, at // BANK, 0:n], parts[:, b, t, :],
                                                onehot(s)[:, at:at + n], start=(k == 0 and t == 0),
                                                stop=(k == CH - 1 and t == L - 1))
                            ins.then_inc(onehot_used, 1)

                    chunks(pe, [(hot, 2 * L), (part, 2)], step)

                pe.wait_ge(consts_made, 15)
                pe.wait_ge(weights_loaded, SLOT * (18 + KU))
                pe.transpose(ps[:, 2, 0:3 * D], w_ih[:, :], ident[0:3 * D, 0:3 * D])
                pe.transpose(ps[:, 2, 3 * D:4 * D], w_gat[:, :], ident[0:D, 0:D])
                pe.transpose(ps[0:D, 3, 0:3 * D], w_hh[:, :], ident[0:3 * D, 0:3 * D]).then_inc(pe_for_vec, 1)
                pe.wait_ge(x_loaded, SLOT)
                in_groups(lambda bank, a, j: pe.transpose(bank[0:D, a * NP:(a + 1) * NP], X[:, j, :],
                                                          ident[0:NP, 0:NP]))
                pe.wait_ge(vec_for_pe, operand.up())
                pe.matmul(ps[0:NP, 4, 0:NP], ones[0:NP, 0:NP], diag[:, 0, :], start=True, stop=True)
                pe.matmul(ps[0:NP, 4, NP:2 * NP], ones[0:NP, 0:NP], diag[:, 1, :], start=True, stop=True)\
                    .then_inc(pe_for_vec, 1)
                pe.wait_ge(vec_for_pe, operand.up())
                pe.matmul(ps[:, 5, 0:3 * D], w_gatBD[:, :], w_ihT[:, :], start=True, stop=True)\
                    .then_inc(pe_for_vec, 1)
                pe.wait_ge(vec_for_pe, operand.up())
                all_copied()
                for j in range(J):
                    ins = pe.matmul(ps[0:NP, 3, j * 2 * H:(j + 1) * 2 * H], tile_T(smallT, j)[0:D, :], w_lr[:, :],
                                    start=True, stop=True)
                ins.then_inc(pe_for_vec, 1)
                pe.wait_ge(vec_for_pe, operand.up())
                pe.matmul(ps[0:NP, 4, 2 * NP:2 * NP + 1], shift[0:NP, 0:NP], nodew[:, 0, J - 1:J],
                          start=True, stop=True).then_inc(pe_for_vec, 1)

                mend("gat")
                pe.wait_ge(vec_for_pe, operand.up())
                in_groups(lambda bank, a, j: pe.transpose(bank[:, a * NP:(a + 1) * NP], aggn[:, j, :],
                                                          ident[0:NP, 0:NP]))
                all_copied()

                def gates(bank, a, j):
                    pe.matmul(bank[0:NP, a * P:(a + 1) * P], tile_T(bigT, j), w_agg[:, :], start=True, stop=False)
                    return pe.matmul(bank[0:NP, a * P:(a + 1) * P], tile_T(smallT, j), w_x[:, :],
                                     start=False, stop=True)

                in_groups(gates)
                mend("cheb0")
                mend("cheb1")
                pe.wait_ge(vec_for_pe, operand.up())
                in_groups(lambda bank, a, j: pe.transpose(bank[0:3 * D, a * NP:(a + 1) * NP],
                                                          aggn[:, j, 0:3 * D], ident[0:NP, 0:NP]))
                all_copied()
                in_groups(lambda bank, a, j: pe.matmul(bank[0:D, a * NP:(a + 1) * NP], w_cheb[:, :],
                                                       bigT[0:3 * D + 1, j * NP:(j + 1) * NP],
                                                       start=True, stop=True))
                all_copied()
                in_groups(lambda bank, a, j: pe.matmul(bank[0:NP, a * 2 * D:(a + 1) * 2 * D], tile_T(smallT, j),
                                                       w_sd[:, :], start=True, stop=True))
                mend("gatv2")
                all_copied()
                spline_messages()
                sum_into_sources()
                pe.wait_ge(vec_for_pe, operand.up())
                in_groups(lambda bank, a, j: pe.matmul(bank[0:NP, a * D:(a + 1) * D],
                                                       bigT[0:3 * D, j:N:J], stack3[:, :], start=True, stop=True))
                mend("agnn")

            @block.scalar
            def _(act):
                group, arg, value = Count(), Count(), Count()

                def copy_groups(place, source, func=ACT.Copy):
                    for tiles in GROUPS:
                        bank = ps[:, group.n % 2, :]
                        act.wait_ge(group_in_psum, group.up())
                        nc.scalar.activation(place(tiles), source(bank, len(tiles)), func)\
                            .then_inc(group_copied, 1)

                def apply(func, t):
                    act.wait_ge(vec_for_act, arg.up())
                    nc.scalar.activation(t, t, func).then_inc(act_for_vec, 1)

                def columns(tiles):
                    return slice(tiles[0] * NP, (tiles[-1] + 1) * NP)

                def softmax_pass(heads):
                    def step(k, b, t0):
                        apply(ACT.Exp, rw[:, b, :, 0:heads, :])
                    chunks(act, [(arg, 2)], step)
                    apply(ACT.Exp, cross[:, 0:heads * NP + heads])

                def layer_norm():
                    apply(ACT.Sqrt, nodew[:, 7, :])

                copy_groups(lambda tiles: smallT[0:D, columns(tiles)], lambda bank, n: bank[0:D, 0:n * NP])
                apply(ACT.Sqrt, nodew[:, 4, :])
                softmax_pass(H)
                copy_groups(lambda tiles: bigT[:, columns(tiles)], lambda bank, n: bank[:, 0:n * NP])
                copy_groups(lambda tiles: aggn[:, tiles[0]:tiles[-1] + 1, :].rearrange("p j c -> p (j c)"),
                            lambda bank, n: bank[0:NP, 0:n * P])
                act.wait_ge(group_copied, group.n)
                nc.scalar.activation(aggn[:, :, 0:2 * D], aggn[:, :, 0:2 * D], ACT.Sigmoid).then_inc(act_for_vec, 1)
                apply(ACT.Tanh, work[:, :, :])
                apply(ACT.Exp, work2[:, :, :])
                layer_norm()
                copy_groups(lambda tiles: bigT[0:3 * D, columns(tiles)], lambda bank, n: bank[0:3 * D, 0:n * NP])
                copy_groups(lambda tiles: smallT[0:D, columns(tiles)], lambda bank, n: bank[0:D, 0:n * NP], ACT.Relu)
                copy_groups(lambda tiles: aggn[:, tiles[0]:tiles[-1] + 1, 0:2 * D],
                            lambda bank, n: bank[0:NP, 0:n * 2 * D].rearrange("p (j c) -> p j c", j=n))
                softmax_pass(1)
                layer_norm()

                made, in_psum, used = Count(), Count(), Count()
                act.wait_ge(edges_filled, 1)

                def step(k, b, t0):
                    if k:
                        act.wait_ge(bx_ready, made.at())
                    made.up(L)
                    for at in (0, 16):
                        n = min(16, L - at)
                        ins = nc.scalar.activation(ps[0:NP, 2 + at // 16, 0:n * D],
                                                   edges_d[0:NP, bass.ds(t0 * D + at * D, n * D)], ACT.Copy)
                    ins.then_inc(rows_in_psum, 1)
                    for t in range(L):
                        s = (L * b + t) % 2
                        act.wait_ge(bx_in_psum, in_psum.up())
                        if k or t >= 2:
                            act.wait_ge(msg_in_psum, used.up())
                        nc.scalar.activation(bxT[:, s, :], ps[:, s, 0:KU * NP], ACT.Copy)\
                            .then_inc(bx_turned, 1)

                chunks(act, [(made, 2 * L), (in_psum, 2 * L), (used, 2 * L)], step)
                copy_groups(lambda tiles: work2[:, tiles[0]:tiles[-1] + 1, :],
                            lambda bank, n: bank[0:NP, 0:n * D].rearrange("p (j c) -> p j c", j=n))
                layer_norm()
                apply(ACT.Sqrt, nodew[:, 7, :])
                softmax_pass(1)
                apply(ACT.Exp, nodew[:, 0:2, :])
                layer_norm()

            @block.vector
            def _(vec):
                own = Count()
                pe_n, group_n, act_n = Count(), Count(), Count()
                gathered, stored = [Count(), Count()], [Count(), Count()]
                scanned = Count()
                edges_n, first_n, local_n, agg_n = Count(), Count(), Count(), Count()
                CUM, PREV, DEG, SOME, DINV, DSOME, MEAN, RSTD, RN, ROW, CNT, TMP, SELF = range(13)

                def per_node(slot):
                    return nodew[:, slot, :]

                def over(a, n):
                    return a.unsqueeze(len(a.shape)).broadcast_to(list(a.shape) + [n])

                def settle():
                    vec.wait_ge(vec_done, own.up())

                vec.memset(scan[:, :, :], 0.0).then_inc(scan_cleared, 1)
                vec.memset(mended[:, :], 0.0)
                vec.memset(scat[:, :, :], 0.0)
                vec.memset(w_agg[:, :], 0.0)
                vec.memset(w_gatBD[:, :], 0.0)
                vec.memset(w_x[:, :], 0.0)
                vec.memset(smallT[D:D + 1, :], 1.0)
                vec.memset(same[:, 0:1], 0.0).then_inc(vec_done, 1)
                settle()

                vec.wait_ge(graph_loaded, SLOT)
                vec.wait_ge(consts_made, 15)
                vec.tensor_copy(ends[:, 0:1], dst_i[:, 0:1])
                vec.tensor_copy(first_i[0:NP, :], dst_i[:, 0:1])
                vec.tensor_copy(node_f[:, :], node_i[0:NP, :])
                vec.tensor_copy(base_f[:, :], base_i[0:NP, :])
                vec.tensor_copy(ends[:, 1:2], dst_i[:, T - 1:T]).then_inc(vec_done, 1)
                settle()
                for i in range(2):
                    ins = vec.tensor_scalar(diag[:, i, :], ident[0:NP, 0:NP], ends[:, i:i + 1], None, ALU.mult)
                ins.then_inc(vec_for_pe, 1)
                vec.tensor_tensor(same[:, 1:T], dst_i[:, 1:T], dst_i[:, 0:T - 1], ALU.is_equal)

                vec.wait_ge(weights_loaded, SLOT * (18 + KU))
                vec.tensor_scalar(src_f[:, :], src_i[:, :], -float(MID), None, ALU.add)
                for i in range(3):
                    vec.tensor_copy(stack3[i * D:(i + 1) * D, :], ident[i * D:(i + 1) * D, i * D:(i + 1) * D])
                vec.wait_ge(pe_for_vec, pe_n.up())
                vec.tensor_copy(w_ihT[:, :], ps[:, 2, 0:3 * D])
                for h in range(H):
                    ins = vec.tensor_copy(w_gatBD[h * D:(h + 1) * D, h * D:(h + 1) * D],
                                          ps[h * D:(h + 1) * D, 2, 3 * D:4 * D])
                ins.then_inc(vec_for_pe, 1)
                vec.tensor_tensor(att_lr[:, :, :], att_lr[:, :, :],
                                  w_gat[:, :].unsqueeze(1).broadcast_to([D, 2, P]), ALU.mult).then_inc(vec_done, 1)
                settle()
                vec.tensor_reduce(w_lr[:, :], att_lr[:, :, :].rearrange("p s (h f) -> p (s h) f", h=H), X_AXIS, ALU.add)
                vec.tensor_copy(w_x[0:D, 0:2 * D], ps[0:D, 3, 0:2 * D])
                vec.tensor_copy(w_x[0:D, 3 * D:4 * D], ps[0:D, 3, 2 * D:3 * D])
                vec.tensor_tensor(w_x[D:D + 1, 0:2 * D], b_row[D:D + 1, 0:2 * D], b_row[D:D + 1, 3 * D:5 * D], ALU.add)
                vec.tensor_copy(w_x[D:D + 1, 2 * D:3 * D], b_row[D:D + 1, 2 * D:3 * D])
                vec.tensor_copy(w_x[D:D + 1, 3 * D:4 * D], b_row[D:D + 1, 5 * D:6 * D]).then_inc(vec_for_pe, 1)
                vec.reciprocal(scal[:, 7:8], scal[:, 0:1]).then_inc(vec_done, 1)
                settle()
                vec.tensor_scalar(scal[:, 2:3], scal[:, 7:8], 2.0, None, ALU.mult)
                vec.tensor_scalar(scal[:, 3:4], scal[:, 7:8], -2.0, None, ALU.mult)
                vec.tensor_scalar(scal[:, 4:5], scal[:, 7:8], 2.0, -1.0, ALU.mult, ALU.add)
                vec.tensor_scalar(scal[:, 5:6], scal[:, 7:8], -4.0, None, ALU.mult)
                vec.tensor_scalar(scal[:, 6:7], scal[:, 7:8], 4.0, -2.0, ALU.mult, ALU.add)

                vec.wait_ge(pe_for_vec, pe_n.up())
                firsts, lasts = ps[0:NP, 4, 0:NP], ps[0:NP, 4, NP:2 * NP]
                vec.scalar_tensor_tensor(carry_qp[:, :], firsts, ends[:, 1:2], before_qp[0:NP, 0:NP],
                                         ALU.is_equal, ALU.mult)
                vec.scalar_tensor_tensor(carry_pq[:, :], lasts, ends[:, 0:1], before_pq[0:NP, 0:NP],
                                         ALU.is_equal, ALU.mult)
                upto = edges_d[0:NP, 0:J * NP].rearrange("p (j q) -> p j q", j=J)
                vec.tensor_tensor(upto, over(node_f[:, :], NP), firsts.unsqueeze(1).broadcast_to([NP, J, NP]),
                                  ALU.is_ge).then_inc(vec_done, 1)
                settle()
                vec.tensor_scalar(no_carry_pq[:, :], carry_pq[:, :], -1.0, BIG, ALU.add, ALU.mult)
                vec.tensor_reduce(per_node(CNT), upto, X_AXIS, ALU.add).then_inc(vec_done, 1)
                settle()
                vec.tensor_scalar(per_node(ROW), per_node(CNT), -1.0, 0.0, ALU.add, ALU.max).then_inc(vec_done, 1)
                settle()
                vec.tensor_copy(row_of[0:NP, :], per_node(ROW)).then_inc(vec_for_pool, 1)

                vec.wait_ge(pe_for_vec, pe_n.up())
                vec.tensor_copy(w_agg[:, 0:3 * D], ps[:, 5, 0:3 * D])

                vec.wait_ge(x_loaded, SLOT)
                vec.wait_ge(pe_for_vec, pe_n.up())
                lr = ps[0:NP, 3, 0:J * 2 * H].rearrange("p (j c) -> p j c", j=J)
                vec.tensor_copy(tab[0:NP, :, 0:D], X[:, :, :])
                vec.tensor_copy(scat[0:NP, :, 0:H], lr[:, :, H:2 * H])
                vec.tensor_copy(tab[0:NP, :, D:W0], lr).then_inc(vec_for_sync, 1)

                flat = work[:, :, :].rearrange("p j c -> p (j c)")[:, 0:T]
                vec.tensor_scalar(flat, dst_i[:, :], ends[:, 0:1], None, ALU.is_equal).then_inc(vec_done, 1)
                settle()
                vec.tensor_reduce(ends[:, 2:3], flat, X_AXIS, ALU.add).then_inc(vec_done, 1)
                settle()
                vec.scalar_tensor_tensor(ends[:, 3:4], ends[:, 2:3], -1.0, base_f[:, :], ALU.add, ALU.add)\
                    .then_inc(vec_done, 1)
                settle()
                vec.tensor_copy(mend_get_i[0:NP, :], ends[:, 3:4])
                vec.tensor_copy(mend_put_i[0:NP, :], ends[:, 3:4])

                vec.wait_ge(dst_rows_in, J * SLOT)
                there = edges_d[0:NP, 0:J * T].bitcast(I32).rearrange("p (j t) -> p j t", j=J)
                upto = edges_d[0:NP, 0:J * T].rearrange("p (j t) -> p j t", j=J)
                vec.tensor_tensor(upto, there, over(node_f[:, :], T), ALU.is_le).then_inc(vec_done, 1)
                settle()
                vec.tensor_reduce(per_node(CNT), upto, X_AXIS, ALU.add).then_inc(vec_done, 1)
                settle()
                vec.scalar_tensor_tensor(per_node(CUM), per_node(ROW), float(T), per_node(CNT), ALU.mult, ALU.add)\
                    .then_inc(vec_for_pe, 1)
                vec.wait_ge(vec_for_pe, 4)
                vec.tensor_copy(nodew[:, PREV, 1:J], nodew[:, CUM, 0:J - 1])
                vec.wait_ge(pe_for_vec, pe_n.up())
                vec.tensor_copy(nodew[:, PREV, 0:1], ps[0:NP, 4, 2 * NP:2 * NP + 1]).then_inc(vec_done, 1)
                settle()
                vec.tensor_tensor(per_node(DEG), per_node(CUM), per_node(PREV), ALU.subtract).then_inc(vec_done, 1)
                settle()
                vec.tensor_scalar(per_node(CNT), per_node(CUM), -1.0, 0.0, ALU.add, ALU.max)
                vec.tensor_scalar(per_node(SOME), per_node(DEG), 1.0, None, ALU.min)
                vec.tensor_scalar(per_node(DINV), per_node(DEG), 1.0, None, ALU.max).then_inc(vec_for_act, 1)
                vec.wait_ge(vec_for_act, 1)
                vec.tensor_scalar(per_node(TMP), per_node(SOME), -SKIP, SKIP, ALU.mult, ALU.add).then_inc(vec_done, 1)
                settle()
                vec.tensor_tensor(per_node(TMP), per_node(TMP), per_node(PREV), ALU.add).then_inc(vec_done, 1)
                settle()
                vec.tensor_copy(end_i[0:NP, :], per_node(CNT))
                vec.tensor_copy(start_i[0:NP, :], per_node(TMP)).then_inc(vec_for_pool, 1)
                vec.wait_ge(act_for_vec, act_n.up())
                vec.reciprocal(per_node(DINV), per_node(DINV)).then_inc(vec_done, 1)
                settle()
                vec.tensor_tensor(per_node(DSOME), per_node(DINV), per_node(SOME), ALU.mult)

                def fill_edges(width, at, filled=vec_done):
                    ed = edges_d[0:NP, 0:T * width].rearrange("p (t c) -> p t c", c=width)
                    vec.wait_ge(edges_in, edges_n.up(SLOT))
                    vec.wait_ge(first_in, first_n.up(SLOT))
                    vec.tensor_copy(ed[:, 0, :], first_row[0:NP, at:at + width]).then_inc(vec_done, 1)
                    settle()
                    for c in range(width):
                        ins = vec.tensor_tensor_scan(ed[:, :, c], same[:, :], ed[:, :, c], 0.0, ALU.mult, ALU.add)
                    ins.then_inc(filled, 1)
                    if filled is vec_done:
                        settle()

                def scan_rows(b, C, cols, keep, source):
                    z = scan[0:NP, b, 0:L * C].rearrange("p (t c) -> p t c", c=C)
                    if scanned.n:
                        vec.wait_ge(chunk_scanned, scanned.at())
                    for c in range(cols):
                        at = (L - 1) * C + c
                        ins = vec.tensor_tensor_scan(z[:, :, c], keep(c), source(z, c),
                                                     scan[0:NP, 1 - b, at:at + 1], ALU.mult, ALU.add)
                    ins.then_inc(chunk_scanned, 1)
                    scanned.up()

                def buffer_free(k, b):
                    if stored[b].n or k >= 2:
                        vec.wait_ge(scan_stored[b], stored[b].at())
                    stored[b].up(SLOT)

                def softmax_pass(name, logits):
                    table, width, scan_dram, C, heads = PASSES[name]
                    vec.memset(mrun[:, 1, :, L:L + 1], -BIG).then_inc(vec_done, 1)
                    settle()

                    def step(k, b, t0):
                        r = rows[0:NP, b, 0:L * width].rearrange("p (t w) -> p t w", w=width)
                        z = scan[0:NP, b, 0:L * C].rearrange("p (t c) -> p t c", c=C)
                        vec.wait_ge(rows_in[b], gathered[b].up(SLOT * L))
                        vec.tensor_scalar(brk[:, :], same[:, bass.ds(t0, L)], -1.0, BIG, ALU.add, ALU.mult)
                        logits(r, t0)
                        vec.tensor_copy(mrun[:, b, 0:heads, 0:1], mrun[:, 1 - b, 0:heads, L:L + 1])
                        for h in range(heads):
                            ins = vec.tensor_tensor_scan(mrun[:, b, h, 1:L + 1], brk[:, :], logit[:, h, :],
                                                         mrun[:, 1 - b, h, L:L + 1], ALU.add, ALU.max)
                        ins.then_inc(vec_done, 1)
                        settle()
                        m_now, m_before = mrun[:, b, 0:heads, 1:L + 1], mrun[:, b, 0:heads, 0:L]
                        vec.tensor_tensor(rw[:, b, 1, 0:heads, :], logit[:, 0:heads, :], m_now, ALU.subtract)
                        vec.tensor_tensor(rw[:, b, 0, 0:heads, :], m_before, m_now, ALU.subtract).then_inc(vec_done, 1)
                        settle()
                        vec.tensor_tensor(rw[:, b, 0, 0:heads, :], rw[:, b, 0, 0:heads, :],
                                          brk[:, :].unsqueeze(1).broadcast_to([NP, heads, L]), ALU.add)\
                            .then_inc(vec_for_act, 1)
                        buffer_free(k, b)
                        zh = z[:, :, 0:heads * HG].rearrange("p t (h g) -> p t h g", g=HG)
                        vec.tensor_copy(z[:, :, heads * HG:C], m_now.rearrange("p h t -> p t h"))
                        vec.wait_ge(act_for_vec, act_n.up())
                        w = rw[:, b, 1, 0:heads, :].rearrange("p h t -> p t h")
                        vec.tensor_copy(zh[:, :, :, D], w)
                        vec.tensor_tensor(zh[:, :, :, 0:D], over(w, D),
                                          r[:, :, 0:D].unsqueeze(2).broadcast_to([NP, L, heads, D]), ALU.mult)\
                            .then_inc(rows_used, 1)
                        vec.wait_ge(rows_used, used.up())
                        scan_rows(b, C, heads * HG, lambda c: rw[:, b, 0, c // HG, :], lambda z, c: z[:, :, c])

                    chunks(vec, [(gathered[0], SLOT * L), (gathered[1], SLOT * L), (own, None), (act_n, 2),
                                 (stored[0], SLOT), (stored[1], SLOT), (used, 2), (scanned, 2)], step)

                    for h in range(heads):
                        ins = vec.tensor_scalar(diag[:, h, :], ident[0:NP, 0:NP], mrun[:, 0, h, L:L + 1], None,
                                                ALU.mult)
                    ins.then_inc(vec_for_pe, 1)
                    cr = cross[:, 0:heads * NP].rearrange("p (h q) -> p h q", h=heads)
                    ps6 = ps[0:NP, 6, 0:heads * NP].rearrange("p (h q) -> p h q", h=heads)
                    vec.wait_ge(pe_for_vec, pe_n.up())
                    vec.tensor_tensor(cr, ps6, carry_pq[:, :].unsqueeze(1).broadcast_to([NP, heads, NP]), ALU.mult)\
                        .then_inc(vec_done, 1)
                    settle()
                    vec.tensor_tensor(cr, cr, no_carry_pq[:, :].unsqueeze(1).broadcast_to([NP, heads, NP]), ALU.add)\
                        .then_inc(vec_done, 1)
                    settle()
                    vec.tensor_reduce(small[:, 0, 0:heads], cr, X_AXIS, ALU.max).then_inc(vec_done, 1)
                    settle()
                    m_local = local[0:NP, heads * HG:C]
                    vec.wait_ge(local_in, local_n.up(SLOT))
                    vec.tensor_tensor(small[:, 1, 0:heads], small[:, 0, 0:heads], m_local, ALU.max)\
                        .then_inc(vec_done, 1)
                    settle()
                    vec.tensor_tensor(cross[:, heads * NP:heads * NP + heads], m_local, small[:, 1, 0:heads],
                                      ALU.subtract)
                    vec.tensor_tensor(cr, cr, over(small[:, 1, 0:heads], NP), ALU.subtract).then_inc(vec_for_act, 1)
                    vec.wait_ge(act_for_vec, act_n.up())
                    vec.tensor_copy(mended[0:NP, heads * HG:C], small[:, 1, 0:heads])
                    me = mended[0:NP, 0:heads * HG].rearrange("p (h g) -> p h g", g=HG)
                    vec.tensor_tensor(me, local[0:NP, 0:heads * HG].rearrange("p (h g) -> p h g", g=HG),
                                      over(cross[:, heads * NP:heads * NP + heads], HG), ALU.mult)\
                        .then_inc(vec_for_pe, 1)
                    vec.wait_ge(pe_for_vec, pe_n.up())
                    vec.tensor_copy(crossT[:, 0:heads, :],
                                    ps[0:NP, 7, 0:heads * NP].rearrange("p (h q) -> p h q", h=heads))\
                        .then_inc(vec_for_pe, 1)
                    vec.wait_ge(pe_for_vec, pe_n.up())
                    vec.tensor_tensor(mended[0:NP, 0:heads * HG], mended[0:NP, 0:heads * HG],
                                      ps[0:NP, 6, 0:heads * HG], ALU.add).then_inc(vec_for_pool, 1)
                    vec.wait_ge(agg_in, agg_n.up(J * SLOT))

                def finish_sums():
                    vec.wait_ge(pe_for_vec, pe_n.up())
                    vec.wait_ge(local_in, local_n.up(SLOT))
                    vec.tensor_tensor(mended[0:NP, 0:D], local[0:NP, 0:D], ps[0:NP, 6, 0:D], ALU.add)\
                        .then_inc(vec_for_pool, 1)
                    vec.wait_ge(agg_in, agg_n.up(J * SLOT))

                def sum_pass(name):
                    def step(k, b, t0):
                        r = rows[0:NP, b, 0:L * D].rearrange("p (t w) -> p t w", w=D)
                        vec.tensor_scalar(samec[:, b, :], same[:, bass.ds(t0, L)], 1.0, None, ALU.mult)\
                            .then_inc(vec_done, 1)
                        settle()
                        buffer_free(k, b)
                        vec.wait_ge(rows_in[b], gathered[b].up(SLOT * L))
                        scan_rows(b, D, D, lambda c: samec[:, b, :], lambda z, c: r[:, :, c])

                    chunks(vec, [(gathered[0], SLOT * L), (gathered[1], SLOT * L), (own, None),
                                 (stored[0], SLOT), (stored[1], SLOT), (scanned, 2)], step)
                    finish_sums()

                def divide(heads):
                    a = agg[0:NP, :, 0:heads * HG].rearrange("p j (h g) -> p j h g", g=HG)
                    rd = rden[:, :, 0:heads]
                    vec.tensor_scalar(rd, a[:, :, :, D], TINY, None, ALU.max).then_inc(vec_done, 1)
                    settle()
                    vec.reciprocal(rd, rd).then_inc(vec_done, 1)
                    settle()
                    vec.tensor_tensor(rd, rd, over(per_node(SOME), heads), ALU.mult).then_inc(vec_done, 1)
                    settle()
                    return a[:, :, :, 0:D], over(rd, D)

                def layer_norm(last=False):
                    vec.tensor_reduce(per_node(MEAN), X[:, :, :], X_AXIS, ALU.add).then_inc(vec_done, 1)
                    settle()
                    vec.tensor_scalar(per_node(MEAN), per_node(MEAN), 1.0 / D, None, ALU.mult).then_inc(vec_done, 1)
                    settle()
                    vec.tensor_tensor(X[:, :, :], X[:, :, :], over(per_node(MEAN), D), ALU.subtract)\
                        .then_inc(vec_done, 1)
                    settle()
                    vec.tensor_tensor(work[:, :, :], X[:, :, :], X[:, :, :], ALU.mult).then_inc(vec_done, 1)
                    settle()
                    vec.tensor_reduce(per_node(RSTD), work[:, :, :], X_AXIS, ALU.add).then_inc(vec_done, 1)
                    settle()
                    vec.tensor_scalar(per_node(RSTD), per_node(RSTD), 1.0 / D, LN_EPS, ALU.mult, ALU.add)\
                        .then_inc(vec_for_act, 1)
                    vec.wait_ge(act_for_vec, act_n.up())
                    vec.reciprocal(per_node(RSTD), per_node(RSTD)).then_inc(vec_done, 1)
                    settle()
                    vec.tensor_tensor(X[:, :, :], X[:, :, :], over(per_node(RSTD), D), ALU.mult)\
                        .then_inc(vec_for_sync if last else vec_done, 1)
                    if not last:
                        settle()

                used = Count()
                tabD = tab[:, :, :].rearrange("p j c -> p (j c)")[0:NP, 0:J * D].rearrange("p (j c) -> p j c", c=D)
                tabG = tab[:, :, :].rearrange("p j c -> p (j c)")[0:NP, 0:J * HG].rearrange("p (j c) -> p j c", c=HG)

                fill_edges(H, D + H)

                def gat_logits(r, t0):
                    ed = edges_d[0:NP, bass.ds(t0 * H, L * H)].rearrange("p (t h) -> p h t", h=H)
                    vec.tensor_tensor(logit[:, :, :], r[:, :, D:D + H].rearrange("p t h -> p h t"), ed, ALU.add)\
                        .then_inc(vec_done, 1)
                    settle()
                    vec.scalar_tensor_tensor(logit[:, :, :], logit[:, :, :], 0.2, logit[:, :, :], ALU.mult, ALU.max)\
                        .then_inc(vec_done, 1)
                    settle()

                softmax_pass("gat", gat_logits)
                num, rd = divide(H)
                vec.tensor_tensor(aggn[:, :, :].rearrange("p j (h f) -> p j h f", h=H), num, rd, ALU.mult)\
                    .then_inc(vec_for_pe, 1)
                vec.wait_ge(group_copied, group_n.up(3 * len(GROUPS)))
                vec.wait_ge(act_for_vec, act_n.up())
                vec.tensor_tensor(work[:, :, :], aggn[:, :, 0:D], aggn[:, :, 3 * D:4 * D], ALU.mult)\
                    .then_inc(vec_done, 1)
                settle()
                vec.tensor_tensor(work[:, :, :], work[:, :, :], aggn[:, :, 2 * D:3 * D], ALU.add)\
                    .then_inc(vec_for_act, 1)
                vec.wait_ge(act_for_vec, act_n.up())
                vec.tensor_tensor(work2[:, :, :], X[:, :, :], work[:, :, :], ALU.subtract).then_inc(vec_done, 1)
                settle()
                vec.tensor_tensor(work2[:, :, :], work2[:, :, :], aggn[:, :, D:2 * D], ALU.mult).then_inc(vec_done, 1)
                settle()
                vec.tensor_tensor(work[:, :, :], work[:, :, :], work2[:, :, :], ALU.add).then_inc(vec_done, 1)
                settle()
                vec.tensor_scalar(work2[:, :, :], work[:, :, :], 0.0, None, ALU.min).then_inc(vec_for_act, 1)
                vec.wait_ge(act_for_vec, act_n.up())
                vec.scalar_tensor_tensor(work[:, :, :], work[:, :, :], 0.0, work2[:, :, :], ALU.max, ALU.add)\
                    .then_inc(vec_done, 1)
                settle()
                vec.scalar_tensor_tensor(X[:, :, :], work[:, :, :], -1.0, X[:, :, :], ALU.add, ALU.add)\
                    .then_inc(vec_done, 1)
                settle()
                layer_norm()

                vec.tensor_copy(aggn[:, :, 0:D], X[:, :, :])
                vec.memset(bigT[3 * D:3 * D + 1, :], 1.0)
                vec.tensor_tensor(tabD, X[:, :, :], over(per_node(DINV), D), ALU.mult).then_inc(vec_for_sync, 1)
                sum_pass("cheb0")
                vec.tensor_tensor(work[:, :, :], agg[0:NP, :, 0:D], over(per_node(DSOME), D), ALU.mult)
                vec.tensor_scalar(work2[:, :, :], X[:, :, :], scal[:, 4:5], None, ALU.mult).then_inc(vec_done, 1)
                settle()
                vec.scalar_tensor_tensor(aggn[:, :, D:2 * D], work[:, :, :], scal[:, 3:4], work2[:, :, :],
                                         ALU.mult, ALU.add).then_inc(vec_done, 1)
                settle()
                vec.tensor_tensor(tabD, aggn[:, :, D:2 * D], over(per_node(DINV), D), ALU.mult)\
                    .then_inc(vec_for_sync, 1)
                sum_pass("cheb1")
                vec.tensor_tensor(work[:, :, :], agg[0:NP, :, 0:D], over(per_node(DSOME), D), ALU.mult)
                vec.scalar_tensor_tensor(work2[:, :, :], aggn[:, :, D:2 * D], scal[:, 6:7], X[:, :, :],
                                         ALU.mult, ALU.subtract).then_inc(vec_done, 1)
                settle()
                vec.scalar_tensor_tensor(aggn[:, :, 2 * D:3 * D], work[:, :, :], scal[:, 5:6], work2[:, :, :],
                                         ALU.mult, ALU.add).then_inc(vec_for_pe, 1)
                vec.wait_ge(group_copied, group_n.up(3 * len(GROUPS)))
                vec.tensor_copy(tabD, aggn[:, :, 0:D]).then_inc(vec_for_sync, 1)
                vec.tensor_copy(scat[0:NP, :, :], aggn[:, :, D:2 * D]).then_inc(vec_for_sync, 1)
                fill_edges(D, 0)

                def gatv2_logits(r, t0):
                    ed = edges_d[0:NP, bass.ds(t0 * D, L * D)].rearrange("p (t c) -> p t c", c=D)
                    vec.tensor_tensor(prod[:, :, :], r, ed, ALU.add).then_inc(vec_done, 1)
                    settle()
                    vec.scalar_tensor_tensor(prod[:, :, :], prod[:, :, :], 0.2, prod[:, :, :], ALU.mult, ALU.max)\
                        .then_inc(vec_done, 1)
                    settle()
                    vec.tensor_tensor(prod[:, :, :], prod[:, :, :], att1[:, :].unsqueeze(1).broadcast_to([NP, L, D]),
                                      ALU.mult).then_inc(vec_done, 1)
                    settle()
                    vec.tensor_reduce(logit[:, 0, :], prod[:, :, :], X_AXIS, ALU.add).then_inc(vec_done, 1)
                    settle()

                softmax_pass("gatv2", gatv2_logits)
                num, rd = divide(1)
                vec.tensor_tensor(work[:, :, :], num[:, :, 0, :], rd[:, :, 0, :], ALU.mult).then_inc(vec_done, 1)
                settle()
                vec.tensor_tensor(X[:, :, :], X[:, :, :], work[:, :, :], ALU.add).then_inc(vec_done, 1)
                settle()
                layer_norm()

                vec.tensor_copy(scat[0:NP, :, :], X[:, :, :]).then_inc(vec_for_sync, 1)
                fill_edges(D, 0, edges_filled)
                vec.wait_ge(edges_filled, 1)
                rows_n, turned, msgs = Count(), Count(), Count()

                def spline_step(k, b, t0):
                    for i in range(KU):
                        centre, width = -1.0 + 2.0 * i / (KU - 1), 2.0 / (KU - 1)
                        ins = vec.tensor_scalar(tent[:, :, :, i],
                                                attr[:, bass.ds(t0, L), :].rearrange("p t c -> p c t"),
                                                centre, 1.0 / width, ALU.subtract, ALU.mult)
                    ins.then_inc(vec_done, 1)
                    settle()
                    vec.scalar_tensor_tensor(tent[:, :, :, :], tent[:, :, :, :], -1.0, tent[:, :, :, :],
                                             ALU.mult, ALU.max).then_inc(vec_done, 1)
                    settle()
                    vec.tensor_scalar(tent[:, :, :, :], tent[:, :, :, :], -1.0, 1.0, ALU.mult, ALU.add)\
                        .then_inc(vec_done, 1)
                    settle()
                    vec.tensor_scalar(tent[:, :, :, :], tent[:, :, :, :], 0.0, None, ALU.max).then_inc(vec_done, 1)
                    settle()
                    vec.tensor_tensor(basis[:, :, :, :], over(tent[:, 0, :, :], KV),
                                      tent[:, 1, :, :].unsqueeze(2).broadcast_to([NP, L, KU, KV]), ALU.mult)\
                        .then_inc(vec_done, 1)
                    settle()
                    vec.wait_ge(rows_in_psum, rows_n.up())
                    for t in range(L):
                        s = (L * b + t) % 2
                        if k or t >= 2:
                            vec.wait_ge(bx_in_psum, turned.up())
                        xs = ps[0:NP, 2 + t // 16, (t % 16) * D:(t % 16 + 1) * D]
                        vec.tensor_tensor(bx[:, s, :].rearrange("p (k f) -> p k f", f=D),
                                          xs.unsqueeze(1).broadcast_to([NP, K2, D]),
                                          over(basis[:, t, :, :].rearrange("p u v -> p (u v)"), D), ALU.mult)\
                            .then_inc(bx_ready, 1)
                    msg = ps[0:NP, 4 + 2 * b:6 + 2 * b, :].rearrange("p n c -> p (n c)")[:, 0:L * D]
                    vec.wait_ge(msg_in_psum, msgs.up(L))
                    vec.tensor_scalar(edges_d[0:NP, bass.ds(t0 * D, L * D)], msg, 1.0, None, ALU.mult)\
                        .then_inc(msg_moved, 1)

                chunks(vec, [(own, None), (rows_n, 2), (turned, 2 * L), (msgs, 2 * L)], spline_step)

                vec.wait_ge(msg_moved, CH)
                for b in range(2):
                    vec.wait_ge(scan_stored[b], stored[b].n)
                hot_used = Count()

                def source_step(k, b, t0):
                    high, mid, low = (parts[:, b, :, i * D:(i + 1) * D] for i in range(3))
                    msg = edges_d[0:NP, bass.ds(t0 * D, L * D)].rearrange("p (t c) -> p t c", c=D)
                    vec.tensor_scalar(prod[:, :, :], msg, 1.0, None, ALU.mult)
                    vec.tensor_scalar(srcc[:, b, :], src_f[:, bass.ds(t0, L)], 1.0, None, ALU.mult)\
                        .then_inc(vec_done, 1)
                    settle()
                    vec.tensor_copy(high, prod[:, :, :]).then_inc(vec_done, 1)
                    settle()
                    vec.tensor_tensor(prod[:, :, :], prod[:, :, :], high, ALU.subtract).then_inc(vec_done, 1)
                    settle()
                    vec.tensor_copy(mid, prod[:, :, :]).then_inc(vec_done, 1)
                    settle()
                    vec.tensor_tensor(prod[:, :, :], prod[:, :, :], mid, ALU.subtract).then_inc(vec_done, 1)
                    settle()
                    vec.tensor_copy(low, prod[:, :, :]).then_inc(parts_ready, 1)
                    for t in range(L):
                        s = (L * b + t) % 2
                        if k or t >= 2:
                            vec.wait_ge(onehot_used, hot_used.up())
                        vec.tensor_scalar(onehot(s), nodes16[:, :], srcc[:, b, t:t + 1], None, ALU.is_equal)\
                            .then_inc(onehot_ready, 1)

                chunks(vec, [(own, None), (hot_used, 2 * L)], source_step)
                vec.wait_ge(onehot_used, T)
                vec.tensor_copy(bigT[0:3 * D, :], ps[0:3 * D, 0:7, :].rearrange("p n c -> p (n c)")[:, 0:N])\
                    .then_inc(vec_for_pe, 1)
                vec.wait_ge(group_copied, group_n.up(len(GROUPS)))
                vec.tensor_tensor(X[:, :, :], X[:, :, :], work2[:, :, :], ALU.add).then_inc(vec_done, 1)
                settle()
                layer_norm()

                vec.tensor_tensor(work[:, :, :], X[:, :, :], X[:, :, :], ALU.mult).then_inc(vec_done, 1)
                settle()
                vec.tensor_reduce(per_node(RSTD), work[:, :, :], X_AXIS, ALU.add).then_inc(vec_for_act, 1)
                vec.wait_ge(act_for_vec, act_n.up())
                vec.tensor_scalar(per_node(RN), per_node(RSTD), NORM_EPS, None, ALU.max).then_inc(vec_done, 1)
                settle()
                vec.reciprocal(per_node(RN), per_node(RN)).then_inc(vec_done, 1)
                settle()
                vec.tensor_copy(tabG[:, :, 0:D], X[:, :, :])
                vec.tensor_copy(tabG[:, :, D:HG], over(per_node(RN), 1)).then_inc(vec_for_sync, 1)
                vec.tensor_tensor(scat[0:NP, :, :], X[:, :, :], over(per_node(RN), D), ALU.mult)\
                    .then_inc(vec_for_sync, 1)
                vec.wait_ge(vec_for_sync, 8)
                vec.tensor_tensor(work[:, :, :], scat[0:NP, :, :], scat[0:NP, :, :], ALU.mult).then_inc(vec_done, 1)
                settle()
                vec.tensor_reduce(per_node(TMP), work[:, :, :], X_AXIS, ALU.add).then_inc(vec_done, 1)
                settle()
                vec.tensor_scalar(per_node(SELF), per_node(TMP), scal[:, 1:2], None, ALU.mult)
                fill_edges(D, 0)

                def agnn_logits(r, t0):
                    ed = edges_d[0:NP, bass.ds(t0 * D, L * D)].rearrange("p (t c) -> p t c", c=D)
                    vec.tensor_tensor(prod[:, :, :], r[:, :, 0:D], ed, ALU.mult).then_inc(vec_done, 1)
                    settle()
                    vec.tensor_reduce(logit[:, 0, :], prod[:, :, :], X_AXIS, ALU.add).then_inc(vec_done, 1)
                    settle()
                    vec.scalar_tensor_tensor(logit[:, 0, :], logit[:, 0, :], scal[:, 1:2], r[:, :, D],
                                             ALU.mult, ALU.mult).then_inc(vec_done, 1)
                    settle()

                softmax_pass("agnn", agnn_logits)
                vec.tensor_tensor(per_node(TMP), agg[0:NP, :, HG], per_node(SOME), ALU.mult)
                vec.tensor_scalar(per_node(MEAN), per_node(SOME), -1.0, BIG, ALU.add, ALU.mult).then_inc(vec_done, 1)
                settle()
                vec.tensor_tensor(per_node(TMP), per_node(TMP), per_node(MEAN), ALU.add).then_inc(vec_done, 1)
                settle()
                vec.tensor_tensor(per_node(MEAN), per_node(TMP), per_node(SELF), ALU.max).then_inc(vec_done, 1)
                settle()
                vec.tensor_tensor(nodew[:, 0, :], per_node(TMP), per_node(MEAN), ALU.subtract)
                vec.tensor_tensor(nodew[:, 1, :], per_node(SELF), per_node(MEAN), ALU.subtract).then_inc(vec_for_act, 1)
                vec.wait_ge(act_for_vec, act_n.up())
                vec.tensor_tensor(work[:, :, :], agg[0:NP, :, 0:D], over(nodew[:, 0, :], D), ALU.mult)
                vec.tensor_tensor(work2[:, :, :], X[:, :, :], over(nodew[:, 1, :], D), ALU.mult)
                vec.tensor_tensor(per_node(TMP), agg[0:NP, :, D], nodew[:, 0, :], ALU.mult).then_inc(vec_done, 1)
                settle()
                vec.tensor_tensor(work[:, :, :], work[:, :, :], work2[:, :, :], ALU.add)
                vec.tensor_tensor(per_node(TMP), per_node(TMP), nodew[:, 1, :], ALU.add).then_inc(vec_done, 1)
                settle()
                vec.tensor_scalar(per_node(TMP), per_node(TMP), NORM_EPS, None, ALU.max).then_inc(vec_done, 1)
                settle()
                vec.reciprocal(per_node(TMP), per_node(TMP)).then_inc(vec_done, 1)
                settle()
                vec.tensor_tensor(work[:, :, :], work[:, :, :], over(per_node(TMP), D), ALU.mult).then_inc(vec_done, 1)
                settle()
                vec.scalar_tensor_tensor(work[:, :, :], work[:, :, :], 0.0, X[:, :, :], ALU.max, ALU.add)\
                    .then_inc(vec_done, 1)
                settle()
                vec.tensor_tensor(X[:, :, :], X[:, :, :], work[:, :, :], ALU.add).then_inc(vec_done, 1)
                settle()
                layer_norm(last=True)


_INS = ["x", "src", "dst", "edge_attr_2", "L0_gnn_W_gat", "L0_gnn_attn_l", "L0_gnn_attn_r", "L0_gnn_W_ih",
        "L0_gnn_W_hh", "L0_gnn_b_ih", "L0_gnn_b_hh", "L1_gnn_lambda_max", "L1_gnn_cheb_W", "L1_gnn_cheb_b",
        "L1_gnn_src_W", "L1_gnn_src_b", "L1_gnn_dst_W", "L1_gnn_dst_b", "L1_gnn_attn", "L2_gnn_weight",
        "L3_gnn_beta"]


def kernel(**inputs):
    import numpy as np
    import concourse.bacc as bacc
    from concourse import mybir as mb
    from concourse.bass_utils import run_bass_kernel_spmd

    nc = bacc.Bacc("TRN2", target_bir_lowering=False, num_devices=1)
    arrays, args = {}, []
    for name in _INS:
        a = np.ascontiguousarray(inputs[name])
        arrays[f"in_{name}"] = a
        args.append(nc.dram_tensor(f"in_{name}", a.shape, mb.dt.from_np(a.dtype), kind="ExternalInput").ap())
    shape = inputs["x"].shape
    out = nc.dram_tensor("out", shape, mb.dt.float32, kind="ExternalOutput").ap()
    gnn_kernel(nc, *args, out)
    r = run_bass_kernel_spmd(nc, [arrays], core_ids=[0])
    return r.results[0]["out"]
```

```python
from contextlib import ExitStack

import concourse.bass as bass
from concourse import mybir

F32 = mybir.dt.float32
I32 = mybir.dt.int32
BF16 = mybir.dt.bfloat16
F16 = mybir.dt.float16
ALU = mybir.AluOpType
ACT = mybir.ActivationFunctionType
X_AXIS = mybir.AxisListType.X

BIG = 1.0e30
TINY = 1.0e-30
SKIP = 1.0e6
LN_EPS = 1.0e-5
NORM_EPS = 1.0e-12


class Count:

    def __init__(self, n=0):
        self.n = n
        self.reg = None
        self.per = 0

    def up(self, k=1):
        self.n += k
        return self.at()

    def at(self, ahead=0):
        if self.reg is None:
            return self.n + ahead
        return self.reg * self.per + (self.n + ahead)

    def enter(self, reg, per):
        self.reg, self.per, self.first = reg, per, self.n

    def leave(self, turns):
        assert self.n - self.first == self.per, (self.n - self.first, self.per)
        self.n = self.first + self.per * turns
        self.reg = None


def gnn_kernel(nc, x, src, dst, edge_attr, W_gat, attn_l, attn_r, W_ih, W_hh, b_ih, b_hh,
               lambda_max, cheb_W, cheb_b, src_W, src_b, dst_W, dst_b, attn, weight, beta, out):
    N, D = x.shape
    E = src.shape[0]
    H = attn_l.shape[0]
    P = 128
    NP = 125
    J = N // NP
    T = E // NP
    L = 25
    CH = T // L
    TURNS = (CH - 5) // 2
    HG = D + 1
    C0 = H * HG + H
    C1 = HG + 1
    W0 = D + 2 * H
    KV, KU = weight.shape[1], weight.shape[0]
    K2 = KU * KV
    CELLS = KU - 1
    CORNERS = 4
    YROW = CELLS * CELLS * CORNERS * D
    assert K2 * D == 512 and KU == KV == 4 and L == J and H * D == P
    assert N == NP * J and E == NP * T and T == CH * L and CH == 2 * TURNS + 5
    WIDTH = 2.0 / (KU - 1)
    assert KU == 4
    GT = 4
    GROUPS = [range(g, min(g + GT, J)) for g in range(0, J, GT)]
    MID = N // 2
    assert MID <= 2048
    BANK = 512
    LS = 5
    SLOTS = L // LS
    BLOCKS = J // LS
    ACT_HOT = [(c, t) for c in range(SLOTS) for t in range(LS) if t == 4]
    PE_COLS = {"gat": 8, "cheb0": 10, "cheb1": 10, "gatv2": 9, "agnn": 10}
    PE_MOST = max(PE_COLS.values())
    PG = 4
    SLOT = 16

    with ExitStack() as ctx:
        def sb(name, shape, dt=F32):
            return ctx.enter_context(nc.sbuf_tensor(name, shape, dt))

        def sem(name):
            return ctx.enter_context(nc.semaphore(name))

        def dram(name, shape, dt=F32):
            return nc.dram_tensor(name, shape, dt, kind="Internal").ap()

        tab0_dram = dram("tab0_dram", (N, W0))
        tab_cheb_dram = [dram("tab_cheb0_dram", (N, D)), dram("tab_cheb1_dram", (N, D))]
        tab_fsrc_dram = dram("tab_fsrc_dram", (N, D))
        tab_fdst_dram = dram("tab_fdst_dram", (N, D))
        tab_y_dram = dram("tab_y_dram", (N * CELLS * CELLS, CORNERS * D))
        cell_dram = dram("cell_dram", (E,), I32)
        srcT_dram = dram("srcT_dram", (T, NP), F16)
        tab_x3_dram = dram("tab_x3_dram", (N, HG))
        tab_xn_dram = dram("tab_xn_dram", (N, D))
        starts4_dram = dram("starts4_dram", (P * T, H))
        starts32_dram = dram("starts32_dram", (P * T, D))
        scan0_dram = dram("scan0_dram", (P * T, C0))
        scan1_dram = dram("scan1_dram", (P * T, C1))
        scanD_dram = dram("scanD_dram", (P * T, D))

        dst_i = sb("dst_i", [NP, T], I32)
        fence = sb("fence", [P, 2])
        same = sb("same", [NP, T])
        ident = sb("ident", [P, P])
        ones = sb("ones", [P, P])
        before_qp = sb("before_qp", [P, P])
        before_pq = sb("before_pq", [P, P])
        shift = sb("shift", [P, P])
        carry_qp = sb("carry_qp", [NP, NP])
        carry_pq = sb("carry_pq", [NP, NP])
        no_carry_pq = sb("no_carry_pq", [NP, NP])
        ends = sb("ends", [NP, 4])
        node_i = sb("node_i", [P, J], I32)
        node_f = sb("node_f", [NP, J])
        base_i = sb("base_i", [P, 1], I32)
        base_f = sb("base_f", [NP, 1])
        row_of = sb("row_of", [P, J], I32)
        first_i = sb("first_i", [P, 1], I32)
        end_i = sb("end_i", [P, J], I32)
        start_i = sb("start_i", [P, J], I32)
        mend_get_i = sb("mend_get_i", [P, 1], I32)
        mend_put_i = sb("mend_put_i", [P, 1], I32)
        nodew = sb("nodew", [NP, 13, J])
        idx = sb("idx", [P, 2, L], I32)
        rows = sb("rows", [P, 2, L * W0])
        scan = sb("scan", [P, 2, L * C0])
        edges_d = sb("edges_d", [P, T * D])
        samec = sb("samec", [NP, 2, L])
        brk = sb("brk", [NP, L])
        mrun = sb("mrun", [NP, 2, H, L + 1])
        logit = sb("logit", [NP, H, L])
        rw = sb("rw", [NP, 2, 2, H, L])
        prod = sb("prod", [NP, L, D])
        local = sb("local", [P, C0])
        mended = sb("mended", [P, C0])
        diag = sb("diag", [NP, H, NP])
        cross = sb("cross", [NP, 2 * H * NP + H])
        crossT = cross[:, H * NP + H:].rearrange("p (h q) -> p h q", h=H)
        three = cross[:, :].bitcast(BF16)
        small = sb("small", [NP, 4, H])
        X = sb("X", [NP, J, D])
        agg = sb("agg", [P, J, C0])
        aggn = sb("aggn", [NP, J, P])
        bigT = sb("bigT", [P, J * NP])
        smallT = sb("smallT", [P, J * NP])
        tab = sb("tab", [P, J, W0])
        scat = sb("scat", [P, J, D])
        work = sb("work", [NP, J, D])
        work2 = sb("work2", [NP, J, D])
        rden = sb("rden", [NP, J, H])
        first_row = sb("first_row", [P, W0])
        attr = sb("attr", [NP, T, 2])
        src_f = sb("src_f", [NP, T])
        srcc = sb("srcc", [NP, SLOTS, LS])
        srcc_neg = sb("srcc_neg", [NP, SLOTS, LS])
        nodes16 = sb("nodes16", [NP, N], F16)
        node_c = sb("node_c", [NP, J])
        src16 = sb("src16", [P, 2, PE_MOST * NP], F16)
        stacks = sb("stacks", [P, D + HG + D + H], BF16)
        stack3 = sb("stack3", [3 * D, D])
        w_gat = sb("w_gat", [D, P])
        att_lr = sb("att_lr", [D, 2, P])
        w_lr = sb("w_lr", [D, 2 * H])
        w_ih = sb("w_ih", [3 * D, P])
        w_hh = sb("w_hh", [3 * D, D])
        w_ihT = sb("w_ihT", [P, 3 * D])
        w_gatBD = sb("w_gatBD", [P, P])
        w_agg = sb("w_agg", [P, P])
        w_x = sb("w_x", [D + 1, P])
        b_row = sb("b_row", [D + 1, 6 * D])
        w_cheb = sb("w_cheb", [3 * D + 1, D])
        w_sd = sb("w_sd", [D + 1, 2 * D])
        att1 = sb("att1", [NP, D])
        w_spl = sb("w_spl", [D, K2, D])
        scal = sb("scal", [NP, 8])
        ps = ctx.enter_context(nc.psum_tensor("ps", [P, 8, 512], F32))

        consts_made = sem("consts_made")
        scan_cleared = sem("scan_cleared")
        graph_loaded = sem("graph_loaded")
        x_loaded = sem("x_loaded")
        weights_loaded = sem("weights_loaded")
        starts_cleared = sem("starts_cleared")
        vec_done = sem("vec_done")
        vec_for_pe = sem("vec_for_pe")
        pe_for_vec = sem("pe_for_vec")
        group_in_psum = sem("group_in_psum")
        group_copied = sem("group_copied")
        vec_for_act = sem("vec_for_act")
        act_for_vec = sem("act_for_vec")
        vec_for_sync = sem("vec_for_sync")
        vec_for_pool = sem("vec_for_pool")
        cells_made = sem("cells_made")
        cells_stored = sem("cells_stored")
        products_stored = [sem("products_stored0"), sem("products_stored1")]
        table_stored = sem("table_stored")
        dst_rows_in = [sem(f"dst_rows_in{i}") for i in range(5)]
        scattered = sem("scattered")
        first_in = sem("first_in")
        edges_in = sem("edges_in")
        local_in = sem("local_in")
        agg_in = sem("agg_in")
        idx_in = [sem("idx_in0"), sem("idx_in1")]
        rows_in = [sem("rows_in0"), sem("rows_in1")]
        srcT_made = sem("srcT_made")
        srcT_turned = sem("srcT_turned")
        srcT_ready = sem("srcT_ready")
        srcT_stored = sem("srcT_stored")
        src16_in = [sem("src16_in0"), sem("src16_in1")]
        source_hots_ready = sem("source_hots_ready")
        source_hots_used = sem("source_hots_used")
        parts_copied = sem("parts_copied")
        rows_gathered = sem("rows_gathered")
        rows_filled = sem("rows_filled")
        nodes16_made = sem("nodes16_made")
        fence_done = sem("fence_done")
        rows_used = sem("rows_used")
        keep_ready = sem("keep_ready")
        chunk_scanned = sem("chunk_scanned")
        rows_turned = sem("rows_turned")
        scan_stored = [sem("scan_stored0"), sem("scan_stored1")]
        slot_in = [sem(f"slot_in{c}") for c in range(SLOTS)]
        slot_idx_in = [sem(f"slot_idx_in{c}") for c in range(SLOTS)]
        slot_used = sem("slot_used")
        sources_ready = sem("sources_ready")
        parts_ready = sem("parts_ready")
        onehot_ready = sem("onehot_ready")
        act_onehot_ready = sem("act_onehot_ready")
        half_hot_ready = sem("half_hot_ready")
        onehot_used = sem("onehot_used")
        out_stored = sem("out_stored")

        src_grid = src.rearrange("(p t) -> p t", t=T)
        dst_grid = dst.rearrange("(p t) -> p t", t=T)
        cell_grid = cell_dram.rearrange("(p t) -> p t", t=T)

        def nodes(a):
            return a.rearrange("(p j) c -> p (j c)", j=J)


        def chunks(eng, counts, step, between=None):
            before = [c.n for c, per in counts]
            step(0, 0, 0)
            step(1, 1, L)
            if between:
                between()
            counts = [(c, c.n - n if per is None else per) for (c, per), n in zip(counts, before)]
            with eng.Fori(0, TURNS) as turn:
                for c, per in counts:
                    c.enter(turn, per)
                step(2, 0, turn * (2 * L) + 2 * L)
                step(3, 1, turn * (2 * L) + 3 * L)
            for c, per in counts:
                c.leave(TURNS)
            for k in range(CH - 3, CH):
                step(k, k % 2, k * L)

        PASSES = {
            "gat": (tab0_dram, W0, scan0_dram, C0, H),
            "cheb0": (tab_cheb_dram[0], D, scanD_dram, D, 0),
            "cheb1": (tab_cheb_dram[1], D, scanD_dram, D, 0),
            "gatv2": (tab_fsrc_dram, D, scan1_dram, C1, 1),
            "agnn": (tab_x3_dram, HG, scan1_dram, C1, 1),
        }
        ORDER = list(PASSES)
        GATHERED = {name: HG if name == "agnn" else D + H if name == "gat" else D for name in PASSES}
        STACKS = {D: stacks[0:3 * D, 0:D], HG: stacks[0:3 * HG, D:D + HG],
                  D + H: stacks[0:3 * (D + H), D + HG:2 * D + HG + H]}

        def table_parts(name):
            w = GATHERED[name]
            return nodes16[:, :].bitcast(BF16)[:, 0:J * 3 * w].rearrange("p (j c) -> p j c", j=J)

        def flat2(t):
            return t[0:NP, :, :].rearrange("p a b -> p (a b)")

        def source_hots(name):
            if name == "gat":
                lots = [flat2(agg), flat2(aggn), bigT[0:NP, :], edges_d[0:NP, T * H + 3 * H * HG * L:],
                        flat2(work), flat2(work2), flat2(prod)]
            elif name in ("cheb0", "cheb1"):
                lots = [edges_d[0:NP, :], flat2(agg), flat2(work), flat2(work2)]
            else:
                lots = [flat2(agg), flat2(aggn), smallT[0:NP, :], scan[0:NP, 0, L * C1:], scan[0:NP, 1, L * C1:],
                        flat2(work), flat2(work2)]
            n = PE_COLS[name] * NP
            cut = [a.bitcast(BF16)[:, i * n:(i + 1) * n] for a in lots for i in range(2 * a.shape[1] // n)]
            return cut[0:J]

        def banks(name, b):
            n = PE_COLS[name]
            return [(3 * b + i, a, min(PG, n - a)) for i, a in enumerate(range(0, n, PG))]

        def scan_views(name):
            C = max(PASSES[name][4], 0) * HG or D
            free = edges_d[0:NP, T * H:] if name == "gat" else bigT[0:NP, :]
            z = [free[:, b * C * L:(b + 1) * C * L].rearrange("p (c t) -> p c t", t=L) for b in range(2)]
            return z, free[:, 2 * C * L:3 * C * L].rearrange("p (c t) -> p c t", t=L), C

        staged = edges_d[0:NP, 0:2 * LS * YROW].rearrange("p (b j c) -> p b j c", b=2, j=LS)
        slots = edges_d[:, 0:SLOTS * LS * CORNERS * D].rearrange("p (s c) -> p s c", s=SLOTS)
        at = 2 * LS * YROW
        basis = edges_d[0:NP, at:at + T * CORNERS].rearrange("p (t k) -> p t k", k=CORNERS)
        tents = bigT[0:NP, 0:4 * T].rearrange("p (d a t) -> p d a t", d=2, a=2)
        free = aggn[:, :, :].rearrange("p j c -> p (j c)")
        coord, cell, offset = (free[:, i * 2 * T:(i + 1) * 2 * T].rearrange("p (d t) -> p d t", d=2) for i in range(3))
        cell_i = free[:, 6 * T:7 * T].bitcast(I32)
        parts = agg[0:NP, :, :].rearrange("p j c -> p (j c)").bitcast(BF16)[:, 0:SLOTS * LS * 3 * D]\
            .rearrange("p (s t c) -> p s t c", s=SLOTS, t=LS)
        NA = N + N % 2

        def lay(t, at, count):
            return [t.bitcast(BF16)[0:NP, at + i * NA:at + i * NA + N] for i in range(count)]

        hots = [lay(scan[:, :, :].rearrange("p b c -> p (b c)"), 0, 4) + lay(bigT[:, :], 0, 1),
                lay(edges_d[:, :], 2 * SLOTS * LS * CORNERS * D, LS)]
        half_hot = lay(agg[:, :, :].rearrange("p j c -> p (j c)"), SLOTS * LS * 3 * D, 1)[0]
        assert 2 * SLOTS * LS * CORNERS * D + LS * NA <= 2 * at
        HOT_LAG = [1, 3] + [2] * (SLOTS - 2)
        assert SLOTS % 2 == 1

        with nc.Block() as block:

            @block.sync
            def _(sp):
                vec_sync, scanned = Count(), Count()
                gathered = [Count(), Count()]

                sp.dma_start(dst_i[:, :], dst_grid).then_inc(graph_loaded, SLOT)
                sp.dma_start(src_f[:, :].bitcast(I32), src_grid).then_inc(weights_loaded, SLOT)
                sp.dma_start(X[:, :, :].rearrange("p j c -> p (j c)"), nodes(x)).then_inc(x_loaded, SLOT)
                for t, a in [
                    (w_gat[:, :], W_gat),
                    (att_lr[:, 0, :], attn_l.rearrange("h f -> (h f)").partition_broadcast(D)),
                    (att_lr[:, 1, :], attn_r.rearrange("h f -> (h f)").partition_broadcast(D)),
                    (w_ih[:, :], W_ih),
                    (w_hh[:, :], W_hh),
                    (b_row[D:D + 1, 0:3 * D], b_ih.rearrange("(a n) -> a n", a=1)),
                    (b_row[D:D + 1, 3 * D:6 * D], b_hh.rearrange("(a n) -> a n", a=1)),
                    (w_cheb[0:3 * D, :], cheb_W),
                    (w_cheb[3 * D:3 * D + 1, :], cheb_b.rearrange("(a n) -> a n", a=1)),
                    (w_sd[0:D, 0:D], src_W),
                    (w_sd[0:D, D:2 * D], dst_W),
                    (w_sd[D:D + 1, 0:D], src_b.rearrange("(a n) -> a n", a=1)),
                    (w_sd[D:D + 1, D:2 * D], dst_b.rearrange("(a n) -> a n", a=1)),
                    (att1[:, :], attn.rearrange("h f -> (h f)").partition_broadcast(NP)),
                    (scal[:, 0:1], lambda_max.partition_broadcast(NP)),
                    (scal[:, 1:2], beta.partition_broadcast(NP)),
                    (attr[:, :, :].rearrange("p t c -> p (t c)"), edge_attr.rearrange("(p t) c -> p (t c)", t=T)),
                ]:
                    sp.dma_start(t, a).then_inc(weights_loaded, SLOT)
                for u in range(KU):
                    sp.dma_start(w_spl[:, u * KV:(u + 1) * KV, :], weight[u].rearrange("v f o -> f v o"))\
                        .then_inc(weights_loaded, SLOT)
                sp.wait_ge(scan_cleared, 1)
                sp.dma_start(starts4_dram.rearrange("(p t) c -> p (t c)", t=T), scan[:, 0, 0:T * H])\
                    .then_inc(starts_cleared, SLOT)
                whole = scan[:, :, :].rearrange("p b c -> p (b c)")
                flat = starts32_dram.rearrange("(p t) c -> p (t c)", t=T)
                for a in range(0, T * D, 2 * L * C0):
                    sp.dma_start(flat[:, a:a + 2 * L * C0], whole).then_inc(starts_cleared, SLOT)

                def store_table(a, t):
                    sp.wait_ge(vec_for_sync, vec_sync.up())
                    sp.dma_start(nodes(a), t).then_inc(table_stored, SLOT)

                def load_edges(a, width, lots):
                    sp.wait_ge(scattered, lots * SLOT)
                    sp.dma_start(edges_d[:, 0:T * width], a.rearrange("(p t) c -> p (t c)", t=T))\
                        .then_inc(edges_in, SLOT)

                hots_n = Count()

                def run_pass(name, between=None):
                    table, width, scan_dram, C, heads = PASSES[name]
                    grid = scan_dram.rearrange("(p t) c -> p (t c)", t=T)

                    def load_sources(k, b, t0):
                        if hots_n.n and k == 0:
                            sp.wait_ge(source_hots_ready, hots_n.at())
                        if k >= 2:
                            sp.wait_ge(source_hots_ready, hots_n.at(-BLOCKS))
                        hots_n.up(BLOCKS)
                        n = PE_COLS[name]
                        sp.dma_start(src16[0:NP, b, 0:n * NP], srcT_dram[bass.ds(t0 + L - n, n), :]
                                     .rearrange("t p -> (t p)").partition_broadcast(NP)).then_inc(src16_in[b], SLOT)

                    def step(k, b, t0):
                        if gathered[b].n or k >= 2:
                            sp.wait_ge(rows_in[b], gathered[b].at())
                        sp.dma_start(idx[0:NP, b, :], src_grid[:, bass.ds(t0, L)]).then_inc(idx_in[b], SLOT)
                        gathered[b].up(SLOT * (L - PE_COLS[name]))
                        if k < CH - 1:
                            load_sources(k + 1, 1 - b, t0 + L)
                        if k >= 2:
                            store(b, t0 - 2 * L)

                    def store(b, t0):
                        sp.wait_ge(rows_turned, scanned.up())
                        sp.dma_start(grid[:, bass.ds(t0 * C, L * C)], scan[:, b, 0:L * C])\
                            .then_inc(scan_stored[b], SLOT)

                    load_sources(0, 0, 0)
                    chunks(sp, [(gathered[0], None), (gathered[1], None), (scanned, 2), (hots_n, 2 * BLOCKS)], step,
                           between)
                    store(1, (CH - 2) * L)
                    store(0, (CH - 1) * L)

                tabf = tab[:, :, :].rearrange("p j c -> p (j c)")
                scatf = scat[:, :, :].rearrange("p j c -> p (j c)")
                sp.wait_ge(srcT_ready, 1)
                TP = T // 5
                sp.dma_start(srcT_dram.rearrange("(i t) p -> t i p", t=TP),
                             src16[0:TP, 0, 0:5 * NP].rearrange("t (i p) -> t i p", i=5)).then_inc(srcT_stored, SLOT)
                store_table(tab0_dram, tabf[0:NP, :])
                sp.wait_ge(srcT_stored, SLOT)
                run_pass("gat", lambda: load_edges(starts4_dram, H, J))
                store_table(tab_cheb_dram[0], tabf[0:NP, 0:J * D])
                run_pass("cheb0")
                store_table(tab_cheb_dram[1], tabf[0:NP, 0:J * D])
                run_pass("cheb1")
                store_table(tab_fsrc_dram, tabf[0:NP, 0:J * D])
                store_table(tab_fdst_dram, scatf[0:NP, :])
                run_pass("gatv2", lambda: load_edges(starts32_dram, D, 2 * J + 3))
                copied = 7 * len(GROUPS)
                for g in range(J // LS):
                    sp.wait_ge(group_copied, copied + (g + 1) * LS)
                    sp.dma_start(tab_y_dram.rearrange("(p j r) c -> p j (r c)", j=J, r=CELLS * CELLS)
                                 [:, g * LS:(g + 1) * LS, :], staged[:, g % 2, :, :])\
                        .then_inc(products_stored[g % 2], SLOT)
                    if g == 0:
                        sp.wait_ge(cells_made, 1)
                        sp.dma_start(cell_grid, cell_i).then_inc(cells_stored, SLOT)
                sp.wait_ge(cells_stored, SLOT)

                def load_indices(turn0, first):
                    for c in range(SLOTS):
                        if not first:
                            sp.wait_ge(slot_in[c], slot_n[c].up(SLOT * LS))
                        sp.dma_start(idx[0:NP, 0, c * LS:(c + 1) * LS], cell_grid[:, bass.ds(turn0 + c * LS, LS)])\
                            .then_inc(slot_idx_in[c], SLOT)

                slot_n = [Count() for c in range(SLOTS)]
                load_indices(0, True)
                with sp.Fori(0, CH - 1) as turn:
                    for c in slot_n:
                        c.enter(turn, SLOT * LS)
                    load_indices(turn * L + L, False)
                store_table(tab_x3_dram, tabf[0:NP, 0:J * HG])
                store_table(tab_xn_dram, scatf[0:NP, :])
                run_pass("agnn", lambda: load_edges(starts32_dram, D, 3 * J + 4))
                sp.wait_ge(vec_for_sync, vec_sync.up())
                sp.dma_start(nodes(out), X[:, :, :].rearrange("p j c -> p (j c)")).then_inc(out_stored, SLOT)
                sp.wait_ge(out_stored, SLOT)
                for b in range(2):
                    sp.wait_ge(scan_stored[b], len(ORDER) * SLOT * ((CH + 1 - b) // 2))
                sp.wait_ge(table_stored, 7 * SLOT)
                sp.wait_ge(scattered, (3 * J + len(ORDER)) * SLOT)

            @block.gpsimd
            def _(pool):
                vec_pool, used = Count(), Count()
                loaded = [Count(), Count()]
                put = Count()
                fences = Count()
                stored = [Count(), Count()]
                tables = Count()

                pool.memset(ones[:, :], 1.0).then_inc(consts_made, 1)
                pool.memset(row_of[:, :], 0).then_inc(consts_made, 1)
                pool.memset(first_i[:, :], 0).then_inc(consts_made, 1)
                pool.memset(end_i[:, :], 0).then_inc(consts_made, 1)
                pool.memset(start_i[:, :], int(SKIP)).then_inc(consts_made, 1)
                pool.memset(mend_get_i[:, :], 0).then_inc(consts_made, 1)
                pool.memset(mend_put_i[:, :], int(SKIP)).then_inc(consts_made, 1)
                pool.memset(idx[:, :, :], 0).then_inc(consts_made, 1)
                pool.iota(node_i[:, :], [[1, J]], base=0, channel_multiplier=J).then_inc(consts_made, 1)
                pool.iota(base_i[:, :], [[1, 1]], base=0, channel_multiplier=T).then_inc(consts_made, 1)
                pool.wait_ge(consts_made, 10)
                for t, op, base, cm, st in [
                    (ident, ALU.is_equal, 0, 1, -1),
                    (before_qp, ALU.is_gt, 0, -1, 1),
                    (before_pq, ALU.is_gt, 0, 1, -1),
                    (shift, ALU.is_equal, 1, 1, -1),
                ]:
                    pool.affine_select(t[:, :], ones[:, :], [[st, P]], op, 0.0, base=base,
                                       channel_multiplier=cm).then_inc(consts_made, 1)

                def gather(o, table, index, s):
                    pool.indirect_dma_start(o, None, table, bass.IndirectOffsetOnAxis(index, 0)).then_inc(s, SLOT)

                def scatter(table, index, rows_, last):
                    pool.indirect_dma_start(table, bass.IndirectOffsetOnAxis(index, 0), rows_, None,
                                            bounds_check=last, oob_is_err=False).then_inc(scattered, SLOT)
                    put.up(SLOT)

                def scatter_starts(a, c):
                    for j in range(J):
                        scatter(a, start_i[:, j:j + 1], scat[:, j, 0:c], E - 1)

                def run_pass(name):
                    table, width, scan_dram, C, heads = PASSES[name]
                    n = ORDER.index(name)

                    def step(k, b, t0):
                        pool.wait_ge(idx_in[b], loaded[b].up(SLOT))
                        if k >= 2:
                            pool.wait_ge(rows_used, used.up())
                        if fences.n:
                            pool.wait_ge(fence_done, fences.at())
                        pool.tensor_tensor(fence[:, b:b + 1], ones[:, 0:1], ones[:, 1:2], ALU.add)\
                            .then_inc(fence_done, 1)
                        fences.up()
                        for t in range(L - PE_COLS[name]):
                            gather(rows[:, b, t * width:(t + 1) * width], table, idx[:, b, t:t + 1], rows_in[b])

                    chunks(pool, [(loaded[0], SLOT), (loaded[1], SLOT), (used, 2), (fences, 2)], step)
                    used.up(2)
                    for b in range(2):
                        pool.wait_ge(scan_stored[b], stored[b].up(SLOT * ((CH + 1 - b) // 2)))
                    gather(local[:, 0:C], scan_dram, mend_get_i[:, 0:1], local_in)
                    pool.wait_ge(vec_for_pool, vec_pool.up())
                    scatter(scan_dram, mend_put_i[:, 0:1], mended[:, 0:C], E - 1)
                    pool.wait_ge(scattered, put.at())
                    for j in range(J):
                        gather(agg[:, j, 0:C], scan_dram, end_i[:, j:j + 1], agg_in)

                pool.wait_ge(vec_for_pool, vec_pool.up())
                for j in range(J):
                    gather(edges_d[:, j * T:(j + 1) * T].bitcast(I32), dst_grid, row_of[:, j:j + 1],
                           dst_rows_in[j // LS])
                pool.wait_ge(table_stored, tables.up(SLOT))
                gather(first_row[:, 0:W0], tab0_dram, first_i[:, 0:1], first_in)
                pool.wait_ge(vec_for_pool, vec_pool.up())
                pool.wait_ge(starts_cleared, SLOT * (1 + T * D // (2 * L * C0)))
                scatter_starts(starts4_dram, H)
                run_pass("gat")
                for name in ("cheb0", "cheb1"):
                    pool.wait_ge(table_stored, tables.up(SLOT))
                    run_pass(name)
                pool.wait_ge(vec_for_sync, 5)
                scatter_starts(starts32_dram, D)
                pool.wait_ge(table_stored, tables.up(2 * SLOT))
                gather(first_row[:, 0:D], tab_fdst_dram, first_i[:, 0:1], first_in)
                run_pass("gatv2")
                pool.iota(nodes16[:, :], [[1, N]], base=-MID, channel_multiplier=0,
                          allow_small_or_imprecise_dtypes=True).then_inc(nodes16_made, 1)
                for b in range(2):
                    pool.wait_ge(products_stored[b], SLOT * ((J // LS + 1 - b) // 2))
                idx_n = [Count() for c in range(SLOTS)]
                slots_used = Count()

                def gather_slot(c):
                    for t in range(LS):
                        gather(slots[:, c, t * CORNERS * D:(t + 1) * CORNERS * D], tab_y_dram,
                               idx[:, 0, c * LS + t:c * LS + t + 1], slot_in[c])

                for c in range(SLOTS):
                    pool.wait_ge(slot_idx_in[c], idx_n[c].up(SLOT))
                    gather_slot(c)
                with pool.Fori(0, CH - 1) as turn:
                    for c in idx_n:
                        c.enter(turn, SLOT)
                    slots_used.enter(turn, SLOTS)
                    fences.enter(turn, SLOTS)
                    for c in range(SLOTS):
                        pool.wait_ge(slot_idx_in[c], idx_n[c].up(SLOT))
                        pool.wait_ge(slot_used, slots_used.up())
                        pool.wait_ge(fence_done, fences.at())
                        pool.tensor_tensor(fence[:, 0:1], ones[:, 0:1], ones[:, 1:2], ALU.add)\
                            .then_inc(fence_done, 1)
                        fences.up()
                        gather_slot(c)
                for c in idx_n:
                    c.leave(CH - 1)
                slots_used.leave(CH - 1)
                fences.leave(CH - 1)
                pool.wait_ge(vec_for_sync, 7)
                scatter_starts(starts32_dram, D)
                pool.wait_ge(table_stored, tables.up(2 * SLOT))
                gather(first_row[:, 0:D], tab_xn_dram, first_i[:, 0:1], first_in)
                run_pass("agnn")

            @block.tensor
            def _(pe):
                operand, group, copied = Count(), Count(), Count()

                def in_groups(product, groups=GROUPS):
                    for tiles in groups:
                        n = group.n
                        if n >= 2:
                            pe.wait_ge(group_copied, n - 1)
                        for a, j in enumerate(tiles):
                            ins = product(ps[:, n % 2, :], a, j)
                        ins.then_inc(group_in_psum, 1)
                        group.up()

                def all_copied():
                    pe.wait_ge(group_copied, group.n)

                def tile_T(t, j):
                    return t[:, j * NP:(j + 1) * NP]

                hots_n, filled = Count(), Count()

                def gather_rows(name):
                    w = GATHERED[name]
                    hots_, table_ = source_hots(name), table_parts(name)

                    def step(k, b, t0):
                        if filled.n and k == 0:
                            pe.wait_ge(rows_filled, filled.at())
                        if k >= 1:
                            pe.wait_ge(parts_copied, filled.at(-1))
                        for m in range(BLOCKS):
                            pe.wait_ge(source_hots_ready, hots_n.up())
                            for j in range(m * LS, (m + 1) * LS):
                                for bank, a, n in banks(name, b):
                                    ins = pe.matmul(ps[0:3 * w, bank, 0:n * NP], table_[:, j, :],
                                                    hots_[j][:, a * NP:(a + n) * NP],
                                                    start=(j == 0), stop=(j == J - 1))
                            ins.then_inc(source_hots_used, 1)
                        if k >= 2:
                            pe.wait_ge(rows_filled, filled.at(-1))
                        pe.wait_ge(parts_copied, filled.up())
                        for i in range(PE_COLS[name]):
                            ins = pe.matmul(ps[0:NP, 6 + b, i * w:(i + 1) * w], three[0:3 * w, i * NP:(i + 1) * NP],
                                            STACKS[w], start=True, stop=True)
                        ins.then_inc(rows_gathered, 1)

                    chunks(pe, [(hots_n, 2 * BLOCKS), (filled, 2)], step)

                def mend(name):
                    table, width, scan_dram, C, heads = PASSES[name]
                    gather_rows(name)
                    if heads == 0:
                        pe.wait_ge(rows_turned, (ORDER.index(name) + 1) * CH)
                        pe.matmul(ps[0:NP, 6, 0:C], carry_qp[:, :], scan[0:NP, 0, (L - 1) * C:L * C],
                                  start=True, stop=True).then_inc(pe_for_vec, 1)
                        return
                    pe.wait_ge(vec_for_pe, operand.up())
                    for h in range(heads):
                        ins = pe.matmul(ps[0:NP, 6, h * NP:(h + 1) * NP], ones[0:NP, 0:NP], diag[:, h, :],
                                        start=True, stop=True)
                    ins.then_inc(pe_for_vec, 1)
                    pe.wait_ge(vec_for_pe, operand.up())
                    for h in range(heads):
                        ins = pe.transpose(ps[0:NP, 7, h * NP:(h + 1) * NP], cross[:, h * NP:(h + 1) * NP],
                                           ident[0:NP, 0:NP])
                    ins.then_inc(pe_for_vec, 1)
                    pe.wait_ge(vec_for_pe, operand.up())
                    for h in range(heads):
                        at = (L - 1) * C + h * HG
                        ins = pe.matmul(ps[0:NP, 6, h * HG:(h + 1) * HG], crossT[:, h, :],
                                        scan[0:NP, 0, at:at + HG], start=True, stop=True)
                    ins.then_inc(pe_for_vec, 1)

                def sum_into_sources():
                    hot, act_hot, part = Count(), Count(), Count()

                    def turn_of(begin, end):
                        for c in range(SLOTS):
                            pe.wait_ge(parts_ready, part.up())
                            for t in range(LS):
                                if (c, t) in ACT_HOT:
                                    pe.wait_ge(act_onehot_ready, act_hot.up())
                                else:
                                    pe.wait_ge(onehot_ready, hot.up())
                                for at in range(0, N, BANK):
                                    n = min(BANK, N - at)
                                    ins = pe.matmul(ps[0:3 * D, at // BANK, 0:n], parts[:, c, t, :],
                                                    hots[c % 2][t][:, at:at + n], start=(begin and c == 0 and t == 0),
                                                    stop=(end and c == SLOTS - 1 and t == LS - 1))
                                ins.then_inc(onehot_used, 1)

                    turn_of(True, False)
                    with pe.Fori(0, CH - 2) as turn:
                        part.enter(turn, SLOTS)
                        act_hot.enter(turn, len(ACT_HOT))
                        hot.enter(turn, L - len(ACT_HOT))
                        turn_of(False, False)
                    for n in (part, act_hot, hot):
                        n.leave(CH - 2)
                    turn_of(False, True)

                pe.wait_ge(consts_made, 14)
                pe.wait_ge(weights_loaded, SLOT * (18 + KU))
                pe.transpose(ps[:, 2, 0:3 * D], w_ih[:, :], ident[0:3 * D, 0:3 * D])
                pe.transpose(ps[:, 2, 3 * D:4 * D], w_gat[:, :], ident[0:D, 0:D])
                pe.transpose(ps[0:D, 3, 0:3 * D], w_hh[:, :], ident[0:3 * D, 0:3 * D]).then_inc(pe_for_vec, 1)
                pe.wait_ge(srcT_made, 1)
                TP = T // 5
                for i in range(5):
                    ins = pe.transpose(ps[0:TP, 6 + i // 4, i % 4 * NP:(i % 4 + 1) * NP],
                                       src_f[:, i * TP:(i + 1) * TP], ident[0:NP, 0:NP])
                ins.then_inc(srcT_turned, 1)
                pe.wait_ge(x_loaded, SLOT)
                in_groups(lambda bank, a, j: pe.transpose(bank[0:D, a * NP:(a + 1) * NP], X[:, j, :],
                                                          ident[0:NP, 0:NP]))
                pe.wait_ge(vec_for_pe, operand.up())
                pe.matmul(ps[0:NP, 4, 0:NP], ones[0:NP, 0:NP], diag[:, 0, :], start=True, stop=True)
                pe.matmul(ps[0:NP, 4, NP:2 * NP], ones[0:NP, 0:NP], diag[:, 1, :], start=True, stop=True)\
                    .then_inc(pe_for_vec, 1)
                pe.wait_ge(vec_for_pe, operand.up())
                pe.matmul(ps[:, 5, 0:3 * D], w_gatBD[:, :], w_ihT[:, :], start=True, stop=True)\
                    .then_inc(pe_for_vec, 1)
                pe.wait_ge(vec_for_pe, operand.up())
                all_copied()
                for j in range(J):
                    ins = pe.matmul(ps[0:NP, 3, j * 2 * H:(j + 1) * 2 * H], tile_T(smallT, j)[0:D, :], w_lr[:, :],
                                    start=True, stop=True)
                ins.then_inc(pe_for_vec, 1)
                pe.wait_ge(vec_for_pe, operand.up())
                pe.matmul(ps[0:NP, 4, 2 * NP:2 * NP + 1], shift[0:NP, 0:NP], nodew[:, 0, J - 1:J],
                          start=True, stop=True).then_inc(pe_for_vec, 1)

                mend("gat")
                pe.wait_ge(vec_for_pe, operand.up())
                in_groups(lambda bank, a, j: pe.transpose(bank[:, a * NP:(a + 1) * NP], aggn[:, j, :],
                                                          ident[0:NP, 0:NP]))
                all_copied()

                def gates(bank, a, j):
                    pe.matmul(bank[0:NP, a * P:(a + 1) * P], tile_T(bigT, j), w_agg[:, :], start=True, stop=False)
                    return pe.matmul(bank[0:NP, a * P:(a + 1) * P], tile_T(smallT, j)[0:D + 1, :], w_x[:, :],
                                     start=False, stop=True)

                in_groups(gates)
                mend("cheb0")
                mend("cheb1")
                pe.wait_ge(vec_for_pe, operand.up())
                in_groups(lambda bank, a, j: pe.transpose(bank[0:3 * D, a * NP:(a + 1) * NP],
                                                          aggn[:, j, 0:3 * D], ident[0:NP, 0:NP]))
                all_copied()
                in_groups(lambda bank, a, j: pe.matmul(bank[0:D, a * NP:(a + 1) * NP], w_cheb[:, :],
                                                       bigT[0:3 * D + 1, j * NP:(j + 1) * NP],
                                                       start=True, stop=True))
                all_copied()
                in_groups(lambda bank, a, j: pe.matmul(bank[0:NP, a * 2 * D:(a + 1) * 2 * D], tile_T(smallT, j)[0:D + 1, :],
                                                       w_sd[:, :], start=True, stop=True))
                mend("gatv2")
                pe.wait_ge(vec_for_pe, operand.up())
                in_groups(lambda bank, a, j: pe.transpose(bank[0:D, a * NP:(a + 1) * NP], X[:, j, :],
                                                          ident[0:NP, 0:NP]))
                all_copied()
                in_groups(lambda bank, a, j: pe.matmul(bank[0:NP, :], smallT[0:D, j * NP:(j + 1) * NP],
                                                       w_spl[:, :, :].rearrange("p k f -> p (k f)"),
                                                       start=True, stop=True), [[j] for j in range(J)])
                all_copied()
                sum_into_sources()
                pe.wait_ge(vec_for_pe, operand.up())
                in_groups(lambda bank, a, j: pe.matmul(bank[0:NP, a * D:(a + 1) * D],
                                                       bigT[0:3 * D, j:N:J], stack3[:, :], start=True, stop=True))
                mend("agnn")

            @block.scalar
            def _(act):
                group, arg, value = Count(), Count(), Count()

                def copy_groups(place, source, func=ACT.Copy, groups=GROUPS):
                    for tiles in groups:
                        bank = ps[:, group.n % 2, :]
                        act.wait_ge(group_in_psum, group.up())
                        nc.scalar.activation(place(tiles), source(bank, len(tiles)), func)\
                            .then_inc(group_copied, 1)

                def apply(func, t):
                    act.wait_ge(vec_for_act, arg.up())
                    nc.scalar.activation(t, t, func).then_inc(act_for_vec, 1)
                    value.up()

                def columns(tiles):
                    return slice(tiles[0] * NP, (tiles[-1] + 1) * NP)

                scanned, stored = Count(), [Count(), Count()]
                gathered = [Count(), Count()]

                filled, used = Count(), Count()

                def copy_gathered(k, b, name):
                    width, w, n = PASSES[name][1], GATHERED[name], PE_COLS[name]
                    if filled.n or k >= 1:
                        act.wait_ge(rows_gathered, filled.at())
                    act.wait_ge(source_hots_used, hots_n.up(BLOCKS))
                    for bank, a, cols in banks(name, b):
                        ins = nc.scalar.activation(three[0:3 * w, a * NP:(a + cols) * NP],
                                                   ps[0:3 * w, bank, 0:cols * NP], ACT.Copy)
                    ins.then_inc(parts_copied, 1)
                    if filled.n and k == 0:
                        act.wait_ge(rows_used, filled.at())
                    if k >= 2:
                        act.wait_ge(rows_used, filled.at(-1))
                    act.wait_ge(rows_gathered, filled.up())
                    nc.scalar.activation(
                        rows[0:NP, b, (L - n) * width:L * width].rearrange("p (t c) -> p t c", c=width)[:, :, 0:w],
                        ps[0:NP, 6 + b, 0:n * w].rearrange("p (t c) -> p t c", c=w), ACT.Copy)\
                        .then_inc(rows_filled, 1)

                hots_n = Count()

                def copy_next(k, b, name):
                    if k < CH - 1:
                        copy_gathered(k + 1, 1 - b, name)

                def turn_rows(k, b, C, z):
                    act.wait_ge(chunk_scanned, scanned.up())
                    if stored[b].n or k >= 2:
                        act.wait_ge(scan_stored[b], stored[b].at())
                    stored[b].up(SLOT)
                    rows_ = scan[0:NP, b, 0:L * C].rearrange("p (t c) -> p t c", c=C)
                    n = z.shape[1]
                    return rows_[:, :, 0:n], z.rearrange("p c t -> p t c"), rows_[:, :, n:C]

                def softmax_pass(name):
                    table, width, scan_dram, C, heads = PASSES[name]
                    z, keep, n = scan_views(name)

                    def step(k, b, t0):
                        gathered[b].up(SLOT * (L - PE_COLS[name]))
                        apply(ACT.Exp, rw[:, b, :, 0:heads, :])
                        act.wait_ge(act_for_vec, value.at())
                        nc.scalar.activation(
                            keep.rearrange("p (h g) t -> p h g t", g=HG)[:, :, :, 1:L],
                            rw[:, b, 0, 0:heads, 1:L].unsqueeze(2).broadcast_to([NP, heads, HG, L - 1]),
                            ACT.Copy).then_inc(keep_ready, 1)
                        copy_next(k, b, name)
                        to, of, maxima = turn_rows(k, b, C, z[b])
                        nc.scalar.activation(maxima, mrun[:, b, 0:heads, 1:L + 1].rearrange("p h t -> p t h"),
                                             ACT.Copy)
                        nc.scalar.activation(to, of, ACT.Copy).then_inc(rows_turned, 1)

                    copy_gathered(0, 0, name)
                    chunks(act, [(arg, 2), (value, 2), (scanned, 2), (stored[0], SLOT), (stored[1], SLOT),
                                 (gathered[0], None), (gathered[1], None), (filled, 2),
                                 (hots_n, 2 * BLOCKS)], step)
                    apply(ACT.Exp, cross[:, 0:heads * NP + heads])

                def sum_pass(name):
                    z, keep, n = scan_views(name)

                    def step(k, b, t0):
                        act.wait_ge(rows_in[b], gathered[b].up(SLOT * (L - PE_COLS[name])))
                        act.wait_ge(rows_filled, filled.at())
                        nc.scalar.activation(z[b], rows[0:NP, b, 0:L * D].rearrange("p (t c) -> p c t", c=D),
                                             ACT.Copy).then_inc(rows_used, 1)
                        act.wait_ge(vec_for_act, arg.up())
                        nc.scalar.activation(keep[:, :, 1:L],
                                             samec[:, b, 1:L].unsqueeze(1).broadcast_to([NP, D, L - 1]),
                                             ACT.Copy).then_inc(act_for_vec, 1)
                        value.up()
                        copy_next(k, b, name)
                        to, of, _ = turn_rows(k, b, D, z[b])
                        nc.scalar.activation(to, of, ACT.Copy).then_inc(rows_turned, 1)

                    copy_gathered(0, 0, name)
                    chunks(act, [(arg, 2), (value, 2), (scanned, 2), (stored[0], SLOT), (stored[1], SLOT),
                                 (gathered[0], None), (gathered[1], None), (filled, 2),
                                 (hots_n, 2 * BLOCKS)], step)

                def layer_norm():
                    apply(ACT.Sqrt, nodew[:, 7, :])

                copy_groups(lambda tiles: smallT[0:D, columns(tiles)], lambda bank, n: bank[0:D, 0:n * NP])
                apply(ACT.Sqrt, nodew[:, 4, :])
                softmax_pass("gat")
                copy_groups(lambda tiles: bigT[:, columns(tiles)], lambda bank, n: bank[:, 0:n * NP])
                copy_groups(lambda tiles: aggn[:, tiles[0]:tiles[-1] + 1, :].rearrange("p j c -> p (j c)"),
                            lambda bank, n: bank[0:NP, 0:n * P])
                act.wait_ge(group_copied, group.n)
                nc.scalar.activation(aggn[:, :, 0:2 * D], aggn[:, :, 0:2 * D], ACT.Sigmoid).then_inc(act_for_vec, 1)
                value.up()
                apply(ACT.Tanh, work[:, :, :])
                apply(ACT.Exp, work2[:, :, :])
                layer_norm()
                sum_pass("cheb0")
                sum_pass("cheb1")
                copy_groups(lambda tiles: bigT[0:3 * D, columns(tiles)], lambda bank, n: bank[0:3 * D, 0:n * NP])
                copy_groups(lambda tiles: smallT[0:D, columns(tiles)], lambda bank, n: bank[0:D, 0:n * NP], ACT.Relu)
                copy_groups(lambda tiles: aggn[:, tiles[0]:tiles[-1] + 1, 0:2 * D],
                            lambda bank, n: bank[0:NP, 0:n * 2 * D].rearrange("p (j c) -> p j c", j=n))
                softmax_pass("gatv2")
                layer_norm()

                copy_groups(lambda tiles: smallT[0:D, columns(tiles)], lambda bank, n: bank[0:D, 0:n * NP])
                for j in range(J):
                    g = j // LS
                    if g >= 2 and j % LS == 0:
                        act.wait_ge(products_stored[g % 2], SLOT * (g // 2))
                    made_ = ps[0:NP, group.n % 2, :].rearrange("p (u v c) -> p u v c", u=KU, v=KV)
                    to = staged[:, g % 2, j % LS, :].rearrange("p (v u a c) -> p v u a c", v=CELLS, u=CELLS, a=2)
                    act.wait_ge(group_in_psum, group.up())
                    for v in range(CELLS):
                        for a in range(2):
                            ins = nc.scalar.activation(
                                to[:, v, :, a, :].rearrange("p u (b c) -> p u b c", b=2),
                                made_[:, a:a + CELLS, v:v + 2, :], ACT.Copy)
                    ins.then_inc(group_copied, 1)
                sources, half, hot_used = Count(), Count(), Count(-L)

                def one_hots(first):
                    act.wait_ge(sources_ready, sources.up())
                    if first:
                        act.wait_ge(nodes16_made, 1)
                        for b in range(2):
                            act.wait_ge(products_stored[b], SLOT * ((J // LS + 1 - b) // 2))
                    for c in range(SLOTS):
                        for t in range(LS):
                            hot_used.up()
                            if (c, t) not in ACT_HOT:
                                continue
                            if half.n:
                                act.wait_ge(act_onehot_ready, half.at())
                            nc.scalar.activation(half_hot, nodes16[:, :], ACT.Square,
                                                 bias=srcc_neg[:, c, t:t + 1]).then_inc(half_hot_ready, 1)
                            half.up()
                            act.wait_ge(half_hot_ready, half.at())
                            if not first or c >= HOT_LAG[c]:
                                act.wait_ge(onehot_used, hot_used.at(L - HOT_LAG[c] * LS))
                            nc.scalar.activation(hots[c % 2][t], half_hot, ACT.Relu, bias=1.0, scale=-1.0)\
                                .then_inc(act_onehot_ready, 1)

                one_hots(True)
                with act.Fori(0, CH - 1) as turn:
                    for c, per in ((sources, 1), (half, len(ACT_HOT)), (hot_used, L)):
                        c.enter(turn, per)
                    one_hots(False)
                copy_groups(lambda tiles: work2[:, tiles[0]:tiles[-1] + 1, :],
                            lambda bank, n: bank[0:NP, 0:n * D].rearrange("p (j c) -> p j c", j=n))
                layer_norm()
                apply(ACT.Sqrt, nodew[:, 7, :])
                softmax_pass("agnn")
                apply(ACT.Exp, nodew[:, 0:2, :])
                layer_norm()

            @block.vector
            def _(vec):
                own = Count()
                pe_n, group_n, act_n = Count(), Count(), Count()
                gathered = [Count(), Count()]
                scanned = Count()
                edges_n, first_n, local_n, agg_n = Count(), Count(), Count(), Count()
                CUM, PREV, DEG, SOME, DINV, DSOME, MEAN, RSTD, RN, ROW, CNT, TMP, SELF = range(13)

                def per_node(slot):
                    return nodew[:, slot, :]

                def over(a, n):
                    return a.unsqueeze(len(a.shape)).broadcast_to(list(a.shape) + [n])

                hots_n, filled = Count(), Count()
                src16_n = [Count(), Count()]

                making = {"row": J}

                def start_hots(k, b, name):
                    making.update(row=0 if k < CH else J, b=b, hots=source_hots(name), n=PE_COLS[name] * NP)
                    if k < CH:
                        vec.wait_ge(src16_in[b], src16_n[b].up(SLOT))

                def more_hots(count=1):
                    for j in range(making["row"], min(making["row"] + count, J)):
                        if j % LS == 0 and not making.get("first"):
                            vec.wait_ge(source_hots_used, hots_n.at(1 - BLOCKS))
                        ins = vec.tensor_scalar(making["hots"][j], src16[0:NP, making["b"], 0:making["n"]],
                                                node_c[:, j:j + 1], None, ALU.is_equal)
                        if j % LS == LS - 1:
                            ins.then_inc(source_hots_ready, 1)
                            hots_n.up()
                        making["row"] = j + 1

                def settle():
                    more_hots()
                    vec.wait_ge(vec_done, own.up())

                vec.memset(scan[:, :, :], 0.0).then_inc(scan_cleared, 1)
                vec.memset(mended[:, :], 0.0)
                vec.memset(scat[:, :, :], 0.0)
                vec.memset(w_agg[:, :], 0.0)
                vec.memset(w_gatBD[:, :], 0.0)
                vec.memset(w_x[:, :], 0.0)
                vec.memset(smallT[D:D + 1, :], 1.0)
                vec.memset(same[:, 0:1], 0.0).then_inc(vec_done, 1)
                settle()

                vec.wait_ge(graph_loaded, SLOT)
                vec.wait_ge(consts_made, 14)
                vec.tensor_copy(ends[:, 0:1], dst_i[:, 0:1])
                vec.tensor_copy(first_i[0:NP, :], dst_i[:, 0:1])
                vec.tensor_copy(node_f[:, :], node_i[0:NP, :])
                vec.tensor_copy(base_f[:, :], base_i[0:NP, :])
                vec.tensor_copy(ends[:, 1:2], dst_i[:, T - 1:T]).then_inc(vec_done, 1)
                settle()
                for i in range(2):
                    ins = vec.tensor_scalar(diag[:, i, :], ident[0:NP, 0:NP], ends[:, i:i + 1], None, ALU.mult)
                ins.then_inc(vec_for_pe, 1)
                vec.tensor_tensor(same[:, 1:T], dst_i[:, 1:T], dst_i[:, 0:T - 1], ALU.is_equal)

                vec.wait_ge(weights_loaded, SLOT * (18 + KU))
                vec.tensor_scalar(src_f[:, :], src_f[:, :].bitcast(I32), -float(MID), None, ALU.add)\
                    .then_inc(srcT_made, 1)
                vec.tensor_scalar(node_c[:, :], node_f[:, :], -float(MID), None, ALU.add)
                for w in STACKS:
                    vec.tensor_tensor(STACKS[w], ident[0:3 * w, 0:w], ident[0:3 * w, w:2 * w], ALU.add)\
                        .then_inc(vec_done, 1)
                    settle()
                    vec.tensor_tensor(STACKS[w], STACKS[w], ident[0:3 * w, 2 * w:3 * w], ALU.add)
                for i in range(3):
                    vec.tensor_copy(stack3[i * D:(i + 1) * D, :], ident[i * D:(i + 1) * D, i * D:(i + 1) * D])
                vec.wait_ge(pe_for_vec, pe_n.up())
                vec.tensor_copy(w_ihT[:, :], ps[:, 2, 0:3 * D])
                for h in range(H):
                    ins = vec.tensor_copy(w_gatBD[h * D:(h + 1) * D, h * D:(h + 1) * D],
                                          ps[h * D:(h + 1) * D, 2, 3 * D:4 * D])
                ins.then_inc(vec_for_pe, 1)
                vec.tensor_tensor(att_lr[:, :, :], att_lr[:, :, :],
                                  w_gat[:, :].unsqueeze(1).broadcast_to([D, 2, P]), ALU.mult).then_inc(vec_done, 1)
                settle()
                vec.tensor_reduce(w_lr[:, :], att_lr[:, :, :].rearrange("p s (h f) -> p (s h) f", h=H), X_AXIS, ALU.add)
                vec.tensor_copy(w_x[0:D, 0:2 * D], ps[0:D, 3, 0:2 * D])
                vec.tensor_copy(w_x[0:D, 3 * D:4 * D], ps[0:D, 3, 2 * D:3 * D])
                vec.tensor_tensor(w_x[D:D + 1, 0:2 * D], b_row[D:D + 1, 0:2 * D], b_row[D:D + 1, 3 * D:5 * D], ALU.add)
                vec.tensor_copy(w_x[D:D + 1, 2 * D:3 * D], b_row[D:D + 1, 2 * D:3 * D])
                vec.tensor_copy(w_x[D:D + 1, 3 * D:4 * D], b_row[D:D + 1, 5 * D:6 * D]).then_inc(vec_for_pe, 1)
                vec.reciprocal(scal[:, 7:8], scal[:, 0:1]).then_inc(vec_done, 1)
                settle()
                vec.tensor_scalar(scal[:, 2:3], scal[:, 7:8], 2.0, None, ALU.mult)
                vec.tensor_scalar(scal[:, 3:4], scal[:, 7:8], -2.0, None, ALU.mult)
                vec.tensor_scalar(scal[:, 4:5], scal[:, 7:8], 2.0, -1.0, ALU.mult, ALU.add)
                vec.tensor_scalar(scal[:, 5:6], scal[:, 7:8], -4.0, None, ALU.mult)
                vec.tensor_scalar(scal[:, 6:7], scal[:, 7:8], 4.0, -2.0, ALU.mult, ALU.add)

                vec.wait_ge(pe_for_vec, pe_n.up())
                firsts, lasts = ps[0:NP, 4, 0:NP], ps[0:NP, 4, NP:2 * NP]
                vec.scalar_tensor_tensor(carry_qp[:, :], firsts, ends[:, 1:2], before_qp[0:NP, 0:NP],
                                         ALU.is_equal, ALU.mult)
                vec.scalar_tensor_tensor(carry_pq[:, :], lasts, ends[:, 0:1], before_pq[0:NP, 0:NP],
                                         ALU.is_equal, ALU.mult)
                upto = edges_d[0:NP, 0:J * NP].rearrange("p (j q) -> p j q", j=J)
                vec.tensor_tensor(upto, over(node_f[:, :], NP), firsts.unsqueeze(1).broadcast_to([NP, J, NP]),
                                  ALU.is_ge).then_inc(vec_done, 1)
                settle()
                vec.tensor_scalar(no_carry_pq[:, :], carry_pq[:, :], -1.0, BIG, ALU.add, ALU.mult)
                vec.tensor_reduce(per_node(CNT), upto, X_AXIS, ALU.add).then_inc(vec_done, 1)
                settle()
                vec.tensor_scalar(per_node(ROW), per_node(CNT), -1.0, 0.0, ALU.add, ALU.max).then_inc(vec_done, 1)
                settle()
                vec.tensor_copy(row_of[0:NP, :], per_node(ROW)).then_inc(vec_for_pool, 1)

                vec.wait_ge(pe_for_vec, pe_n.up())
                vec.tensor_copy(w_agg[:, 0:3 * D], ps[:, 5, 0:3 * D])

                TP = T // 5
                vec.wait_ge(srcT_turned, 1)
                vec.tensor_copy(src16[0:TP, 0, 0:4 * NP], ps[0:TP, 6, 0:4 * NP])
                vec.tensor_copy(src16[0:TP, 0, 4 * NP:5 * NP], ps[0:TP, 7, 0:NP]).then_inc(srcT_ready, 1)

                vec.wait_ge(x_loaded, SLOT)
                vec.wait_ge(pe_for_vec, pe_n.up())
                lr = ps[0:NP, 3, 0:J * 2 * H].rearrange("p (j c) -> p j c", j=J)
                vec.tensor_copy(tab[0:NP, :, 0:D], X[:, :, :])
                vec.tensor_copy(scat[0:NP, :, 0:H], lr[:, :, H:2 * H])
                vec.tensor_copy(tab[0:NP, :, D:W0], lr).then_inc(vec_for_sync, 1)

                flat = work[:, :, :].rearrange("p j c -> p (j c)")[:, 0:T]
                vec.tensor_scalar(flat, dst_i[:, :], ends[:, 0:1], None, ALU.is_equal).then_inc(vec_done, 1)
                settle()
                vec.tensor_reduce(ends[:, 2:3], flat, X_AXIS, ALU.add).then_inc(vec_done, 1)
                settle()
                vec.scalar_tensor_tensor(ends[:, 3:4], ends[:, 2:3], -1.0, base_f[:, :], ALU.add, ALU.add)\
                    .then_inc(vec_done, 1)
                settle()
                vec.tensor_copy(mend_get_i[0:NP, :], ends[:, 3:4])
                vec.tensor_copy(mend_put_i[0:NP, :], ends[:, 3:4])

                for j in range(J):
                    if j % LS == 0:
                        vec.wait_ge(dst_rows_in[j // LS], LS * SLOT)
                    there = edges_d[0:NP, j * T:(j + 1) * T]
                    ins = vec.tensor_scalar(there, there.bitcast(I32), node_f[:, j:j + 1], 0.0, ALU.is_le, ALU.add,
                                            accum_out=nodew[:, CNT, j:j + 1])
                ins.then_inc(vec_done, 1)
                settle()
                vec.scalar_tensor_tensor(per_node(CUM), per_node(ROW), float(T), per_node(CNT), ALU.mult, ALU.add)\
                    .then_inc(vec_for_pe, 1)
                vec.wait_ge(vec_for_pe, 4)
                vec.tensor_copy(nodew[:, PREV, 1:J], nodew[:, CUM, 0:J - 1])
                vec.wait_ge(pe_for_vec, pe_n.up())
                vec.tensor_copy(nodew[:, PREV, 0:1], ps[0:NP, 4, 2 * NP:2 * NP + 1]).then_inc(vec_done, 1)
                settle()
                vec.tensor_tensor(per_node(DEG), per_node(CUM), per_node(PREV), ALU.subtract).then_inc(vec_done, 1)
                settle()
                vec.tensor_scalar(per_node(CNT), per_node(CUM), -1.0, 0.0, ALU.add, ALU.max)
                vec.tensor_scalar(per_node(SOME), per_node(DEG), 1.0, None, ALU.min)
                vec.tensor_scalar(per_node(DINV), per_node(DEG), 1.0, None, ALU.max).then_inc(vec_for_act, 1)
                vec.wait_ge(vec_for_act, 1)
                vec.tensor_scalar(per_node(TMP), per_node(SOME), -SKIP, SKIP, ALU.mult, ALU.add).then_inc(vec_done, 1)
                settle()
                vec.tensor_tensor(per_node(TMP), per_node(TMP), per_node(PREV), ALU.add).then_inc(vec_done, 1)
                settle()
                vec.tensor_copy(end_i[0:NP, :], per_node(CNT))
                vec.tensor_copy(start_i[0:NP, :], per_node(TMP)).then_inc(vec_for_pool, 1)
                vec.wait_ge(act_for_vec, act_n.up())
                vec.reciprocal(per_node(DINV), per_node(DINV)).then_inc(vec_done, 1)
                settle()
                vec.tensor_tensor(per_node(DSOME), per_node(DINV), per_node(SOME), ALU.mult)

                def fill_edges(width, at, filled=vec_done):
                    ed = edges_d[0:NP, 0:T * width].rearrange("p (t c) -> p t c", c=width)
                    vec.wait_ge(edges_in, edges_n.up(SLOT))
                    vec.wait_ge(first_in, first_n.up(SLOT))
                    vec.tensor_copy(ed[:, 0, :], first_row[0:NP, at:at + width]).then_inc(vec_done, 1)
                    settle()
                    for c in range(width):
                        ins = vec.tensor_tensor_scan(ed[:, :, c], same[:, :], ed[:, :, c], 0.0, ALU.mult, ALU.add)
                    ins.then_inc(filled, 1)
                    if filled is vec_done:
                        settle()

                def begin_pass(name, table_, stores):
                    w = GATHERED[name]
                    rest = scan[0:NP, 1, 0:J * w].rearrange("p (j c) -> p j c", j=J)
                    high, mid, low = (table_parts(name)[:, :, i * w:(i + 1) * w] for i in range(3))
                    vec.wait_ge(vec_for_sync, stores)
                    vec.tensor_copy(high, table_).then_inc(vec_done, 1)
                    settle()
                    vec.tensor_tensor(rest, table_, high, ALU.subtract).then_inc(vec_done, 1)
                    settle()
                    vec.tensor_copy(mid, rest).then_inc(vec_done, 1)
                    settle()
                    vec.tensor_tensor(rest, rest, mid, ALU.subtract).then_inc(vec_done, 1)
                    settle()
                    vec.tensor_copy(low, rest)
                    for k in range(2):
                        making["first"] = name == "gat" and k == 0
                        start_hots(k, k, name)
                        more_hots(J)

                HOT_COUNTS = [(hots_n, 2 * BLOCKS), (filled, 2), (src16_n[0], SLOT), (src16_n[1], SLOT)]

                def start_scans(name):
                    z, keep, n = scan_views(name)
                    vec.memset(z[1][:, :, L - 1:L], 0.0)
                    vec.memset(keep[:, :, 0:1], 0.0)
                    vec.memset(mrun[:, 1, :, L:L + 1], -BIG).then_inc(vec_done, 1)
                    settle()

                def scan_chunk(z, keep, b):
                    flat = z[b].rearrange("p c t -> p (c t)")
                    vec.tensor_tensor_scan(flat, keep.rearrange("p c t -> p (c t)"), flat, 0.0,
                                           ALU.mult, ALU.add).then_inc(chunk_scanned, 1)
                    scanned.up()

                def softmax_pass(name, logits):
                    table, width, scan_dram, C, heads = PASSES[name]
                    z, keep, n = scan_views(name)
                    start_scans(name)

                    def step(k, b, t0):
                        r = rows[0:NP, b, 0:L * width].rearrange("p (t w) -> p t w", w=width)
                        vec.wait_ge(rows_in[b], gathered[b].up(SLOT * (L - PE_COLS[name])))
                        vec.wait_ge(rows_filled, filled.up())
                        start_hots(k + 2, b, name)
                        vec.tensor_scalar(brk[:, :], same[:, bass.ds(t0, L)], -1.0, BIG, ALU.add, ALU.mult)
                        logits(r, t0)
                        vec.tensor_copy(mrun[:, b, 0:heads, 0:1], mrun[:, 1 - b, 0:heads, L:L + 1])
                        for h in range(heads):
                            ins = vec.tensor_tensor_scan(mrun[:, b, h, 1:L + 1], brk[:, :], logit[:, h, :],
                                                         mrun[:, 1 - b, h, L:L + 1], ALU.add, ALU.max)
                        ins.then_inc(vec_done, 1)
                        settle()
                        m_now, m_before = mrun[:, b, 0:heads, 1:L + 1], mrun[:, b, 0:heads, 0:L]
                        vec.tensor_tensor(rw[:, b, 1, 0:heads, :], logit[:, 0:heads, :], m_now, ALU.subtract)
                        vec.tensor_tensor(rw[:, b, 0, 0:heads, :], m_before, m_now, ALU.subtract).then_inc(vec_done, 1)
                        settle()
                        vec.tensor_tensor(rw[:, b, 0, 0:heads, :], rw[:, b, 0, 0:heads, :],
                                          brk[:, :].unsqueeze(1).broadcast_to([NP, heads, L]), ALU.add)\
                            .then_inc(vec_for_act, 1)
                        zh = z[b].rearrange("p (h g) t -> p h g t", g=HG)
                        more_hots(LS)
                        vec.wait_ge(act_for_vec, act_n.up())
                        w = rw[:, b, 1, 0:heads, :]
                        vec.tensor_tensor(zh[:, :, 0:D, :], w.unsqueeze(2).broadcast_to([NP, heads, D, L]),
                                          r[:, :, 0:D].rearrange("p t f -> p f t").unsqueeze(1)
                                          .broadcast_to([NP, heads, D, L]), ALU.mult).then_inc(rows_used, 1)
                        vec.tensor_copy(zh[:, :, D, :], w).then_inc(vec_done, 1)
                        settle()
                        used.up()
                        if scanned.n:
                            vec.wait_ge(chunk_scanned, scanned.at())
                        for h in range(heads):
                            one_head = slice(h * HG, (h + 1) * HG)
                            ins = vec.scalar_tensor_tensor(z[b][:, one_head, 0], z[1 - b][:, one_head, L - 1],
                                                           rw[:, b, 0, h, 0:1], z[b][:, one_head, 0],
                                                           ALU.mult, ALU.add)
                        ins.then_inc(vec_done, 1)
                        settle()
                        vec.wait_ge(keep_ready, kept.up())
                        scan_chunk(z, keep, b)
                        more_hots(J)

                    chunks(vec, [(gathered[0], None), (gathered[1], None), (own, None), (act_n, 2),
                                 (kept, 2), (used, 2), (scanned, 2)] + HOT_COUNTS, step)

                    for h in range(heads):
                        ins = vec.tensor_scalar(diag[:, h, :], ident[0:NP, 0:NP], mrun[:, 0, h, L:L + 1], None,
                                                ALU.mult)
                    ins.then_inc(vec_for_pe, 1)
                    cr = cross[:, 0:heads * NP].rearrange("p (h q) -> p h q", h=heads)
                    ps6 = ps[0:NP, 6, 0:heads * NP].rearrange("p (h q) -> p h q", h=heads)
                    vec.wait_ge(pe_for_vec, pe_n.up())
                    vec.tensor_tensor(cr, ps6, carry_pq[:, :].unsqueeze(1).broadcast_to([NP, heads, NP]), ALU.mult)\
                        .then_inc(vec_done, 1)
                    settle()
                    vec.tensor_tensor(cr, cr, no_carry_pq[:, :].unsqueeze(1).broadcast_to([NP, heads, NP]), ALU.add)\
                        .then_inc(vec_done, 1)
                    settle()
                    vec.tensor_reduce(small[:, 0, 0:heads], cr, X_AXIS, ALU.max).then_inc(vec_done, 1)
                    settle()
                    m_local = local[0:NP, heads * HG:C]
                    vec.wait_ge(local_in, local_n.up(SLOT))
                    vec.tensor_tensor(small[:, 1, 0:heads], small[:, 0, 0:heads], m_local, ALU.max)\
                        .then_inc(vec_done, 1)
                    settle()
                    vec.tensor_tensor(cross[:, heads * NP:heads * NP + heads], m_local, small[:, 1, 0:heads],
                                      ALU.subtract)
                    vec.tensor_tensor(cr, cr, over(small[:, 1, 0:heads], NP), ALU.subtract).then_inc(vec_for_act, 1)
                    vec.wait_ge(act_for_vec, act_n.up())
                    vec.tensor_copy(mended[0:NP, heads * HG:C], small[:, 1, 0:heads])
                    me = mended[0:NP, 0:heads * HG].rearrange("p (h g) -> p h g", g=HG)
                    vec.tensor_tensor(me, local[0:NP, 0:heads * HG].rearrange("p (h g) -> p h g", g=HG),
                                      over(cross[:, heads * NP:heads * NP + heads], HG), ALU.mult)\
                        .then_inc(vec_for_pe, 1)
                    vec.wait_ge(pe_for_vec, pe_n.up())
                    vec.tensor_copy(crossT[:, 0:heads, :],
                                    ps[0:NP, 7, 0:heads * NP].rearrange("p (h q) -> p h q", h=heads))\
                        .then_inc(vec_for_pe, 1)
                    vec.wait_ge(pe_for_vec, pe_n.up())
                    vec.tensor_tensor(mended[0:NP, 0:heads * HG], mended[0:NP, 0:heads * HG],
                                      ps[0:NP, 6, 0:heads * HG], ALU.add).then_inc(vec_for_pool, 1)
                    vec.wait_ge(agg_in, agg_n.up(J * SLOT))

                def finish_sums():
                    vec.wait_ge(pe_for_vec, pe_n.up())
                    vec.wait_ge(local_in, local_n.up(SLOT))
                    vec.tensor_tensor(mended[0:NP, 0:D], local[0:NP, 0:D], ps[0:NP, 6, 0:D], ALU.add)\
                        .then_inc(vec_for_pool, 1)
                    vec.wait_ge(agg_in, agg_n.up(J * SLOT))

                def sum_pass(name):
                    z, keep, n = scan_views(name)
                    start_scans(name)

                    def step(k, b, t0):
                        vec.tensor_scalar(samec[:, b, :], same[:, bass.ds(t0, L)], 1.0, None, ALU.mult)\
                            .then_inc(vec_for_act, 1)
                        gathered[b].up(SLOT * (L - PE_COLS[name]))
                        filled.up()
                        start_hots(k + 2, b, name)
                        more_hots(2 * LS)
                        vec.wait_ge(act_for_vec, act_n.up())
                        vec.wait_ge(chunk_scanned, scanned.at())
                        vec.scalar_tensor_tensor(z[b][:, :, 0], z[1 - b][:, :, L - 1], samec[:, b, 0:1],
                                                 z[b][:, :, 0], ALU.mult, ALU.add).then_inc(vec_done, 1)
                        settle()
                        scan_chunk(z, keep, b)
                        more_hots(J)

                    chunks(vec, [(gathered[0], None), (gathered[1], None), (own, None), (act_n, 2),
                                 (scanned, 2)] + HOT_COUNTS, step)
                    used.up(CH)
                    finish_sums()

                def divide(heads):
                    a = agg[0:NP, :, 0:heads * HG].rearrange("p j (h g) -> p j h g", g=HG)
                    rd = rden[:, :, 0:heads]
                    vec.tensor_scalar(rd, a[:, :, :, D], TINY, None, ALU.max).then_inc(vec_done, 1)
                    settle()
                    vec.reciprocal(rd, rd).then_inc(vec_done, 1)
                    settle()
                    vec.tensor_tensor(rd, rd, over(per_node(SOME), heads), ALU.mult).then_inc(vec_done, 1)
                    settle()
                    return a[:, :, :, 0:D], over(rd, D)

                def layer_norm(ready=vec_done):
                    vec.tensor_reduce(per_node(MEAN), X[:, :, :], X_AXIS, ALU.add).then_inc(vec_done, 1)
                    settle()
                    vec.tensor_scalar(per_node(MEAN), per_node(MEAN), 1.0 / D, None, ALU.mult).then_inc(vec_done, 1)
                    settle()
                    vec.tensor_tensor(X[:, :, :], X[:, :, :], over(per_node(MEAN), D), ALU.subtract)\
                        .then_inc(vec_done, 1)
                    settle()
                    vec.tensor_tensor(work[:, :, :], X[:, :, :], X[:, :, :], ALU.mult).then_inc(vec_done, 1)
                    settle()
                    vec.tensor_reduce(per_node(RSTD), work[:, :, :], X_AXIS, ALU.add).then_inc(vec_done, 1)
                    settle()
                    vec.tensor_scalar(per_node(RSTD), per_node(RSTD), 1.0 / D, LN_EPS, ALU.mult, ALU.add)\
                        .then_inc(vec_for_act, 1)
                    vec.wait_ge(act_for_vec, act_n.up())
                    vec.reciprocal(per_node(RSTD), per_node(RSTD)).then_inc(vec_done, 1)
                    settle()
                    vec.tensor_tensor(X[:, :, :], X[:, :, :], over(per_node(RSTD), D), ALU.mult)\
                        .then_inc(ready, 1)
                    if ready is vec_done:
                        settle()

                used, kept = Count(), Count()
                tabD = tab[:, :, :].rearrange("p j c -> p (j c)")[0:NP, 0:J * D].rearrange("p (j c) -> p j c", c=D)
                tabG = tab[:, :, :].rearrange("p j c -> p (j c)")[0:NP, 0:J * HG].rearrange("p (j c) -> p j c", c=HG)

                vec.wait_ge(starts_cleared, SLOT * (1 + T * D // (2 * L * C0)))
                begin_pass("gat", tab[0:NP, :, 0:D + H], 1)
                fill_edges(H, D + H)

                def gat_logits(r, t0):
                    ed = edges_d[0:NP, bass.ds(t0 * H, L * H)].rearrange("p (t h) -> p h t", h=H)
                    vec.tensor_tensor(logit[:, :, :], r[:, :, D:D + H].rearrange("p t h -> p h t"), ed, ALU.add)\
                        .then_inc(vec_done, 1)
                    settle()
                    vec.scalar_tensor_tensor(logit[:, :, :], logit[:, :, :], 0.2, logit[:, :, :], ALU.mult, ALU.max)\
                        .then_inc(vec_done, 1)
                    settle()

                softmax_pass("gat", gat_logits)
                num, rd = divide(H)
                vec.tensor_tensor(aggn[:, :, :].rearrange("p j (h f) -> p j h f", h=H), num, rd, ALU.mult)\
                    .then_inc(vec_for_pe, 1)
                vec.wait_ge(group_copied, group_n.up(3 * len(GROUPS)))
                vec.wait_ge(act_for_vec, act_n.up())
                vec.tensor_tensor(work[:, :, :], aggn[:, :, 0:D], aggn[:, :, 3 * D:4 * D], ALU.mult)\
                    .then_inc(vec_done, 1)
                settle()
                vec.tensor_tensor(work[:, :, :], work[:, :, :], aggn[:, :, 2 * D:3 * D], ALU.add)\
                    .then_inc(vec_for_act, 1)
                vec.wait_ge(act_for_vec, act_n.up())
                vec.tensor_tensor(work2[:, :, :], X[:, :, :], work[:, :, :], ALU.subtract).then_inc(vec_done, 1)
                settle()
                vec.tensor_tensor(work2[:, :, :], work2[:, :, :], aggn[:, :, D:2 * D], ALU.mult).then_inc(vec_done, 1)
                settle()
                vec.tensor_tensor(work[:, :, :], work[:, :, :], work2[:, :, :], ALU.add).then_inc(vec_done, 1)
                settle()
                vec.tensor_scalar(work2[:, :, :], work[:, :, :], 0.0, None, ALU.min).then_inc(vec_for_act, 1)
                vec.wait_ge(act_for_vec, act_n.up())
                vec.scalar_tensor_tensor(work[:, :, :], work[:, :, :], 0.0, work2[:, :, :], ALU.max, ALU.add)\
                    .then_inc(vec_done, 1)
                settle()
                vec.scalar_tensor_tensor(X[:, :, :], work[:, :, :], -1.0, X[:, :, :], ALU.add, ALU.add)\
                    .then_inc(vec_done, 1)
                settle()
                layer_norm()

                vec.tensor_copy(aggn[:, :, 0:D], X[:, :, :])
                vec.tensor_tensor(tabD, X[:, :, :], over(per_node(DINV), D), ALU.mult).then_inc(vec_for_sync, 1)
                begin_pass("cheb0", tabD, 2)
                sum_pass("cheb0")
                vec.tensor_tensor(work[:, :, :], agg[0:NP, :, 0:D], over(per_node(DSOME), D), ALU.mult)
                vec.tensor_scalar(work2[:, :, :], X[:, :, :], scal[:, 4:5], None, ALU.mult).then_inc(vec_done, 1)
                settle()
                vec.scalar_tensor_tensor(aggn[:, :, D:2 * D], work[:, :, :], scal[:, 3:4], work2[:, :, :],
                                         ALU.mult, ALU.add).then_inc(vec_done, 1)
                settle()
                vec.tensor_tensor(tabD, aggn[:, :, D:2 * D], over(per_node(DINV), D), ALU.mult)\
                    .then_inc(vec_for_sync, 1)
                begin_pass("cheb1", tabD, 3)
                sum_pass("cheb1")
                vec.memset(bigT[3 * D:3 * D + 1, :], 1.0)
                vec.tensor_tensor(work[:, :, :], agg[0:NP, :, 0:D], over(per_node(DSOME), D), ALU.mult)
                vec.scalar_tensor_tensor(work2[:, :, :], aggn[:, :, D:2 * D], scal[:, 6:7], X[:, :, :],
                                         ALU.mult, ALU.subtract).then_inc(vec_done, 1)
                settle()
                vec.scalar_tensor_tensor(aggn[:, :, 2 * D:3 * D], work[:, :, :], scal[:, 5:6], work2[:, :, :],
                                         ALU.mult, ALU.add).then_inc(vec_for_pe, 1)
                vec.wait_ge(group_copied, group_n.up(3 * len(GROUPS)))
                vec.tensor_copy(tabD, aggn[:, :, 0:D]).then_inc(vec_for_sync, 1)
                vec.tensor_copy(scat[0:NP, :, :], aggn[:, :, D:2 * D]).then_inc(vec_for_sync, 1)
                begin_pass("gatv2", tabD, 5)
                fill_edges(D, 0)

                def gatv2_logits(r, t0):
                    ed = edges_d[0:NP, bass.ds(t0 * D, L * D)].rearrange("p (t c) -> p t c", c=D)
                    vec.tensor_tensor(prod[:, :, :], r, ed, ALU.add).then_inc(vec_done, 1)
                    settle()
                    vec.scalar_tensor_tensor(prod[:, :, :], prod[:, :, :], 0.2, prod[:, :, :], ALU.mult, ALU.max)\
                        .then_inc(vec_done, 1)
                    settle()
                    vec.tensor_tensor(prod[:, :, :], prod[:, :, :], att1[:, :].unsqueeze(1).broadcast_to([NP, L, D]),
                                      ALU.mult).then_inc(vec_done, 1)
                    settle()
                    vec.tensor_reduce(logit[:, 0, :], prod[:, :, :], X_AXIS, ALU.add).then_inc(vec_done, 1)
                    settle()

                softmax_pass("gatv2", gatv2_logits)
                num, rd = divide(1)
                vec.tensor_tensor(work[:, :, :], num[:, :, 0, :], rd[:, :, 0, :], ALU.mult).then_inc(vec_done, 1)
                settle()
                vec.tensor_tensor(X[:, :, :], X[:, :, :], work[:, :, :], ALU.add).then_inc(vec_done, 1)
                settle()
                layer_norm(vec_for_pe)

                vec.tensor_scalar(coord, attr[:, :, :].rearrange("p t d -> p d t"), 1.0 / WIDTH, None, ALU.mult)\
                    .then_inc(vec_done, 1)
                settle()
                vec.tensor_scalar(cell, coord, -0.5, -1.5, ALU.is_ge, ALU.add).then_inc(vec_done, 1)
                settle()
                vec.scalar_tensor_tensor(cell, coord, 0.5, cell, ALU.is_ge, ALU.add).then_inc(vec_done, 1)
                settle()
                vec.scalar_tensor_tensor(offset[:, 0, :], cell[:, 1, :], float(CELLS), cell[:, 0, :], ALU.mult, ALU.add)\
                    .then_inc(vec_done, 1)
                settle()
                vec.scalar_tensor_tensor(offset[:, 0, :], dst_i[:, :], float(CELLS * CELLS), offset[:, 0, :],
                                         ALU.mult, ALU.add).then_inc(vec_done, 1)
                settle()
                vec.tensor_scalar(cell_i, offset[:, 0, :], 1.5 * (CELLS + 1), None, ALU.add).then_inc(cells_made, 1)
                vec.tensor_tensor(tents[:, :, 0, :], coord, cell, ALU.subtract).then_inc(vec_done, 1)
                settle()
                vec.tensor_scalar(tents[:, :, 1, :], tents[:, :, 0, :], -1.0, None, ALU.add).then_inc(vec_done, 1)
                settle()
                vec.scalar_tensor_tensor(tents, tents, -1.0, tents, ALU.mult, ALU.max).then_inc(vec_done, 1)
                settle()
                vec.tensor_scalar(tents, tents, -1.0, 1.0, ALU.mult, ALU.add).then_inc(vec_done, 1)
                settle()
                vec.tensor_scalar(tents, tents, 0.0, None, ALU.max).then_inc(vec_done, 1)
                settle()
                for a in range(2):
                    for b in range(2):
                        ins = vec.tensor_tensor(basis[:, :, 2 * a + b], tents[:, 0, a, :], tents[:, 1, b, :], ALU.mult)
                ins.then_inc(vec_done, 1)
                settle()
                for b in range(2):
                    vec.wait_ge(scan_stored[b], len(ORDER[:-1]) * SLOT * ((CH + 1 - b) // 2))
                slot_n = [Count() for c in range(SLOTS)]
                hot_used = Count()

                def spline_turn(t0, first):
                    if not first:
                        vec.wait_ge(onehot_ready, made.at())
                        vec.wait_ge(act_onehot_ready, act_made.at())
                    now = src_f[:, bass.ds(t0, L)]
                    vec.tensor_scalar(srcc[:, :, :].rearrange("p s t -> p (s t)"), now, 1.0, None, ALU.mult)
                    vec.tensor_scalar(srcc_neg[:, :, :].rearrange("p s t -> p (s t)"), now, -1.0, None, ALU.mult)\
                        .then_inc(sources_ready, 1)
                    for c in range(SLOTS):
                        slot = slots[0:NP, c, :].rearrange("p (t k f) -> p t k f", k=CORNERS, f=D)
                        msg = prod[:, c * LS:(c + 1) * LS, :]
                        high, mid, low = (parts[:, c, :, i * D:(i + 1) * D] for i in range(3))

                        def one_hot(t):
                            hot_used.up()
                            if (c, t) in ACT_HOT:
                                act_made.up()
                                return
                            made.up()
                            if not first or c >= HOT_LAG[c]:
                                vec.wait_ge(onehot_used, hot_used.at(-HOT_LAG[c] * LS))
                            vec.tensor_scalar(hots[c % 2][t], nodes16[:, :], srcc[:, c, t:t + 1], None, ALU.is_equal)\
                                .then_inc(onehot_ready, 1)

                        vec.wait_ge(slot_in[c], slot_n[c].up(SLOT * LS))
                        vec.tensor_tensor(slot, slot, over(basis[:, bass.ds(t0 + c * LS, LS), :], D), ALU.mult)\
                            .then_inc(vec_done, 1)
                        if c == 0:
                            vec.wait_ge(sources_ready, sources_n.up())
                        one_hot(0)
                        settle()
                        vec.tensor_reduce(msg, slot.rearrange("p t k f -> p t f k"), X_AXIS, ALU.add)\
                            .then_inc(slot_used, 1)
                        slots_n.up()
                        one_hot(1)
                        vec.wait_ge(slot_used, slots_n.at())
                        vec.tensor_copy(high, msg).then_inc(vec_done, 1)
                        one_hot(2)
                        settle()
                        vec.tensor_tensor(msg, msg, high, ALU.subtract).then_inc(vec_done, 1)
                        one_hot(3)
                        settle()
                        vec.tensor_copy(mid, msg).then_inc(vec_done, 1)
                        settle()
                        vec.tensor_tensor(msg, msg, mid, ALU.subtract).then_inc(vec_done, 1)
                        settle()
                        vec.tensor_copy(low, msg).then_inc(parts_ready, 1)
                        one_hot(4)

                slots_n, made, act_made, sources_n = Count(), Count(), Count(), Count()
                before = own.n
                vec.wait_ge(nodes16_made, 1)
                spline_turn(0, True)
                with vec.Fori(0, CH - 1) as turn:
                    per_turn = [(slots_n, SLOTS), (sources_n, 1), (made, L - len(ACT_HOT)), (act_made, len(ACT_HOT)), (hot_used, L), (own, own.n - before)] + \
                        [(c, SLOT * LS) for c in slot_n]
                    for c, per in per_turn:
                        c.enter(turn, per)
                    spline_turn(turn * L + L, False)
                for c, per in per_turn:
                    c.leave(CH - 1)
                vec.wait_ge(onehot_used, T)
                vec.tensor_copy(bigT[0:3 * D, :], ps[0:3 * D, 0:7, :].rearrange("p n c -> p (n c)")[:, 0:N])\
                    .then_inc(vec_for_pe, 1)
                vec.wait_ge(group_copied, group_n.up(2 * len(GROUPS) + J))
                vec.tensor_tensor(X[:, :, :], X[:, :, :], work2[:, :, :], ALU.add).then_inc(vec_done, 1)
                settle()
                layer_norm()

                vec.tensor_tensor(work[:, :, :], X[:, :, :], X[:, :, :], ALU.mult).then_inc(vec_done, 1)
                settle()
                vec.tensor_reduce(per_node(RSTD), work[:, :, :], X_AXIS, ALU.add).then_inc(vec_for_act, 1)
                vec.wait_ge(act_for_vec, act_n.up())
                vec.tensor_scalar(per_node(RN), per_node(RSTD), NORM_EPS, None, ALU.max).then_inc(vec_done, 1)
                settle()
                vec.reciprocal(per_node(RN), per_node(RN)).then_inc(vec_done, 1)
                settle()
                vec.tensor_copy(tabG[:, :, 0:D], X[:, :, :])
                vec.tensor_copy(tabG[:, :, D:HG], over(per_node(RN), 1)).then_inc(vec_for_sync, 1)
                vec.tensor_tensor(scat[0:NP, :, :], X[:, :, :], over(per_node(RN), D), ALU.mult)\
                    .then_inc(vec_for_sync, 1)
                vec.wait_ge(vec_for_sync, 7)
                vec.tensor_tensor(work[:, :, :], scat[0:NP, :, :], scat[0:NP, :, :], ALU.mult).then_inc(vec_done, 1)
                settle()
                vec.tensor_reduce(per_node(TMP), work[:, :, :], X_AXIS, ALU.add).then_inc(vec_done, 1)
                settle()
                vec.tensor_scalar(per_node(SELF), per_node(TMP), scal[:, 1:2], None, ALU.mult)
                begin_pass("agnn", tabG, 7)
                fill_edges(D, 0)

                def agnn_logits(r, t0):
                    ed = edges_d[0:NP, bass.ds(t0 * D, L * D)].rearrange("p (t c) -> p t c", c=D)
                    vec.tensor_tensor(prod[:, :, :], r[:, :, 0:D], ed, ALU.mult).then_inc(vec_done, 1)
                    settle()
                    vec.tensor_reduce(logit[:, 0, :], prod[:, :, :], X_AXIS, ALU.add).then_inc(vec_done, 1)
                    settle()
                    vec.scalar_tensor_tensor(logit[:, 0, :], logit[:, 0, :], scal[:, 1:2], r[:, :, D],
                                             ALU.mult, ALU.mult).then_inc(vec_done, 1)
                    settle()

                softmax_pass("agnn", agnn_logits)
                vec.tensor_tensor(per_node(TMP), agg[0:NP, :, HG], per_node(SOME), ALU.mult)
                vec.tensor_scalar(per_node(MEAN), per_node(SOME), -1.0, BIG, ALU.add, ALU.mult).then_inc(vec_done, 1)
                settle()
                vec.tensor_tensor(per_node(TMP), per_node(TMP), per_node(MEAN), ALU.add).then_inc(vec_done, 1)
                settle()
                vec.tensor_tensor(per_node(MEAN), per_node(TMP), per_node(SELF), ALU.max).then_inc(vec_done, 1)
                settle()
                vec.tensor_tensor(nodew[:, 0, :], per_node(TMP), per_node(MEAN), ALU.subtract)
                vec.tensor_tensor(nodew[:, 1, :], per_node(SELF), per_node(MEAN), ALU.subtract).then_inc(vec_for_act, 1)
                vec.wait_ge(act_for_vec, act_n.up())
                vec.tensor_tensor(work[:, :, :], agg[0:NP, :, 0:D], over(nodew[:, 0, :], D), ALU.mult)
                vec.tensor_tensor(work2[:, :, :], X[:, :, :], over(nodew[:, 1, :], D), ALU.mult)
                vec.tensor_tensor(per_node(TMP), agg[0:NP, :, D], nodew[:, 0, :], ALU.mult).then_inc(vec_done, 1)
                settle()
                vec.tensor_tensor(work[:, :, :], work[:, :, :], work2[:, :, :], ALU.add)
                vec.tensor_tensor(per_node(TMP), per_node(TMP), nodew[:, 1, :], ALU.add).then_inc(vec_done, 1)
                settle()
                vec.tensor_scalar(per_node(TMP), per_node(TMP), NORM_EPS, None, ALU.max).then_inc(vec_done, 1)
                settle()
                vec.reciprocal(per_node(TMP), per_node(TMP)).then_inc(vec_done, 1)
                settle()
                vec.tensor_tensor(work[:, :, :], work[:, :, :], over(per_node(TMP), D), ALU.mult).then_inc(vec_done, 1)
                settle()
                vec.scalar_tensor_tensor(work[:, :, :], work[:, :, :], 0.0, X[:, :, :], ALU.max, ALU.add)\
                    .then_inc(vec_done, 1)
                settle()
                vec.tensor_tensor(X[:, :, :], X[:, :, :], work[:, :, :], ALU.add).then_inc(vec_done, 1)
                settle()
                layer_norm(vec_for_sync)


_INS = ["x", "src", "dst", "edge_attr_2", "L0_gnn_W_gat", "L0_gnn_attn_l", "L0_gnn_attn_r", "L0_gnn_W_ih",
        "L0_gnn_W_hh", "L0_gnn_b_ih", "L0_gnn_b_hh", "L1_gnn_lambda_max", "L1_gnn_cheb_W", "L1_gnn_cheb_b",
        "L1_gnn_src_W", "L1_gnn_src_b", "L1_gnn_dst_W", "L1_gnn_dst_b", "L1_gnn_attn", "L2_gnn_weight",
        "L3_gnn_beta"]


def kernel(**inputs):
    import numpy as np
    import concourse.bacc as bacc
    from concourse import mybir as mb
    from concourse.bass_utils import run_bass_kernel_spmd

    nc = bacc.Bacc("TRN2", target_bir_lowering=False, num_devices=1)
    arrays, args = {}, []
    for name in _INS:
        a = np.ascontiguousarray(inputs[name])
        arrays[f"in_{name}"] = a
        args.append(nc.dram_tensor(f"in_{name}", a.shape, mb.dt.from_np(a.dtype), kind="ExternalInput").ap())
    shape = inputs["x"].shape
    out = nc.dram_tensor("out", shape, mb.dt.float32, kind="ExternalOutput").ap()
    gnn_kernel(nc, *args, out)
    r = run_bass_kernel_spmd(nc, [arrays], core_ids=[0])
    return r.results[0]["out"]
```

```python
from contextlib import ExitStack

import concourse.bass as bass
from concourse import mybir

F32 = mybir.dt.float32
I32 = mybir.dt.int32
BF16 = mybir.dt.bfloat16
F16 = mybir.dt.float16
ALU = mybir.AluOpType
ACT = mybir.ActivationFunctionType
X_AXIS = mybir.AxisListType.X

BIG = 1.0e30
TINY = 1.0e-30
SKIP = 1.0e6
LN_EPS = 1.0e-5
NORM_EPS = 1.0e-12


class Count:

    def __init__(self, n=0):
        self.n = n
        self.reg = None
        self.per = 0

    def up(self, k=1):
        self.n += k
        return self.at()

    def at(self, ahead=0):
        if self.reg is None:
            return self.n + ahead
        return self.reg * self.per + (self.n + ahead)

    def enter(self, reg, per):
        self.reg, self.per, self.first = reg, per, self.n

    def leave(self, turns):
        assert self.n - self.first == self.per, (self.n - self.first, self.per)
        self.n = self.first + self.per * turns
        self.reg = None


def gnn_kernel(nc, x, src, dst, edge_attr, W_gat, attn_l, attn_r, W_ih, W_hh, b_ih, b_hh,
               lambda_max, cheb_W, cheb_b, src_W, src_b, dst_W, dst_b, attn, weight, beta, out):
    N, D = x.shape
    E = src.shape[0]
    H = attn_l.shape[0]
    P = 128
    NP = 125
    J = N // NP
    T = E // NP
    L = 25
    CH = T // L
    TURNS = (CH - 5) // 2
    HG = D + 1
    C0 = H * HG + H
    C1 = HG + 1
    W0 = D + 2 * H
    KV, KU = weight.shape[1], weight.shape[0]
    K2 = KU * KV
    CELLS = KU - 1
    CORNERS = 4
    YROW = CELLS * CELLS * CORNERS * D
    assert K2 * D == 512 and KU == KV == 4 and L == J and H * D == P
    assert N == NP * J and E == NP * T and T == CH * L and CH == 2 * TURNS + 5
    WIDTH = 2.0 / (KU - 1)
    assert KU == 4
    GT = 4
    GROUPS = [range(g, min(g + GT, J)) for g in range(0, J, GT)]
    last = len(GROUPS) - 1
    SPLINE_ORDER = [("transpose", 0), ("product", 0), ("transpose", 1)] + \
        [step for g in range(2, last + 1) for step in (("transpose", g), ("product", g - 1))] + [("product", last)]
    MID = N // 2
    assert MID <= 2048
    BANK = 512
    LS = 5
    SLOTS = L // LS
    BLOCKS = J // LS
    ACT_HOT = [(c, t) for c in range(SLOTS) for t in range(LS) if t == 4]
    PE_COLS = {"gat": 8, "cheb0": 11, "cheb1": 11, "gatv2": 10, "agnn": 10}
    PE_MOST = max(PE_COLS.values())
    ACT_ROWS = {"gat": 2, "cheb0": 0, "cheb1": 0, "gatv2": 3, "agnn": 2}
    PG = 4
    SLOT = 16

    with ExitStack() as ctx:
        def sb(name, shape, dt=F32):
            return ctx.enter_context(nc.sbuf_tensor(name, shape, dt))

        def sem(name):
            return ctx.enter_context(nc.semaphore(name))

        def dram(name, shape, dt=F32):
            return nc.dram_tensor(name, shape, dt, kind="Internal").ap()

        tab0_dram = dram("tab0_dram", (N, W0))
        tab_cheb_dram = [dram("tab_cheb0_dram", (N, D)), dram("tab_cheb1_dram", (N, D))]
        tab_fsrc_dram = dram("tab_fsrc_dram", (N, D))
        tab_fdst_dram = dram("tab_fdst_dram", (N, D))
        tab_y_dram = dram("tab_y_dram", (N * CELLS * CELLS, CORNERS * D))
        cell_dram = dram("cell_dram", (E,), I32)
        srcT_dram = dram("srcT_dram", (T, NP), F16)
        tab_x3_dram = dram("tab_x3_dram", (N, HG))
        tab_xn_dram = dram("tab_xn_dram", (N, D))
        starts4_dram = dram("starts4_dram", (P * T, H))
        starts32_dram = dram("starts32_dram", (P * T, D))
        scan0_dram = dram("scan0_dram", (P * T, C0))
        scan1_dram = dram("scan1_dram", (P * T, C1))
        scanD_dram = dram("scanD_dram", (P * T, D))

        dst_i = sb("dst_i", [NP, T], I32)
        fence = sb("fence", [P, 2])
        same = sb("same", [NP, T])
        ident = sb("ident", [P, P])
        ones = sb("ones", [P, P])
        before_qp = sb("before_qp", [P, P])
        before_pq = sb("before_pq", [P, P])
        shift = sb("shift", [P, P])
        carry_qp = sb("carry_qp", [NP, NP])
        carry_pq = sb("carry_pq", [NP, NP])
        no_carry_pq = sb("no_carry_pq", [NP, NP])
        ends = sb("ends", [NP, 4])
        node_i = sb("node_i", [P, J], I32)
        node_f = sb("node_f", [NP, J])
        base_i = sb("base_i", [P, 1], I32)
        base_f = sb("base_f", [NP, 1])
        row_of = sb("row_of", [P, J], I32)
        first_i = sb("first_i", [P, 1], I32)
        end_i = sb("end_i", [P, J], I32)
        start_i = sb("start_i", [P, J], I32)
        mend_get_i = sb("mend_get_i", [P, 1], I32)
        mend_put_i = sb("mend_put_i", [P, 1], I32)
        nodew = sb("nodew", [NP, 13, J])
        idx = sb("idx", [P, 2, L], I32)
        rows = sb("rows", [P, 2, L * W0])
        scan = sb("scan", [P, 2, L * C0])
        edges_d = sb("edges_d", [P, T * D])
        samec = sb("samec", [NP, 2, L])
        brk = sb("brk", [NP, L])
        mrun = sb("mrun", [NP, 2, H, L + 1])
        logit = sb("logit", [NP, H, L])
        rw = sb("rw", [NP, 2, 2, H, L])
        prod = sb("prod", [NP, L, D])
        local = sb("local", [P, C0])
        mended = sb("mended", [P, C0])
        diag = sb("diag", [NP, H, NP])
        cross = sb("cross", [NP, 2 * H * NP + H])
        crossT = cross[:, H * NP + H:].rearrange("p (h q) -> p h q", h=H)
        three = cross[:, :].bitcast(BF16)
        small = sb("small", [NP, 4, H])
        X = sb("X", [NP, J, D])
        agg = sb("agg", [P, J, C0])
        aggn = sb("aggn", [NP, J, P])
        bigT = sb("bigT", [P, J * NP])
        smallT = sb("smallT", [P, J * NP])
        tab = sb("tab", [P, J, W0])
        scat = sb("scat", [P, J, D])
        work = sb("work", [NP, J, D])
        work2 = sb("work2", [NP, J, D])
        rden = sb("rden", [NP, J, H])
        first_row = sb("first_row", [P, W0])
        attr = sb("attr", [NP, T, 2])
        src_f = sb("src_f", [NP, T])
        srcc = sb("srcc", [NP, SLOTS, LS])
        srcc_neg = sb("srcc_neg", [NP, SLOTS, LS])
        nodes16 = sb("nodes16", [NP, N], F16)
        node_c = sb("node_c", [NP, J])
        node_c_neg = sb("node_c_neg", [NP, J])
        src16 = sb("src16", [P, 2, PE_MOST * NP], F16)
        stacks = sb("stacks", [P, D + HG + D + H], BF16)
        stack3 = sb("stack3", [3 * D, D])
        w_gat = sb("w_gat", [D, P])
        att_lr = sb("att_lr", [D, 2, P])
        w_lr = sb("w_lr", [D, 2 * H])
        w_ih = sb("w_ih", [3 * D, P])
        w_hh = sb("w_hh", [3 * D, D])
        w_ihT = sb("w_ihT", [P, 3 * D])
        w_gatBD = sb("w_gatBD", [P, P])
        w_agg = sb("w_agg", [P, P])
        w_x = sb("w_x", [D + 1, P])
        b_row = sb("b_row", [D + 1, 6 * D])
        w_cheb = sb("w_cheb", [3 * D + 1, D])
        w_sd = sb("w_sd", [D + 1, 2 * D])
        att1 = sb("att1", [NP, D])
        w_spl = sb("w_spl", [D, K2, D])
        scal = sb("scal", [NP, 8])
        ps = ctx.enter_context(nc.psum_tensor("ps", [P, 8, 512], F32))

        consts_made = sem("consts_made")
        cleared = sem("cleared")
        scan_cleared = sem("scan_cleared")
        graph_loaded = sem("graph_loaded")
        x_loaded = sem("x_loaded")
        weights_loaded = sem("weights_loaded")
        starts4_cleared = sem("starts4_cleared")
        starts32_cleared = sem("starts32_cleared")
        vec_done = sem("vec_done")
        vec_for_pe = sem("vec_for_pe")
        pe_for_vec = sem("pe_for_vec")
        group_in_psum = sem("group_in_psum")
        group_copied = sem("group_copied")
        vec_for_act = sem("vec_for_act")
        act_for_vec = sem("act_for_vec")
        vec_for_sync = sem("vec_for_sync")
        vec_for_pool = sem("vec_for_pool")
        cells_made = sem("cells_made")
        cells_stored = sem("cells_stored")
        products_stored = [sem("products_stored0"), sem("products_stored1")]
        table_stored = sem("table_stored")
        dst_rows_in = [sem(f"dst_rows_in{i}") for i in range(5)]
        scattered = sem("scattered")
        first_in = sem("first_in")
        edges_in = [sem("edges_in0"), sem("edges_in1")]
        local_in = sem("local_in")
        agg_in = [sem(f"agg_in{m}") for m in range(J // LS)]
        block_ready = sem("block_ready")
        idx_in = [sem("idx_in0"), sem("idx_in1")]
        rows_in = [sem("rows_in0"), sem("rows_in1")]
        srcT_made = sem("srcT_made")
        srcT_turned = sem("srcT_turned")
        srcT_ready = sem("srcT_ready")
        srcT_stored = sem("srcT_stored")
        src16_in = [sem("src16_in0"), sem("src16_in1")]
        source_hots_ready = sem("source_hots_ready")
        source_half_ready = sem("source_half_ready")
        source_act_ready = sem("source_act_ready")
        source_hots_used = sem("source_hots_used")
        parts_copied = sem("parts_copied")
        rows_gathered = sem("rows_gathered")
        rows_filled = sem("rows_filled")
        nodes16_made = sem("nodes16_made")
        fence_done = sem("fence_done")
        rows_used = sem("rows_used")
        keep_ready = sem("keep_ready")
        chunk_scanned = sem("chunk_scanned")
        rows_turned = sem("rows_turned")
        scan_stored = [sem("scan_stored0"), sem("scan_stored1")]
        slot_in = [sem(f"slot_in{c}") for c in range(SLOTS)]
        slot_idx_in = [sem(f"slot_idx_in{c}") for c in range(SLOTS)]
        slot_used = sem("slot_used")
        sources_ready = sem("sources_ready")
        parts_ready = sem("parts_ready")
        onehot_ready = sem("onehot_ready")
        act_onehot_ready = sem("act_onehot_ready")
        half_hot_ready = sem("half_hot_ready")
        onehot_used = sem("onehot_used")
        out_stored = sem("out_stored")

        src_grid = src.rearrange("(p t) -> p t", t=T)
        dst_grid = dst.rearrange("(p t) -> p t", t=T)
        cell_grid = cell_dram.rearrange("(p t) -> p t", t=T)

        def nodes(a):
            return a.rearrange("(p j) c -> p (j c)", j=J)


        def chunks(eng, counts, step, between=None):
            before = [c.n for c, per in counts]
            step(0, 0, 0)
            step(1, 1, L)
            if between:
                between()
            counts = [(c, c.n - n if per is None else per) for (c, per), n in zip(counts, before)]
            with eng.Fori(0, TURNS) as turn:
                for c, per in counts:
                    c.enter(turn, per)
                step(2, 0, turn * (2 * L) + 2 * L)
                step(3, 1, turn * (2 * L) + 3 * L)
            for c, per in counts:
                c.leave(TURNS)
            for k in range(CH - 3, CH):
                step(k, k % 2, k * L)

        PASSES = {
            "gat": (tab0_dram, W0, scan0_dram, C0, H),
            "cheb0": (tab_cheb_dram[0], D, scanD_dram, D, 0),
            "cheb1": (tab_cheb_dram[1], D, scanD_dram, D, 0),
            "gatv2": (tab_fsrc_dram, D, scan1_dram, C1, 1),
            "agnn": (tab_x3_dram, HG, scan1_dram, C1, 1),
        }
        ORDER = list(PASSES)
        FILLS = [(0, T // 2), (T // 2, T)]
        GATHERED = {name: HG if name == "agnn" else D + H if name == "gat" else D for name in PASSES}
        STACKS = {D: stacks[0:3 * D, 0:D], HG: stacks[0:3 * HG, D:D + HG],
                  D + H: stacks[0:3 * (D + H), D + HG:2 * D + HG + H]}

        def table_parts(name):
            w = GATHERED[name]
            return nodes16[:, :].bitcast(BF16)[:, 0:J * 3 * w].rearrange("p (j c) -> p j c", j=J)

        def flat2(t):
            return t[0:NP, :, :].rearrange("p a b -> p (a b)")

        def source_hots(name):
            if name == "gat":
                lots = [flat2(agg), flat2(aggn), bigT[0:NP, :], edges_d[0:NP, T * H + 3 * H * HG * L:],
                        flat2(work), flat2(work2), flat2(prod)]
            elif name in ("cheb0", "cheb1"):
                lots = [edges_d[0:NP, :], flat2(agg), flat2(work), flat2(work2)]
            else:
                lots = [flat2(agg), flat2(aggn), smallT[0:NP, :], scan[0:NP, 0, L * C1:], scan[0:NP, 1, L * C1:],
                        flat2(work), flat2(work2)]
            n = PE_COLS[name] * NP
            cut = [a.bitcast(BF16)[:, i * n:(i + 1) * n] for a in lots for i in range(2 * a.shape[1] // n)]
            return cut[0:J]

        def banks(name, b):
            n = PE_COLS[name]
            return [(3 * b + i, a, min(PG, n - a)) for i, a in enumerate(range(0, n, PG))]

        def scan_views(name):
            C = max(PASSES[name][4], 0) * HG or D
            free = edges_d[0:NP, T * H:] if name == "gat" else bigT[0:NP, :]
            z = [free[:, b * C * L:(b + 1) * C * L].rearrange("p (c t) -> p c t", t=L) for b in range(2)]
            return z, free[:, 2 * C * L:3 * C * L].rearrange("p (c t) -> p c t", t=L), C

        staged = edges_d[0:NP, 0:2 * LS * YROW].rearrange("p (b j c) -> p b j c", b=2, j=LS)
        slots = edges_d[:, 0:SLOTS * LS * CORNERS * D].rearrange("p (s c) -> p s c", s=SLOTS)
        at = 2 * LS * YROW
        basis = edges_d[0:NP, at:at + T * CORNERS].rearrange("p (t k) -> p t k", k=CORNERS)
        tents = bigT[0:NP, 0:4 * T].rearrange("p (d a t) -> p d a t", d=2, a=2)
        free = aggn[:, :, :].rearrange("p j c -> p (j c)")
        coord, cell, offset = (free[:, i * 2 * T:(i + 1) * 2 * T].rearrange("p (d t) -> p d t", d=2) for i in range(3))
        cell_i = free[:, 6 * T:7 * T].bitcast(I32)
        parts = agg[0:NP, :, :].rearrange("p j c -> p (j c)").bitcast(BF16)[:, 0:SLOTS * LS * 3 * D]\
            .rearrange("p (s t c) -> p s t c", s=SLOTS, t=LS)
        NA = N + N % 2

        def lay(t, at, count):
            return [t.bitcast(BF16)[0:NP, at + i * NA:at + i * NA + N] for i in range(count)]

        hots = [lay(scan[:, :, :].rearrange("p b c -> p (b c)"), 0, 4) + lay(bigT[:, :], 0, 1),
                lay(edges_d[:, :], 2 * SLOTS * LS * CORNERS * D, LS)]
        half_hot = lay(agg[:, :, :].rearrange("p j c -> p (j c)"), SLOTS * LS * 3 * D, 1)[0]
        assert 2 * SLOTS * LS * CORNERS * D + LS * NA <= 2 * at
        HOT_LAG = [1, 3] + [2] * (SLOTS - 2)
        assert SLOTS % 2 == 1

        with nc.Block() as block:

            @block.sync
            def _(sp):
                vec_sync, scanned = Count(), Count()
                gathered = [Count(), Count()]

                sp.dma_start(dst_i[:, :], dst_grid).then_inc(graph_loaded, SLOT)
                sp.dma_start(src_f[:, :].bitcast(I32), src_grid).then_inc(weights_loaded, SLOT)
                sp.dma_start(X[:, :, :].rearrange("p j c -> p (j c)"), nodes(x)).then_inc(x_loaded, SLOT)
                for t, a in [
                    (w_gat[:, :], W_gat),
                    (att_lr[:, 0, :], attn_l.rearrange("h f -> (h f)").partition_broadcast(D)),
                    (att_lr[:, 1, :], attn_r.rearrange("h f -> (h f)").partition_broadcast(D)),
                    (w_ih[:, :], W_ih),
                    (w_hh[:, :], W_hh),
                    (b_row[D:D + 1, 0:3 * D], b_ih.rearrange("(a n) -> a n", a=1)),
                    (b_row[D:D + 1, 3 * D:6 * D], b_hh.rearrange("(a n) -> a n", a=1)),
                    (w_cheb[0:3 * D, :], cheb_W),
                    (w_cheb[3 * D:3 * D + 1, :], cheb_b.rearrange("(a n) -> a n", a=1)),
                    (w_sd[0:D, 0:D], src_W),
                    (w_sd[0:D, D:2 * D], dst_W),
                    (w_sd[D:D + 1, 0:D], src_b.rearrange("(a n) -> a n", a=1)),
                    (w_sd[D:D + 1, D:2 * D], dst_b.rearrange("(a n) -> a n", a=1)),
                    (att1[:, :], attn.rearrange("h f -> (h f)").partition_broadcast(NP)),
                    (scal[:, 0:1], lambda_max.partition_broadcast(NP)),
                    (scal[:, 1:2], beta.partition_broadcast(NP)),
                    (attr[:, :, :].rearrange("p t c -> p (t c)"), edge_attr.rearrange("(p t) c -> p (t c)", t=T)),
                ]:
                    sp.dma_start(t, a).then_inc(weights_loaded, SLOT)
                for u in range(KU):
                    sp.dma_start(w_spl[:, u * KV:(u + 1) * KV, :], weight[u].rearrange("v f o -> f v o"))\
                        .then_inc(weights_loaded, SLOT)
                sp.wait_ge(scan_cleared, 1)
                sp.dma_start(starts4_dram.rearrange("(p t) c -> p (t c)", t=T), scan[:, 0, 0:T * H])\
                    .then_inc(starts4_cleared, SLOT)
                def store_table(a, t):
                    sp.wait_ge(vec_for_sync, vec_sync.up())
                    sp.dma_start(nodes(a), t).then_inc(table_stored, SLOT)

                def load_edges(a, width, lots):
                    sp.wait_ge(scattered, lots * SLOT)
                    flat = a.rearrange("(p t) c -> p (t c)", t=T)
                    for i, (t0, t1) in enumerate(FILLS):
                        sp.dma_start(edges_d[:, t0 * width:t1 * width], flat[:, t0 * width:t1 * width])\
                            .then_inc(edges_in[i], SLOT)

                def clear_starts():
                    sp.wait_ge(dst_rows_in[J // LS - 1], LS * SLOT)
                    whole = scan[:, :, :].rearrange("p b c -> p (b c)")
                    flat = starts32_dram.rearrange("(p t) c -> p (t c)", t=T)
                    for a in range(0, T * D, 2 * L * C0):
                        sp.dma_start(flat[:, a:a + 2 * L * C0], whole).then_inc(starts32_cleared, SLOT)

                hots_n = Count()

                def run_pass(name, between=None):
                    table, width, scan_dram, C, heads = PASSES[name]
                    grid = scan_dram.rearrange("(p t) c -> p (t c)", t=T)

                    def load_sources(k, b, t0):
                        if hots_n.n and k == 0:
                            sp.wait_ge(source_hots_used, hots_n.at())
                        if k >= 2:
                            sp.wait_ge(source_hots_used, hots_n.at(-BLOCKS))
                        hots_n.up(BLOCKS)
                        n = PE_COLS[name]
                        sp.dma_start(src16[0:NP, b, 0:n * NP], srcT_dram[bass.ds(t0 + L - n, n), :]
                                     .rearrange("t p -> (t p)").partition_broadcast(NP)).then_inc(src16_in[b], SLOT)

                    def step(k, b, t0):
                        if gathered[b].n or k >= 2:
                            sp.wait_ge(rows_in[b], gathered[b].at())
                        sp.dma_start(idx[0:NP, b, :], src_grid[:, bass.ds(t0, L)]).then_inc(idx_in[b], SLOT)
                        gathered[b].up(SLOT * (L - PE_COLS[name]))
                        if k < CH - 1:
                            load_sources(k + 1, 1 - b, t0 + L)
                        if name == "gat" and k == 0:
                            clear_starts()
                        if k >= 2:
                            store(b, t0 - 2 * L)

                    def store(b, t0):
                        sp.wait_ge(rows_turned, scanned.up())
                        sp.dma_start(grid[:, bass.ds(t0 * C, L * C)], scan[:, b, 0:L * C])\
                            .then_inc(scan_stored[b], SLOT)

                    load_sources(0, 0, 0)
                    chunks(sp, [(gathered[0], None), (gathered[1], None), (scanned, 2), (hots_n, 2 * BLOCKS)], step,
                           between)
                    store(1, (CH - 2) * L)
                    store(0, (CH - 1) * L)

                tabf = tab[:, :, :].rearrange("p j c -> p (j c)")
                scatf = scat[:, :, :].rearrange("p j c -> p (j c)")
                sp.wait_ge(srcT_ready, 1)
                TP = T // 5
                sp.dma_start(srcT_dram.rearrange("(i t) p -> t i p", t=TP),
                             src16[0:TP, 0, 0:5 * NP].rearrange("t (i p) -> t i p", i=5)).then_inc(srcT_stored, SLOT)
                store_table(tab0_dram, tabf[0:NP, :])
                sp.wait_ge(srcT_stored, SLOT)
                run_pass("gat", lambda: load_edges(starts4_dram, H, J))
                store_table(tab_cheb_dram[0], tabf[0:NP, 0:J * D])
                run_pass("cheb0")
                store_table(tab_cheb_dram[1], tabf[0:NP, 0:J * D])
                run_pass("cheb1")
                store_table(tab_fsrc_dram, tabf[0:NP, 0:J * D])
                store_table(tab_fdst_dram, scatf[0:NP, :])
                run_pass("gatv2", lambda: load_edges(starts32_dram, D, 2 * J + 3))
                tile_at, n = {}, 6 * len(GROUPS)
                for what, g in SPLINE_ORDER:
                    n += what == "transpose"
                    for j in GROUPS[g] if what == "product" else []:
                        n += 1
                        tile_at[j] = n
                for g in range(J // LS):
                    sp.wait_ge(group_copied, tile_at[(g + 1) * LS - 1])
                    sp.dma_start(tab_y_dram.rearrange("(p j r) c -> p j (r c)", j=J, r=CELLS * CELLS)
                                 [:, g * LS:(g + 1) * LS, :], staged[:, g % 2, :, :])\
                        .then_inc(products_stored[g % 2], SLOT)
                    if g == 0:
                        sp.wait_ge(cells_made, 1)
                        sp.dma_start(cell_grid, cell_i).then_inc(cells_stored, SLOT)
                sp.wait_ge(cells_stored, SLOT)

                def load_indices(turn0, first):
                    for c in range(SLOTS):
                        if not first:
                            sp.wait_ge(slot_in[c], slot_n[c].up(SLOT * LS))
                        sp.dma_start(idx[0:NP, 0, c * LS:(c + 1) * LS], cell_grid[:, bass.ds(turn0 + c * LS, LS)])\
                            .then_inc(slot_idx_in[c], SLOT)

                slot_n = [Count() for c in range(SLOTS)]
                load_indices(0, True)
                with sp.Fori(0, CH - 1) as turn:
                    for c in slot_n:
                        c.enter(turn, SLOT * LS)
                    load_indices(turn * L + L, False)
                store_table(tab_x3_dram, tabf[0:NP, 0:J * HG])
                store_table(tab_xn_dram, scatf[0:NP, :])
                run_pass("agnn", lambda: load_edges(starts32_dram, D, 3 * J + 4))
                for j in range(0, J, LS):
                    sp.wait_ge(vec_for_sync, vec_sync.up())
                    sp.dma_start(nodes(out)[:, j * D:(j + LS) * D], X[:, j:j + LS, :].rearrange("p j c -> p (j c)"))\
                        .then_inc(out_stored, SLOT)
                sp.wait_ge(out_stored, SLOT * (J // LS))
                for b in range(2):
                    sp.wait_ge(scan_stored[b], len(ORDER) * SLOT * ((CH + 1 - b) // 2))
                sp.wait_ge(table_stored, 7 * SLOT)
                sp.wait_ge(scattered, (3 * J + len(ORDER)) * SLOT)

            @block.gpsimd
            def _(pool):
                vec_pool, used = Count(), Count()
                loaded = [Count(), Count()]
                put = Count()
                fences = Count()
                stored = [Count(), Count()]
                tables = Count()

                pool.memset(ones[:, :], 1.0).then_inc(consts_made, 1)
                pool.memset(row_of[:, :], 0).then_inc(consts_made, 1)
                pool.memset(first_i[:, :], 0).then_inc(consts_made, 1)
                pool.memset(end_i[:, :], 0).then_inc(consts_made, 1)
                pool.memset(start_i[:, :], int(SKIP)).then_inc(consts_made, 1)
                pool.memset(mend_get_i[:, :], 0).then_inc(consts_made, 1)
                pool.memset(mend_put_i[:, :], int(SKIP)).then_inc(consts_made, 1)
                pool.memset(idx[:, :, :], 0).then_inc(consts_made, 1)
                pool.iota(node_i[:, :], [[1, J]], base=0, channel_multiplier=J).then_inc(consts_made, 1)
                pool.iota(base_i[:, :], [[1, 1]], base=0, channel_multiplier=T).then_inc(consts_made, 1)
                pool.wait_ge(consts_made, 10)
                for t, op, base, cm, st in [
                    (ident, ALU.is_equal, 0, 1, -1),
                    (before_qp, ALU.is_gt, 0, -1, 1),
                    (before_pq, ALU.is_gt, 0, 1, -1),
                    (shift, ALU.is_equal, 1, 1, -1),
                ]:
                    pool.affine_select(t[:, :], ones[:, :], [[st, P]], op, 0.0, base=base,
                                       channel_multiplier=cm).then_inc(consts_made, 1)

                for i, (t, value) in enumerate((
                                 (w_agg[:, :], 0.0), (w_gatBD[:, :], 0.0), (w_x[:, :], 0.0),
                                 (smallT[D:D + 1, :], 1.0), (scat[:, :, :], 0.0), (mended[:, :], 0.0))):
                    pool.memset(t, value).then_inc(cleared, 1)
                    pool.wait_ge(cleared, i + 1)
                pool.memset(scan[:, :, :], 0.0).then_inc(scan_cleared, 1)

                def gather(o, table, index, s):
                    pool.indirect_dma_start(o, None, table, bass.IndirectOffsetOnAxis(index, 0)).then_inc(s, SLOT)

                def scatter(table, index, rows_, last):
                    pool.indirect_dma_start(table, bass.IndirectOffsetOnAxis(index, 0), rows_, None,
                                            bounds_check=last, oob_is_err=False).then_inc(scattered, SLOT)
                    put.up(SLOT)

                def scatter_starts(a, c):
                    for j in range(J):
                        scatter(a, start_i[:, j:j + 1], scat[:, j, 0:c], E - 1)

                def run_pass(name):
                    table, width, scan_dram, C, heads = PASSES[name]
                    n = ORDER.index(name)

                    def step(k, b, t0):
                        pool.wait_ge(idx_in[b], loaded[b].up(SLOT))
                        if k >= 2:
                            pool.wait_ge(rows_used, used.up())
                        if fences.n:
                            pool.wait_ge(fence_done, fences.at())
                        pool.tensor_tensor(fence[:, b:b + 1], ones[:, 0:1], ones[:, 1:2], ALU.add)\
                            .then_inc(fence_done, 1)
                        fences.up()
                        for t in range(L - PE_COLS[name]):
                            gather(rows[:, b, t * width:(t + 1) * width], table, idx[:, b, t:t + 1], rows_in[b])

                    chunks(pool, [(loaded[0], SLOT), (loaded[1], SLOT), (used, 2), (fences, 2)], step)
                    used.up(2)
                    for b in range(2):
                        pool.wait_ge(scan_stored[b], stored[b].up(SLOT * ((CH + 1 - b) // 2)))
                    gather(local[:, 0:C], scan_dram, mend_get_i[:, 0:1], local_in)
                    pool.wait_ge(vec_for_pool, vec_pool.up())
                    scatter(scan_dram, mend_put_i[:, 0:1], mended[:, 0:C], E - 1)
                    pool.wait_ge(scattered, put.at())
                    for j in range(J):
                        gather(agg[:, j, 0:C], scan_dram, end_i[:, j:j + 1], agg_in[j // LS])

                pool.wait_ge(vec_for_pool, vec_pool.up())
                for j in range(J):
                    gather(edges_d[:, j * T:(j + 1) * T].bitcast(I32), dst_grid, row_of[:, j:j + 1],
                           dst_rows_in[j // LS])
                pool.wait_ge(table_stored, tables.up(SLOT))
                gather(first_row[:, 0:W0], tab0_dram, first_i[:, 0:1], first_in)
                pool.wait_ge(vec_for_pool, vec_pool.up())
                pool.wait_ge(starts4_cleared, SLOT)
                scatter_starts(starts4_dram, H)
                run_pass("gat")
                for name in ("cheb0", "cheb1"):
                    pool.wait_ge(table_stored, tables.up(SLOT))
                    run_pass(name)
                pool.wait_ge(vec_for_sync, 5)
                scatter_starts(starts32_dram, D)
                pool.wait_ge(table_stored, tables.up(2 * SLOT))
                gather(first_row[:, 0:D], tab_fdst_dram, first_i[:, 0:1], first_in)
                run_pass("gatv2")
                pool.iota(nodes16[:, :], [[1, N]], base=-MID, channel_multiplier=0,
                          allow_small_or_imprecise_dtypes=True).then_inc(nodes16_made, 1)
                for b in range(2):
                    pool.wait_ge(products_stored[b], SLOT * ((J // LS + 1 - b) // 2))
                idx_n = [Count() for c in range(SLOTS)]
                slots_used = Count()

                def gather_slot(c):
                    for t in range(LS):
                        gather(slots[:, c, t * CORNERS * D:(t + 1) * CORNERS * D], tab_y_dram,
                               idx[:, 0, c * LS + t:c * LS + t + 1], slot_in[c])

                for c in range(SLOTS):
                    pool.wait_ge(slot_idx_in[c], idx_n[c].up(SLOT))
                    gather_slot(c)
                with pool.Fori(0, CH - 1) as turn:
                    for c in idx_n:
                        c.enter(turn, SLOT)
                    slots_used.enter(turn, SLOTS)
                    fences.enter(turn, SLOTS)
                    for c in range(SLOTS):
                        pool.wait_ge(slot_idx_in[c], idx_n[c].up(SLOT))
                        pool.wait_ge(slot_used, slots_used.up())
                        pool.wait_ge(fence_done, fences.at())
                        pool.tensor_tensor(fence[:, 0:1], ones[:, 0:1], ones[:, 1:2], ALU.add)\
                            .then_inc(fence_done, 1)
                        fences.up()
                        gather_slot(c)
                for c in idx_n:
                    c.leave(CH - 1)
                slots_used.leave(CH - 1)
                fences.leave(CH - 1)
                pool.wait_ge(vec_for_sync, 7)
                scatter_starts(starts32_dram, D)
                pool.wait_ge(table_stored, tables.up(2 * SLOT))
                gather(first_row[:, 0:D], tab_xn_dram, first_i[:, 0:1], first_in)
                run_pass("agnn")

            @block.tensor
            def _(pe):
                operand, group = Count(), Count()

                def in_groups(product, groups=GROUPS):
                    for tiles in groups:
                        n = group.n
                        if n >= 2:
                            pe.wait_ge(group_copied, n - 1)
                        for a, j in enumerate(tiles):
                            ins = product(ps[:, n % 2, :], a, j)
                        ins.then_inc(group_in_psum, 1)
                        group.up()

                def all_copied():
                    pe.wait_ge(group_copied, group.n)

                def tile_T(t, j):
                    return t[:, j * NP:(j + 1) * NP]

                hots_n, filled, act_n = Count(), Count(), Count()

                def gather_rows(name):
                    w = GATHERED[name]
                    hots_, table_ = source_hots(name), table_parts(name)

                    def sum_parts(b, first):
                        if not first:
                            pe.wait_ge(rows_filled, filled.at())
                        pe.wait_ge(parts_copied, filled.up())
                        for i in range(PE_COLS[name]):
                            ins = pe.matmul(ps[0:NP, 6 + b, i * w:(i + 1) * w], three[0:3 * w, i * NP:(i + 1) * NP],
                                            STACKS[w], start=True, stop=True)
                        ins.then_inc(rows_gathered, 1)

                    def step(k, b, t0):
                        if filled.n and k == 0:
                            pe.wait_ge(rows_filled, filled.at())
                        if k >= 2:
                            pe.wait_ge(parts_copied, filled.at())
                        for m in range(BLOCKS):
                            pe.wait_ge(source_hots_ready, hots_n.up())
                            if m == BLOCKS - 1 and ACT_ROWS[name]:
                                pe.wait_ge(source_act_ready, act_n.up(ACT_ROWS[name]))
                            for j in range(m * LS, (m + 1) * LS):
                                for bank, a, n in banks(name, b):
                                    ins = pe.matmul(ps[0:3 * w, bank, 0:n * NP], table_[:, j, :],
                                                    hots_[j][:, a * NP:(a + n) * NP],
                                                    start=(j == 0), stop=(j == J - 1))
                            ins.then_inc(source_hots_used, 1)
                            if m == 0 and k >= 1:
                                sum_parts(1 - b, k == 1)

                    chunks(pe, [(hots_n, 2 * BLOCKS), (filled, 2), (act_n, 2 * ACT_ROWS[name])], step)
                    sum_parts(0, False)

                def mend(name):
                    table, width, scan_dram, C, heads = PASSES[name]
                    gather_rows(name)
                    if heads == 0:
                        pe.wait_ge(rows_turned, (ORDER.index(name) + 1) * CH)
                        pe.matmul(ps[0:NP, 6, 0:C], carry_qp[:, :], scan[0:NP, 0, (L - 1) * C:L * C],
                                  start=True, stop=True).then_inc(pe_for_vec, 1)
                        return
                    pe.wait_ge(vec_for_pe, operand.up())
                    for h in range(heads):
                        ins = pe.matmul(ps[0:NP, 6, h * NP:(h + 1) * NP], ones[0:NP, 0:NP], diag[:, h, :],
                                        start=True, stop=True)
                    ins.then_inc(pe_for_vec, 1)
                    pe.wait_ge(vec_for_pe, operand.up())
                    for h in range(heads):
                        ins = pe.transpose(ps[0:NP, 7, h * NP:(h + 1) * NP], cross[:, h * NP:(h + 1) * NP],
                                           ident[0:NP, 0:NP])
                    ins.then_inc(pe_for_vec, 1)
                    pe.wait_ge(vec_for_pe, operand.up())
                    for h in range(heads):
                        at = (L - 1) * C + h * HG
                        ins = pe.matmul(ps[0:NP, 6, h * HG:(h + 1) * HG], crossT[:, h, :],
                                        scan[0:NP, 0, at:at + HG], start=True, stop=True)
                    ins.then_inc(pe_for_vec, 1)

                def sum_into_sources():
                    hot, act_hot, part = Count(), Count(), Count()

                    def turn_of(begin, end):
                        for c in range(SLOTS):
                            pe.wait_ge(parts_ready, part.up())
                            for t in range(LS):
                                if (c, t) in ACT_HOT:
                                    pe.wait_ge(act_onehot_ready, act_hot.up())
                                else:
                                    pe.wait_ge(onehot_ready, hot.up())
                                for at in range(0, N, BANK):
                                    n = min(BANK, N - at)
                                    ins = pe.matmul(ps[0:3 * D, at // BANK, 0:n], parts[:, c, t, :],
                                                    hots[c % 2][t][:, at:at + n], start=(begin and c == 0 and t == 0),
                                                    stop=(end and c == SLOTS - 1 and t == LS - 1))
                                ins.then_inc(onehot_used, 1)

                    turn_of(True, False)
                    with pe.Fori(0, CH - 2) as turn:
                        part.enter(turn, SLOTS)
                        act_hot.enter(turn, len(ACT_HOT))
                        hot.enter(turn, L - len(ACT_HOT))
                        turn_of(False, False)
                    for n in (part, act_hot, hot):
                        n.leave(CH - 2)
                    turn_of(False, True)

                pe.wait_ge(consts_made, 14)
                pe.wait_ge(vec_for_pe, operand.up())
                pe.matmul(ps[0:NP, 4, 0:NP], ones[0:NP, 0:NP], diag[:, 0, :], start=True, stop=True)
                pe.matmul(ps[0:NP, 4, NP:2 * NP], ones[0:NP, 0:NP], diag[:, 1, :], start=True, stop=True)\
                    .then_inc(pe_for_vec, 1)
                pe.wait_ge(weights_loaded, SLOT * (18 + KU))
                pe.transpose(ps[:, 2, 0:3 * D], w_ih[:, :], ident[0:3 * D, 0:3 * D])
                pe.transpose(ps[:, 2, 3 * D:4 * D], w_gat[:, :], ident[0:D, 0:D])
                pe.transpose(ps[0:D, 3, 0:3 * D], w_hh[:, :], ident[0:3 * D, 0:3 * D]).then_inc(pe_for_vec, 1)
                pe.wait_ge(srcT_made, 1)
                TP = T // 5
                for i in range(5):
                    ins = pe.transpose(ps[0:TP, 6 + i // 4, i % 4 * NP:(i % 4 + 1) * NP],
                                       src_f[:, i * TP:(i + 1) * TP], ident[0:NP, 0:NP])
                ins.then_inc(srcT_turned, 1)
                pe.wait_ge(x_loaded, SLOT)
                in_groups(lambda bank, a, j: pe.transpose(bank[0:D, a * NP:(a + 1) * NP], X[:, j, :],
                                                          ident[0:NP, 0:NP]))
                pe.wait_ge(vec_for_pe, operand.up())
                pe.matmul(ps[:, 5, 0:3 * D], w_gatBD[:, :], w_ihT[:, :], start=True, stop=True)\
                    .then_inc(pe_for_vec, 1)
                pe.wait_ge(vec_for_pe, operand.up())
                all_copied()
                for j in range(J):
                    ins = pe.matmul(ps[0:NP, 3, j * 2 * H:(j + 1) * 2 * H], tile_T(smallT, j)[0:D, :], w_lr[:, :],
                                    start=True, stop=True)
                ins.then_inc(pe_for_vec, 1)
                pe.wait_ge(vec_for_pe, operand.up())
                pe.matmul(ps[0:NP, 4, 2 * NP:2 * NP + 1], shift[0:NP, 0:NP], nodew[:, 0, J - 1:J],
                          start=True, stop=True).then_inc(pe_for_vec, 1)

                mend("gat")
                def transposes(bank, a, j):
                    return pe.transpose(bank[:, a * NP:(a + 1) * NP], aggn[:, j, :], ident[0:NP, 0:NP])

                def gates(bank, a, j):
                    pe.matmul(bank[0:NP, a * P:(a + 1) * P], tile_T(bigT, j), w_agg[:, :], start=True, stop=False)
                    return pe.matmul(bank[0:NP, a * P:(a + 1) * P], tile_T(smallT, j)[0:D + 1, :], w_x[:, :],
                                     start=False, stop=True)

                for tiles in GROUPS:
                    pe.wait_ge(block_ready, tiles[-1] // LS + 1)
                    in_groups(transposes, [tiles])
                    all_copied()
                    in_groups(gates, [tiles])
                mend("cheb0")
                mend("cheb1")
                for tiles in GROUPS:
                    pe.wait_ge(block_ready, J // LS + tiles[-1] // LS + 1)
                    in_groups(lambda bank, a, j: pe.transpose(bank[0:3 * D, a * NP:(a + 1) * NP],
                                                              aggn[:, j, 0:3 * D], ident[0:NP, 0:NP]), [tiles])
                    all_copied()
                    in_groups(lambda bank, a, j: pe.matmul(bank[0:D, a * NP:(a + 1) * NP], w_cheb[:, :],
                                                           bigT[0:3 * D + 1, j * NP:(j + 1) * NP],
                                                           start=True, stop=True), [tiles])
                    all_copied()
                    in_groups(lambda bank, a, j: pe.matmul(bank[0:NP, a * 2 * D:(a + 1) * 2 * D],
                                                           tile_T(smallT, j)[0:D + 1, :], w_sd[:, :],
                                                           start=True, stop=True), [tiles])
                mend("gatv2")
                transposed = {}
                for what, g in SPLINE_ORDER:
                    tiles = GROUPS[g]
                    if what == "transpose":
                        pe.wait_ge(block_ready, 2 * (J // LS) + tiles[-1] // LS + 1)
                        in_groups(lambda bank, a, j: pe.transpose(bank[0:D, a * NP:(a + 1) * NP], X[:, j, :],
                                                                  ident[0:NP, 0:NP]), [tiles])
                        transposed[g] = group.n
                    else:
                        pe.wait_ge(group_copied, transposed[g])
                        in_groups(lambda bank, a, j: pe.matmul(bank[0:NP, :], smallT[0:D, j * NP:(j + 1) * NP],
                                                               w_spl[:, :, :].rearrange("p k f -> p (k f)"),
                                                               start=True, stop=True), [[j] for j in tiles])
                all_copied()
                sum_into_sources()
                pe.wait_ge(vec_for_pe, operand.up())
                in_groups(lambda bank, a, j: pe.matmul(bank[0:NP, a * D:(a + 1) * D],
                                                       bigT[0:3 * D, j:N:J], stack3[:, :], start=True, stop=True))
                mend("agnn")

            @block.scalar
            def _(act):
                group, arg, value = Count(), Count(), Count()

                def copy_groups(place, source, func=ACT.Copy, groups=GROUPS):
                    for tiles in groups:
                        bank = ps[:, group.n % 2, :]
                        act.wait_ge(group_in_psum, group.up())
                        nc.scalar.activation(place(tiles), source(bank, len(tiles)), func)\
                            .then_inc(group_copied, 1)

                def apply(func, t):
                    act.wait_ge(vec_for_act, arg.up())
                    nc.scalar.activation(t, t, func).then_inc(act_for_vec, 1)
                    value.up()

                def columns(tiles):
                    return slice(tiles[0] * NP, (tiles[-1] + 1) * NP)

                scanned, stored = Count(), [Count(), Count()]
                gathered = [Count(), Count()]

                filled, used = Count(), Count()

                def copy_gathered(k, b, name):
                    width, w, n = PASSES[name][1], GATHERED[name], PE_COLS[name]
                    if filled.n or k >= 1:
                        act.wait_ge(rows_gathered, filled.at())
                    act.wait_ge(source_hots_used, hots_n.up(BLOCKS))
                    for bank, a, cols in banks(name, b):
                        ins = nc.scalar.activation(three[0:3 * w, a * NP:(a + cols) * NP],
                                                   ps[0:3 * w, bank, 0:cols * NP], ACT.Copy)
                    ins.then_inc(parts_copied, 1)
                    if filled.n and k == 0:
                        act.wait_ge(rows_used, filled.at())
                    if k >= 2:
                        act.wait_ge(rows_used, filled.at(-1))
                    act.wait_ge(rows_gathered, filled.up())
                    nc.scalar.activation(
                        rows[0:NP, b, (L - n) * width:L * width].rearrange("p (t c) -> p t c", c=width)[:, :, 0:w],
                        ps[0:NP, 6 + b, 0:n * w].rearrange("p (t c) -> p t c", c=w), ACT.Copy)\
                        .then_inc(rows_filled, 1)

                hots_n = Count()

                act_n, chunks_n, src16_n = Count(), Count(), [Count(), Count()]

                def make_last_hots(k, b, name):
                    if k >= CH:
                        return
                    src16_n[b].up(SLOT)
                    n = PE_COLS[name] * NP
                    if chunks_n.n:
                        act.wait_ge(source_hots_used, chunks_n.at())
                    chunks_n.up(BLOCKS)
                    if not ACT_ROWS[name]:
                        return
                    half = tab[0:NP, :, :].rearrange("p j c -> p (j c)").bitcast(BF16)[:, 0:n]
                    act.wait_ge(src16_in[b], src16_n[b].at())
                    for j in range(J - ACT_ROWS[name], J):
                        if act_n.n:
                            act.wait_ge(source_act_ready, act_n.at())
                        nc.scalar.activation(half, src16[0:NP, b, 0:n], ACT.Square, bias=node_c_neg[:, j:j + 1])\
                            .then_inc(source_half_ready, 1)
                        act.wait_ge(source_half_ready, act_n.up())
                        nc.scalar.activation(source_hots(name)[j], half, ACT.Relu, bias=1.0, scale=-1.0)\
                            .then_inc(source_act_ready, 1)

                def begin_pass(name, tables):
                    if ACT_ROWS[name]:
                        act.wait_ge(table_stored, tables * SLOT)
                        act.wait_ge(source_hots_ready, chunks_n.at(1))
                    make_last_hots(0, 0, name)
                    copy_gathered(0, 0, name)
                    make_last_hots(1, 1, name)

                def copy_next(k, b, name):
                    if k < CH - 1:
                        copy_gathered(k + 1, 1 - b, name)

                def turn_rows(k, b, C, z):
                    act.wait_ge(chunk_scanned, scanned.up())
                    if stored[b].n or k >= 2:
                        act.wait_ge(scan_stored[b], stored[b].at())
                    stored[b].up(SLOT)
                    rows_ = scan[0:NP, b, 0:L * C].rearrange("p (t c) -> p t c", c=C)
                    n = z.shape[1]
                    return rows_[:, :, 0:n], z.rearrange("p c t -> p t c"), rows_[:, :, n:C]

                def softmax_pass(name, tables):
                    table, width, scan_dram, C, heads = PASSES[name]
                    z, keep, n = scan_views(name)

                    def step(k, b, t0):
                        gathered[b].up(SLOT * (L - PE_COLS[name]))
                        apply(ACT.Exp, rw[:, b, :, 0:heads, :])
                        act.wait_ge(act_for_vec, value.at())
                        nc.scalar.activation(
                            keep.rearrange("p (h g) t -> p h g t", g=HG)[:, :, :, 1:L],
                            rw[:, b, 0, 0:heads, 1:L].unsqueeze(2).broadcast_to([NP, heads, HG, L - 1]),
                            ACT.Copy).then_inc(keep_ready, 1)
                        copy_next(k, b, name)
                        to, of, maxima = turn_rows(k, b, C, z[b])
                        nc.scalar.activation(maxima, mrun[:, b, 0:heads, 1:L + 1].rearrange("p h t -> p t h"),
                                             ACT.Copy)
                        nc.scalar.activation(to, of, ACT.Copy).then_inc(rows_turned, 1)
                        make_last_hots(k + 2, b, name)

                    begin_pass(name, tables)
                    chunks(act, [(arg, 2), (value, 2), (scanned, 2), (stored[0], SLOT), (stored[1], SLOT),
                                 (gathered[0], None), (gathered[1], None), (filled, 2),
                                 (hots_n, 2 * BLOCKS), (act_n, 2 * ACT_ROWS[name]), (chunks_n, 2 * BLOCKS),
                                 (src16_n[0], SLOT), (src16_n[1], SLOT)], step)
                    apply(ACT.Exp, cross[:, 0:heads * NP + heads])

                def sum_pass(name, tables):
                    z, keep, n = scan_views(name)

                    def step(k, b, t0):
                        act.wait_ge(rows_in[b], gathered[b].up(SLOT * (L - PE_COLS[name])))
                        act.wait_ge(rows_filled, filled.at())
                        nc.scalar.activation(z[b], rows[0:NP, b, 0:L * D].rearrange("p (t c) -> p c t", c=D),
                                             ACT.Copy).then_inc(rows_used, 1)
                        act.wait_ge(vec_for_act, arg.up())
                        nc.scalar.activation(keep[:, :, 1:L],
                                             samec[:, b, 1:L].unsqueeze(1).broadcast_to([NP, D, L - 1]),
                                             ACT.Copy).then_inc(act_for_vec, 1)
                        value.up()
                        copy_next(k, b, name)
                        to, of, _ = turn_rows(k, b, D, z[b])
                        nc.scalar.activation(to, of, ACT.Copy).then_inc(rows_turned, 1)
                        make_last_hots(k + 2, b, name)

                    begin_pass(name, tables)
                    chunks(act, [(arg, 2), (value, 2), (scanned, 2), (stored[0], SLOT), (stored[1], SLOT),
                                 (gathered[0], None), (gathered[1], None), (filled, 2),
                                 (hots_n, 2 * BLOCKS), (act_n, 2 * ACT_ROWS[name]), (chunks_n, 2 * BLOCKS),
                                 (src16_n[0], SLOT), (src16_n[1], SLOT)], step)

                def layer_norm():
                    apply(ACT.Sqrt, nodew[:, 7, :])

                copy_groups(lambda tiles: smallT[0:D, columns(tiles)], lambda bank, n: bank[0:D, 0:n * NP])
                apply(ACT.Sqrt, nodew[:, 4, :])
                act.wait_ge(starts32_cleared, SLOT * (T * D // (2 * L * C0)))
                softmax_pass("gat", 1)
                for group_ in GROUPS:
                    copy_groups(lambda tiles: bigT[:, columns(tiles)], lambda bank, n: bank[:, 0:n * NP],
                                groups=[group_])
                    copy_groups(lambda tiles: aggn[:, tiles[0]:tiles[-1] + 1, :].rearrange("p j c -> p (j c)"),
                                lambda bank, n: bank[0:NP, 0:n * P], groups=[group_])
                act.wait_ge(group_copied, group.n)
                nc.scalar.activation(aggn[:, :, 0:2 * D], aggn[:, :, 0:2 * D], ACT.Sigmoid).then_inc(act_for_vec, 1)
                value.up()
                apply(ACT.Tanh, work[:, :, :])
                apply(ACT.Exp, work2[:, :, :])
                layer_norm()
                sum_pass("cheb0", 2)
                sum_pass("cheb1", 3)
                for group_ in GROUPS:
                    copy_groups(lambda tiles: bigT[0:3 * D, columns(tiles)], lambda bank, n: bank[0:3 * D, 0:n * NP],
                                groups=[group_])
                    copy_groups(lambda tiles: smallT[0:D, columns(tiles)], lambda bank, n: bank[0:D, 0:n * NP],
                                ACT.Relu, [group_])
                    copy_groups(lambda tiles: aggn[:, tiles[0]:tiles[-1] + 1, 0:2 * D],
                                lambda bank, n: bank[0:NP, 0:n * 2 * D].rearrange("p (j c) -> p j c", j=n),
                                groups=[group_])
                softmax_pass("gatv2", 5)

                blocks_n = 0
                for what, g in SPLINE_ORDER:
                    tiles = GROUPS[g]
                    if what == "transpose":
                        while blocks_n < min(tiles[-1] // LS + 2, J // LS):
                            apply(ACT.Sqrt, nodew[:, 7, blocks_n * LS:(blocks_n + 1) * LS])
                            blocks_n += 1
                        copy_groups(lambda tiles: smallT[0:D, columns(tiles)], lambda bank, n: bank[0:D, 0:n * NP],
                                    groups=[tiles])
                        continue
                    for j in tiles:
                        lot = j // LS
                        if lot >= 2 and j % LS == 0:
                            act.wait_ge(products_stored[lot % 2], SLOT * (lot // 2))
                        made_ = ps[0:NP, group.n % 2, :].rearrange("p (u v c) -> p v u c", u=KU, v=KV)
                        to = staged[:, lot % 2, j % LS, :].rearrange("p (v u a b c) -> p v u a b c", v=CELLS, u=CELLS,
                                                                   a=2, b=2)
                        act.wait_ge(group_in_psum, group.up())
                        for a in range(2):
                            for b in range(2):
                                ins = nc.scalar.activation(to[:, :, :, a, b, :], made_[:, b:b + CELLS, a:a + CELLS, :],
                                                           ACT.Copy)
                        ins.then_inc(group_copied, 1)
                sources, half, hot_used = Count(), Count(), Count(-L)

                def one_hots(first):
                    act.wait_ge(sources_ready, sources.up())
                    if first:
                        act.wait_ge(nodes16_made, 1)
                        for b in range(2):
                            act.wait_ge(products_stored[b], SLOT * ((J // LS + 1 - b) // 2))
                    for c in range(SLOTS):
                        for t in range(LS):
                            hot_used.up()
                            if (c, t) not in ACT_HOT:
                                continue
                            if half.n:
                                act.wait_ge(act_onehot_ready, half.at())
                            nc.scalar.activation(half_hot, nodes16[:, :], ACT.Square,
                                                 bias=srcc_neg[:, c, t:t + 1]).then_inc(half_hot_ready, 1)
                            half.up()
                            act.wait_ge(half_hot_ready, half.at())
                            if not first or c >= HOT_LAG[c]:
                                act.wait_ge(onehot_used, hot_used.at(L - HOT_LAG[c] * LS))
                            nc.scalar.activation(hots[c % 2][t], half_hot, ACT.Relu, bias=1.0, scale=-1.0)\
                                .then_inc(act_onehot_ready, 1)

                one_hots(True)
                with act.Fori(0, CH - 1) as turn:
                    for c, per in ((sources, 1), (half, len(ACT_HOT)), (hot_used, L)):
                        c.enter(turn, per)
                    one_hots(False)
                copy_groups(lambda tiles: work2[:, tiles[0]:tiles[-1] + 1, :],
                            lambda bank, n: bank[0:NP, 0:n * D].rearrange("p (j c) -> p j c", j=n))
                layer_norm()
                apply(ACT.Sqrt, nodew[:, 7, :])
                softmax_pass("agnn", 7)
                for j in range(0, J, LS):
                    apply(ACT.Exp, nodew[:, 0:2, j:j + LS])
                    apply(ACT.Sqrt, nodew[:, 7, j:j + LS])

            @block.vector
            def _(vec):
                own = Count()
                pe_n, group_n, act_n = Count(), Count(), Count()
                gathered = [Count(), Count()]
                scanned = Count()
                edges_n, first_n, local_n, agg_n = Count(), Count(), Count(), Count()
                CUM, PREV, DEG, SOME, DINV, DSOME, MEAN, RSTD, RN, ROW, CNT, TMP, SELF = range(13)

                ALL = slice(0, J)
                BLOCK_OF = [slice(m * LS, (m + 1) * LS) for m in range(J // LS)]

                def per_node(slot, js=ALL):
                    return nodew[:, slot, js]

                def over(a, n):
                    return a.unsqueeze(len(a.shape)).broadcast_to(list(a.shape) + [n])

                hots_n, filled = Count(), Count()
                src16_n = [Count(), Count()]

                making = {"row": J, "last": J}

                def start_hots(k, b, name):
                    making.update(row=0 if k < CH else J, b=b, hots=source_hots(name), n=PE_COLS[name] * NP,
                                  last=J - ACT_ROWS[name])
                    if k < CH:
                        vec.wait_ge(src16_in[b], src16_n[b].up(SLOT))

                def more_hots(count=1):
                    for j in range(making["row"], min(making["row"] + count, making["last"])):
                        if j % LS == 0 and not making.get("first"):
                            vec.wait_ge(source_hots_used, hots_n.at(1 - BLOCKS))
                        ins = vec.tensor_scalar(making["hots"][j], src16[0:NP, making["b"], 0:making["n"]],
                                                node_c[:, j:j + 1], None, ALU.is_equal)
                        if j % LS == LS - 1 or j == making["last"] - 1:
                            ins.then_inc(source_hots_ready, 1)
                            hots_n.up()
                        making["row"] = j + 1

                def settle():
                    more_hots()
                    vec.wait_ge(vec_done, own.up())

                vec.memset(same[:, 0:1], 0.0).then_inc(vec_done, 1)
                settle()

                vec.wait_ge(graph_loaded, SLOT)
                vec.wait_ge(consts_made, 14)
                vec.tensor_copy(ends[:, 0:1], dst_i[:, 0:1])
                vec.tensor_copy(first_i[0:NP, :], dst_i[:, 0:1])
                vec.tensor_copy(node_f[:, :], node_i[0:NP, :])
                vec.tensor_copy(base_f[:, :], base_i[0:NP, :])
                vec.tensor_copy(ends[:, 1:2], dst_i[:, T - 1:T]).then_inc(vec_done, 1)
                settle()
                for i in range(2):
                    ins = vec.tensor_scalar(diag[:, i, :], ident[0:NP, 0:NP], ends[:, i:i + 1], None, ALU.mult)
                ins.then_inc(vec_for_pe, 1)
                vec.tensor_tensor(same[:, 1:T], dst_i[:, 1:T], dst_i[:, 0:T - 1], ALU.is_equal)

                vec.wait_ge(pe_for_vec, pe_n.up())
                firsts, lasts = ps[0:NP, 4, 0:NP], ps[0:NP, 4, NP:2 * NP]
                vec.scalar_tensor_tensor(carry_qp[:, :], firsts, ends[:, 1:2], before_qp[0:NP, 0:NP],
                                         ALU.is_equal, ALU.mult)
                vec.scalar_tensor_tensor(carry_pq[:, :], lasts, ends[:, 0:1], before_pq[0:NP, 0:NP],
                                         ALU.is_equal, ALU.mult)
                upto = edges_d[0:NP, 0:J * NP].rearrange("p (j q) -> p j q", j=J)
                vec.tensor_tensor(upto, over(node_f[:, :], NP), firsts.unsqueeze(1).broadcast_to([NP, J, NP]),
                                  ALU.is_ge).then_inc(vec_done, 1)
                settle()
                vec.tensor_scalar(no_carry_pq[:, :], carry_pq[:, :], -1.0, BIG, ALU.add, ALU.mult)
                vec.tensor_reduce(per_node(CNT), upto, X_AXIS, ALU.add).then_inc(vec_done, 1)
                settle()
                vec.tensor_scalar(per_node(ROW), per_node(CNT), -1.0, 0.0, ALU.add, ALU.max).then_inc(vec_done, 1)
                settle()
                vec.tensor_copy(row_of[0:NP, :], per_node(ROW)).then_inc(vec_for_pool, 1)

                vec.wait_ge(weights_loaded, SLOT * (18 + KU))
                vec.wait_ge(cleared, 6)
                vec.tensor_scalar(src_f[:, :], src_f[:, :].bitcast(I32), -float(MID), None, ALU.add)\
                    .then_inc(srcT_made, 1)
                vec.tensor_scalar(node_c[:, :], node_f[:, :], -float(MID), None, ALU.add)
                vec.tensor_scalar(node_c_neg[:, :], node_f[:, :], -1.0, float(MID), ALU.mult, ALU.add)
                for w in STACKS:
                    vec.tensor_tensor(STACKS[w], ident[0:3 * w, 0:w], ident[0:3 * w, w:2 * w], ALU.add)\
                        .then_inc(vec_done, 1)
                    settle()
                    vec.tensor_tensor(STACKS[w], STACKS[w], ident[0:3 * w, 2 * w:3 * w], ALU.add)
                for i in range(3):
                    vec.tensor_copy(stack3[i * D:(i + 1) * D, :], ident[i * D:(i + 1) * D, i * D:(i + 1) * D])
                vec.wait_ge(pe_for_vec, pe_n.up())
                vec.tensor_copy(w_ihT[:, :], ps[:, 2, 0:3 * D])
                for h in range(H):
                    ins = vec.tensor_copy(w_gatBD[h * D:(h + 1) * D, h * D:(h + 1) * D],
                                          ps[h * D:(h + 1) * D, 2, 3 * D:4 * D])
                ins.then_inc(vec_for_pe, 1)
                vec.tensor_tensor(att_lr[:, :, :], att_lr[:, :, :],
                                  w_gat[:, :].unsqueeze(1).broadcast_to([D, 2, P]), ALU.mult).then_inc(vec_done, 1)
                settle()
                vec.tensor_reduce(w_lr[:, :], att_lr[:, :, :].rearrange("p s (h f) -> p (s h) f", h=H), X_AXIS, ALU.add)
                vec.tensor_copy(w_x[0:D, 0:2 * D], ps[0:D, 3, 0:2 * D])
                vec.tensor_copy(w_x[0:D, 3 * D:4 * D], ps[0:D, 3, 2 * D:3 * D])
                vec.tensor_tensor(w_x[D:D + 1, 0:2 * D], b_row[D:D + 1, 0:2 * D], b_row[D:D + 1, 3 * D:5 * D], ALU.add)
                vec.tensor_copy(w_x[D:D + 1, 2 * D:3 * D], b_row[D:D + 1, 2 * D:3 * D])
                vec.tensor_copy(w_x[D:D + 1, 3 * D:4 * D], b_row[D:D + 1, 5 * D:6 * D]).then_inc(vec_for_pe, 1)
                vec.reciprocal(scal[:, 7:8], scal[:, 0:1]).then_inc(vec_done, 1)
                settle()
                vec.tensor_scalar(scal[:, 2:3], scal[:, 7:8], 2.0, None, ALU.mult)
                vec.tensor_scalar(scal[:, 3:4], scal[:, 7:8], -2.0, None, ALU.mult)
                vec.tensor_scalar(scal[:, 4:5], scal[:, 7:8], 2.0, -1.0, ALU.mult, ALU.add)
                vec.tensor_scalar(scal[:, 5:6], scal[:, 7:8], -4.0, None, ALU.mult)
                vec.tensor_scalar(scal[:, 6:7], scal[:, 7:8], 4.0, -2.0, ALU.mult, ALU.add)

                vec.wait_ge(pe_for_vec, pe_n.up())
                vec.tensor_copy(w_agg[:, 0:3 * D], ps[:, 5, 0:3 * D])

                TP = T // 5
                vec.wait_ge(srcT_turned, 1)
                vec.tensor_copy(src16[0:TP, 0, 0:4 * NP], ps[0:TP, 6, 0:4 * NP])
                vec.tensor_copy(src16[0:TP, 0, 4 * NP:5 * NP], ps[0:TP, 7, 0:NP]).then_inc(srcT_ready, 1)

                vec.wait_ge(x_loaded, SLOT)
                vec.wait_ge(pe_for_vec, pe_n.up())
                lr = ps[0:NP, 3, 0:J * 2 * H].rearrange("p (j c) -> p j c", j=J)
                vec.tensor_copy(tab[0:NP, :, 0:D], X[:, :, :])
                vec.tensor_copy(scat[0:NP, :, 0:H], lr[:, :, H:2 * H])
                vec.tensor_copy(tab[0:NP, :, D:W0], lr).then_inc(vec_for_sync, 1)

                flat = work[:, :, :].rearrange("p j c -> p (j c)")[:, 0:T]
                vec.tensor_scalar(flat, dst_i[:, :], ends[:, 0:1], None, ALU.is_equal).then_inc(vec_done, 1)
                settle()
                vec.tensor_reduce(ends[:, 2:3], flat, X_AXIS, ALU.add).then_inc(vec_done, 1)
                settle()
                vec.scalar_tensor_tensor(ends[:, 3:4], ends[:, 2:3], -1.0, base_f[:, :], ALU.add, ALU.add)\
                    .then_inc(vec_done, 1)
                settle()
                vec.tensor_copy(mend_get_i[0:NP, :], ends[:, 3:4])
                vec.tensor_copy(mend_put_i[0:NP, :], ends[:, 3:4])

                for j in range(J):
                    if j % LS == 0:
                        vec.wait_ge(dst_rows_in[j // LS], LS * SLOT)
                    there = edges_d[0:NP, j * T:(j + 1) * T]
                    ins = vec.tensor_scalar(there, there.bitcast(I32), node_f[:, j:j + 1], 0.0, ALU.is_le, ALU.add,
                                            accum_out=nodew[:, CNT, j:j + 1])
                ins.then_inc(vec_done, 1)
                settle()
                vec.scalar_tensor_tensor(per_node(CUM), per_node(ROW), float(T), per_node(CNT), ALU.mult, ALU.add)\
                    .then_inc(vec_for_pe, 1)
                vec.wait_ge(vec_for_pe, 4)
                vec.tensor_copy(nodew[:, PREV, 1:J], nodew[:, CUM, 0:J - 1])
                vec.wait_ge(pe_for_vec, pe_n.up())
                vec.tensor_copy(nodew[:, PREV, 0:1], ps[0:NP, 4, 2 * NP:2 * NP + 1]).then_inc(vec_done, 1)
                settle()
                vec.tensor_tensor(per_node(DEG), per_node(CUM), per_node(PREV), ALU.subtract).then_inc(vec_done, 1)
                settle()
                vec.tensor_scalar(per_node(CNT), per_node(CUM), -1.0, 0.0, ALU.add, ALU.max)
                vec.tensor_scalar(per_node(SOME), per_node(DEG), 1.0, None, ALU.min)
                vec.tensor_scalar(per_node(DINV), per_node(DEG), 1.0, None, ALU.max).then_inc(vec_for_act, 1)
                vec.wait_ge(vec_for_act, 1)
                vec.tensor_scalar(per_node(TMP), per_node(SOME), -SKIP, SKIP, ALU.mult, ALU.add).then_inc(vec_done, 1)
                settle()
                vec.tensor_tensor(per_node(TMP), per_node(TMP), per_node(PREV), ALU.add).then_inc(vec_done, 1)
                settle()
                vec.tensor_copy(end_i[0:NP, :], per_node(CNT))
                vec.tensor_copy(start_i[0:NP, :], per_node(TMP)).then_inc(vec_for_pool, 1)
                vec.wait_ge(act_for_vec, act_n.up())
                vec.reciprocal(per_node(DINV), per_node(DINV)).then_inc(vec_done, 1)
                settle()
                vec.tensor_tensor(per_node(DSOME), per_node(DINV), per_node(SOME), ALU.mult)

                def fill_edges(width, at):
                    ed = edges_d[0:NP, 0:T * width].rearrange("p (t c) -> p t c", c=width)
                    vec.wait_ge(first_in, first_n.up(SLOT))
                    edges_n.up(SLOT)
                    for i, (t0, t1) in enumerate(FILLS):
                        vec.wait_ge(edges_in[i], edges_n.at())
                        if i == 0:
                            vec.tensor_copy(ed[:, 0, :], first_row[0:NP, at:at + width]).then_inc(vec_done, 1)
                            settle()
                        for c in range(width):
                            ins = vec.tensor_tensor_scan(ed[:, t0:t1, c], same[:, t0:t1], ed[:, t0:t1, c],
                                                         ed[:, t0 - 1, c:c + 1] if i else 0.0, ALU.mult, ALU.add)
                        ins.then_inc(vec_done, 1)
                        settle()

                def begin_pass(name, table_, stores):
                    w = GATHERED[name]
                    rest = bigT[0:NP, 0:J * w] if name == "gat" else scan[0:NP, 1, 0:J * w]
                    rest = rest.rearrange("p (j c) -> p j c", j=J)
                    high, mid, low = (table_parts(name)[:, :, i * w:(i + 1) * w] for i in range(3))
                    vec.wait_ge(vec_for_sync, stores)
                    vec.tensor_copy(high, table_).then_inc(vec_done, 1)
                    settle()
                    vec.tensor_tensor(rest, table_, high, ALU.subtract).then_inc(vec_done, 1)
                    settle()
                    vec.tensor_copy(mid, rest).then_inc(vec_done, 1)
                    settle()
                    vec.tensor_tensor(rest, rest, mid, ALU.subtract).then_inc(vec_done, 1)
                    settle()
                    vec.tensor_copy(low, rest).then_inc(vec_done, 1)
                    settle()
                    for k in range(2):
                        making["first"] = name == "gat" and k == 0
                        start_hots(k, k, name)
                        more_hots(J)

                HOT_COUNTS = [(hots_n, 2 * BLOCKS), (filled, 2), (src16_n[0], SLOT), (src16_n[1], SLOT)]

                def start_scans(name):
                    z, keep, n = scan_views(name)
                    vec.memset(z[1][:, :, L - 1:L], 0.0)
                    vec.memset(keep[:, :, 0:1], 0.0)
                    vec.memset(mrun[:, 1, :, L:L + 1], -BIG).then_inc(vec_done, 1)
                    settle()

                def scan_chunk(z, keep, b):
                    flat = z[b].rearrange("p c t -> p (c t)")
                    vec.tensor_tensor_scan(flat, keep.rearrange("p c t -> p (c t)"), flat, 0.0,
                                           ALU.mult, ALU.add).then_inc(chunk_scanned, 1)
                    scanned.up()

                def softmax_pass(name, logits):
                    table, width, scan_dram, C, heads = PASSES[name]
                    z, keep, n = scan_views(name)
                    start_scans(name)

                    def step(k, b, t0):
                        r = rows[0:NP, b, 0:L * width].rearrange("p (t w) -> p t w", w=width)
                        vec.wait_ge(rows_in[b], gathered[b].up(SLOT * (L - PE_COLS[name])))
                        vec.wait_ge(rows_filled, filled.up())
                        start_hots(k + 2, b, name)
                        vec.tensor_scalar(brk[:, :], same[:, bass.ds(t0, L)], -1.0, BIG, ALU.add, ALU.mult)
                        logits(r, t0)
                        vec.tensor_copy(mrun[:, b, 0:heads, 0:1], mrun[:, 1 - b, 0:heads, L:L + 1])
                        for h in range(heads):
                            ins = vec.tensor_tensor_scan(mrun[:, b, h, 1:L + 1], brk[:, :], logit[:, h, :],
                                                         mrun[:, 1 - b, h, L:L + 1], ALU.add, ALU.max)
                        ins.then_inc(vec_done, 1)
                        settle()
                        m_now, m_before = mrun[:, b, 0:heads, 1:L + 1], mrun[:, b, 0:heads, 0:L]
                        vec.tensor_tensor(rw[:, b, 1, 0:heads, :], logit[:, 0:heads, :], m_now, ALU.subtract)
                        vec.tensor_tensor(rw[:, b, 0, 0:heads, :], m_before, m_now, ALU.subtract).then_inc(vec_done, 1)
                        settle()
                        vec.tensor_tensor(rw[:, b, 0, 0:heads, :], rw[:, b, 0, 0:heads, :],
                                          brk[:, :].unsqueeze(1).broadcast_to([NP, heads, L]), ALU.add)\
                            .then_inc(vec_for_act, 1)
                        zh = z[b].rearrange("p (h g) t -> p h g t", g=HG)
                        more_hots(LS)
                        vec.wait_ge(act_for_vec, act_n.up())
                        w = rw[:, b, 1, 0:heads, :]
                        vec.tensor_tensor(zh[:, :, 0:D, :], w.unsqueeze(2).broadcast_to([NP, heads, D, L]),
                                          r[:, :, 0:D].rearrange("p t f -> p f t").unsqueeze(1)
                                          .broadcast_to([NP, heads, D, L]), ALU.mult).then_inc(rows_used, 1)
                        vec.tensor_copy(zh[:, :, D, :], w).then_inc(vec_done, 1)
                        settle()
                        used.up()
                        if scanned.n:
                            vec.wait_ge(chunk_scanned, scanned.at())
                        for h in range(heads):
                            one_head = slice(h * HG, (h + 1) * HG)
                            ins = vec.scalar_tensor_tensor(z[b][:, one_head, 0], z[1 - b][:, one_head, L - 1],
                                                           rw[:, b, 0, h, 0:1], z[b][:, one_head, 0],
                                                           ALU.mult, ALU.add)
                        ins.then_inc(vec_done, 1)
                        settle()
                        vec.wait_ge(keep_ready, kept.up())
                        scan_chunk(z, keep, b)
                        more_hots(J)

                    chunks(vec, [(gathered[0], None), (gathered[1], None), (own, None), (act_n, 2),
                                 (kept, 2), (used, 2), (scanned, 2)] + HOT_COUNTS, step)

                    for h in range(heads):
                        ins = vec.tensor_scalar(diag[:, h, :], ident[0:NP, 0:NP], mrun[:, 0, h, L:L + 1], None,
                                                ALU.mult)
                    ins.then_inc(vec_for_pe, 1)
                    cr = cross[:, 0:heads * NP].rearrange("p (h q) -> p h q", h=heads)
                    ps6 = ps[0:NP, 6, 0:heads * NP].rearrange("p (h q) -> p h q", h=heads)
                    vec.wait_ge(pe_for_vec, pe_n.up())
                    vec.tensor_tensor(cr, ps6, carry_pq[:, :].unsqueeze(1).broadcast_to([NP, heads, NP]), ALU.mult)\
                        .then_inc(vec_done, 1)
                    settle()
                    vec.tensor_tensor(cr, cr, no_carry_pq[:, :].unsqueeze(1).broadcast_to([NP, heads, NP]), ALU.add)\
                        .then_inc(vec_done, 1)
                    settle()
                    vec.tensor_reduce(small[:, 0, 0:heads], cr, X_AXIS, ALU.max).then_inc(vec_done, 1)
                    settle()
                    m_local = local[0:NP, heads * HG:C]
                    vec.wait_ge(local_in, local_n.up(SLOT))
                    vec.tensor_tensor(small[:, 1, 0:heads], small[:, 0, 0:heads], m_local, ALU.max)\
                        .then_inc(vec_done, 1)
                    settle()
                    vec.tensor_tensor(cross[:, heads * NP:heads * NP + heads], m_local, small[:, 1, 0:heads],
                                      ALU.subtract)
                    vec.tensor_tensor(cr, cr, over(small[:, 1, 0:heads], NP), ALU.subtract).then_inc(vec_for_act, 1)
                    vec.wait_ge(act_for_vec, act_n.up())
                    vec.tensor_copy(mended[0:NP, heads * HG:C], small[:, 1, 0:heads])
                    me = mended[0:NP, 0:heads * HG].rearrange("p (h g) -> p h g", g=HG)
                    vec.tensor_tensor(me, local[0:NP, 0:heads * HG].rearrange("p (h g) -> p h g", g=HG),
                                      over(cross[:, heads * NP:heads * NP + heads], HG), ALU.mult)\
                        .then_inc(vec_for_pe, 1)
                    vec.wait_ge(pe_for_vec, pe_n.up())
                    vec.tensor_copy(crossT[:, 0:heads, :],
                                    ps[0:NP, 7, 0:heads * NP].rearrange("p (h q) -> p h q", h=heads))\
                        .then_inc(vec_for_pe, 1)
                    vec.wait_ge(pe_for_vec, pe_n.up())
                    vec.tensor_tensor(mended[0:NP, 0:heads * HG], mended[0:NP, 0:heads * HG],
                                      ps[0:NP, 6, 0:heads * HG], ALU.add).then_inc(vec_for_pool, 1)
                    agg_n.up(LS * SLOT)

                def block_in(m):
                    vec.wait_ge(agg_in[m], agg_n.at())

                def finish_sums():
                    vec.wait_ge(pe_for_vec, pe_n.up())
                    vec.wait_ge(local_in, local_n.up(SLOT))
                    vec.tensor_tensor(mended[0:NP, 0:D], local[0:NP, 0:D], ps[0:NP, 6, 0:D], ALU.add)\
                        .then_inc(vec_for_pool, 1)
                    agg_n.up(LS * SLOT)

                def sum_pass(name):
                    z, keep, n = scan_views(name)
                    start_scans(name)

                    def step(k, b, t0):
                        vec.tensor_scalar(samec[:, b, :], same[:, bass.ds(t0, L)], 1.0, None, ALU.mult)\
                            .then_inc(vec_for_act, 1)
                        gathered[b].up(SLOT * (L - PE_COLS[name]))
                        filled.up()
                        start_hots(k + 2, b, name)
                        more_hots(2 * LS)
                        vec.wait_ge(act_for_vec, act_n.up())
                        vec.wait_ge(chunk_scanned, scanned.at())
                        vec.scalar_tensor_tensor(z[b][:, :, 0], z[1 - b][:, :, L - 1], samec[:, b, 0:1],
                                                 z[b][:, :, 0], ALU.mult, ALU.add).then_inc(vec_done, 1)
                        settle()
                        scan_chunk(z, keep, b)
                        more_hots(J)

                    chunks(vec, [(gathered[0], None), (gathered[1], None), (own, None), (act_n, 2),
                                 (scanned, 2)] + HOT_COUNTS, step)
                    used.up(CH)
                    finish_sums()

                def divide(heads, js):
                    a = agg[0:NP, js, 0:heads * HG].rearrange("p j (h g) -> p j h g", g=HG)
                    rd = rden[:, js, 0:heads]
                    vec.tensor_scalar(rd, a[:, :, :, D], TINY, None, ALU.max).then_inc(vec_done, 1)
                    settle()
                    vec.reciprocal(rd, rd).then_inc(vec_done, 1)
                    settle()
                    vec.tensor_tensor(rd, rd, over(per_node(SOME, js), heads), ALU.mult).then_inc(vec_done, 1)
                    settle()
                    return a[:, :, :, 0:D], over(rd, D)

                def layer_norm(ready=vec_done, js=ALL):
                    x_, squares = X[:, js, :], work[:, js, :]
                    mean, rstd = per_node(MEAN, js), per_node(RSTD, js)
                    vec.tensor_reduce(mean, x_, X_AXIS, ALU.add).then_inc(vec_done, 1)
                    settle()
                    vec.tensor_scalar(mean, mean, 1.0 / D, None, ALU.mult).then_inc(vec_done, 1)
                    settle()
                    vec.tensor_tensor(x_, x_, over(mean, D), ALU.subtract).then_inc(vec_done, 1)
                    settle()
                    vec.tensor_tensor(squares, x_, x_, ALU.mult).then_inc(vec_done, 1)
                    settle()
                    vec.tensor_reduce(rstd, squares, X_AXIS, ALU.add).then_inc(vec_done, 1)
                    settle()
                    vec.tensor_scalar(rstd, rstd, 1.0 / D, LN_EPS, ALU.mult, ALU.add).then_inc(vec_for_act, 1)
                    vec.wait_ge(act_for_vec, act_n.up())
                    vec.reciprocal(rstd, rstd).then_inc(vec_done, 1)
                    settle()
                    vec.tensor_tensor(x_, x_, over(rstd, D), ALU.mult).then_inc(ready, 1)
                    if ready is vec_done:
                        settle()

                used, kept = Count(), Count()
                tabD = tab[:, :, :].rearrange("p j c -> p (j c)")[0:NP, 0:J * D].rearrange("p (j c) -> p j c", c=D)
                tabG = tab[:, :, :].rearrange("p j c -> p (j c)")[0:NP, 0:J * HG].rearrange("p (j c) -> p j c", c=HG)

                begin_pass("gat", tab[0:NP, :, 0:D + H], 1)
                fill_edges(H, D + H)

                def gat_logits(r, t0):
                    ed = edges_d[0:NP, bass.ds(t0 * H, L * H)].rearrange("p (t h) -> p h t", h=H)
                    vec.tensor_tensor(logit[:, :, :], r[:, :, D:D + H].rearrange("p t h -> p h t"), ed, ALU.add)\
                        .then_inc(vec_done, 1)
                    settle()
                    vec.scalar_tensor_tensor(logit[:, :, :], logit[:, :, :], 0.2, logit[:, :, :], ALU.mult, ALU.max)\
                        .then_inc(vec_done, 1)
                    settle()

                softmax_pass("gat", gat_logits)
                for m, js in enumerate(BLOCK_OF):
                    block_in(m)
                    num, rd = divide(H, js)
                    vec.tensor_tensor(aggn[:, js, :].rearrange("p j (h f) -> p j h f", h=H), num, rd, ALU.mult)\
                        .then_inc(block_ready, 1)
                vec.wait_ge(group_copied, group_n.up(3 * len(GROUPS)))
                vec.wait_ge(act_for_vec, act_n.up())
                vec.tensor_tensor(work[:, :, :], aggn[:, :, 0:D], aggn[:, :, 3 * D:4 * D], ALU.mult)\
                    .then_inc(vec_done, 1)
                settle()
                vec.tensor_tensor(work[:, :, :], work[:, :, :], aggn[:, :, 2 * D:3 * D], ALU.add)\
                    .then_inc(vec_for_act, 1)
                vec.wait_ge(act_for_vec, act_n.up())
                vec.tensor_tensor(work2[:, :, :], X[:, :, :], work[:, :, :], ALU.subtract).then_inc(vec_done, 1)
                settle()
                vec.tensor_tensor(work2[:, :, :], work2[:, :, :], aggn[:, :, D:2 * D], ALU.mult).then_inc(vec_done, 1)
                settle()
                vec.tensor_tensor(work[:, :, :], work[:, :, :], work2[:, :, :], ALU.add).then_inc(vec_done, 1)
                settle()
                vec.tensor_scalar(work2[:, :, :], work[:, :, :], 0.0, None, ALU.min).then_inc(vec_for_act, 1)
                vec.wait_ge(act_for_vec, act_n.up())
                vec.scalar_tensor_tensor(work[:, :, :], work[:, :, :], 0.0, work2[:, :, :], ALU.max, ALU.add)\
                    .then_inc(vec_done, 1)
                settle()
                vec.scalar_tensor_tensor(X[:, :, :], work[:, :, :], -1.0, X[:, :, :], ALU.add, ALU.add)\
                    .then_inc(vec_done, 1)
                settle()
                layer_norm()

                vec.tensor_tensor(tabD, X[:, :, :], over(per_node(DINV), D), ALU.mult).then_inc(vec_for_sync, 1)
                vec.tensor_copy(aggn[:, :, 0:D], X[:, :, :])
                begin_pass("cheb0", tabD, 2)
                sum_pass("cheb0")
                for m in range(J // LS):
                    block_in(m)
                vec.tensor_tensor(work[:, :, :], agg[0:NP, :, 0:D], over(per_node(DSOME), D), ALU.mult)
                vec.tensor_scalar(work2[:, :, :], X[:, :, :], scal[:, 4:5], None, ALU.mult).then_inc(vec_done, 1)
                settle()
                vec.scalar_tensor_tensor(aggn[:, :, D:2 * D], work[:, :, :], scal[:, 3:4], work2[:, :, :],
                                         ALU.mult, ALU.add).then_inc(vec_done, 1)
                settle()
                vec.tensor_tensor(tabD, aggn[:, :, D:2 * D], over(per_node(DINV), D), ALU.mult)\
                    .then_inc(vec_for_sync, 1)
                begin_pass("cheb1", tabD, 3)
                sum_pass("cheb1")
                vec.memset(bigT[3 * D:3 * D + 1, :], 1.0)
                vec.scalar_tensor_tensor(work2[:, :, :], aggn[:, :, D:2 * D], scal[:, 6:7], X[:, :, :],
                                         ALU.mult, ALU.subtract).then_inc(vec_done, 1)
                settle()
                for m, js in enumerate(BLOCK_OF):
                    block_in(m)
                    vec.tensor_tensor(work[:, js, :], agg[0:NP, js, 0:D], over(per_node(DSOME, js), D), ALU.mult)\
                        .then_inc(vec_done, 1)
                    settle()
                    vec.scalar_tensor_tensor(aggn[:, js, 2 * D:3 * D], work[:, js, :], scal[:, 5:6], work2[:, js, :],
                                             ALU.mult, ALU.add).then_inc(block_ready, 1)
                vec.wait_ge(group_copied, group_n.up(3 * len(GROUPS)))
                vec.tensor_copy(tabD, aggn[:, :, 0:D]).then_inc(vec_for_sync, 1)
                vec.tensor_copy(scat[0:NP, :, :], aggn[:, :, D:2 * D]).then_inc(vec_for_sync, 1)
                begin_pass("gatv2", tabD, 5)
                fill_edges(D, 0)

                def gatv2_logits(r, t0):
                    ed = edges_d[0:NP, bass.ds(t0 * D, L * D)].rearrange("p (t c) -> p t c", c=D)
                    vec.tensor_tensor(prod[:, :, :], r, ed, ALU.add).then_inc(vec_done, 1)
                    settle()
                    vec.scalar_tensor_tensor(prod[:, :, :], prod[:, :, :], 0.2, prod[:, :, :], ALU.mult, ALU.max)\
                        .then_inc(vec_done, 1)
                    settle()
                    vec.tensor_tensor(prod[:, :, :], prod[:, :, :], att1[:, :].unsqueeze(1).broadcast_to([NP, L, D]),
                                      ALU.mult).then_inc(vec_done, 1)
                    settle()
                    vec.tensor_reduce(logit[:, 0, :], prod[:, :, :], X_AXIS, ALU.add).then_inc(vec_done, 1)
                    settle()

                softmax_pass("gatv2", gatv2_logits)
                for m, js in enumerate(BLOCK_OF):
                    block_in(m)
                    num, rd = divide(1, js)
                    vec.tensor_tensor(work[:, js, :], num[:, :, 0, :], rd[:, :, 0, :], ALU.mult).then_inc(vec_done, 1)
                    settle()
                    vec.tensor_tensor(X[:, js, :], X[:, js, :], work[:, js, :], ALU.add).then_inc(vec_done, 1)
                    settle()
                    layer_norm(block_ready, js)

                vec.tensor_scalar(coord, attr[:, :, :].rearrange("p t d -> p d t"), 1.0 / WIDTH, None, ALU.mult)\
                    .then_inc(vec_done, 1)
                settle()
                vec.tensor_scalar(cell, coord, -0.5, -1.5, ALU.is_ge, ALU.add).then_inc(vec_done, 1)
                settle()
                vec.scalar_tensor_tensor(cell, coord, 0.5, cell, ALU.is_ge, ALU.add).then_inc(vec_done, 1)
                settle()
                vec.scalar_tensor_tensor(offset[:, 0, :], cell[:, 1, :], float(CELLS), cell[:, 0, :],
                                         ALU.mult, ALU.add).then_inc(vec_done, 1)
                settle()
                vec.scalar_tensor_tensor(offset[:, 0, :], dst_i[:, :], float(CELLS * CELLS), offset[:, 0, :],
                                         ALU.mult, ALU.add).then_inc(vec_done, 1)
                settle()
                vec.tensor_scalar(cell_i, offset[:, 0, :], 1.5 * (CELLS + 1), None, ALU.add).then_inc(cells_made, 1)
                vec.tensor_tensor(tents[:, :, 0, :], coord, cell, ALU.subtract).then_inc(vec_done, 1)
                settle()
                vec.tensor_scalar(tents[:, :, 1, :], tents[:, :, 0, :], -1.0, None, ALU.add).then_inc(vec_done, 1)
                settle()
                vec.scalar_tensor_tensor(tents, tents, -1.0, tents, ALU.mult, ALU.max).then_inc(vec_done, 1)
                settle()
                vec.tensor_scalar(tents, tents, -1.0, 1.0, ALU.mult, ALU.add).then_inc(vec_done, 1)
                settle()
                vec.tensor_scalar(tents, tents, 0.0, None, ALU.max).then_inc(vec_done, 1)
                settle()
                for a in range(2):
                    for b in range(2):
                        ins = vec.tensor_tensor(basis[:, :, 2 * a + b], tents[:, 0, a, :], tents[:, 1, b, :], ALU.mult)
                ins.then_inc(vec_done, 1)
                settle()
                for b in range(2):
                    vec.wait_ge(scan_stored[b], len(ORDER[:-1]) * SLOT * ((CH + 1 - b) // 2))
                slot_n = [Count() for c in range(SLOTS)]
                hot_used = Count()

                def spline_turn(t0, first):
                    if not first:
                        vec.wait_ge(onehot_ready, made.at())
                        vec.wait_ge(act_onehot_ready, act_made.at())
                    now = src_f[:, bass.ds(t0, L)]
                    vec.tensor_scalar(srcc[:, :, :].rearrange("p s t -> p (s t)"), now, 1.0, None, ALU.mult)
                    vec.tensor_scalar(srcc_neg[:, :, :].rearrange("p s t -> p (s t)"), now, -1.0, None, ALU.mult)\
                        .then_inc(sources_ready, 1)
                    for c in range(SLOTS):
                        slot = slots[0:NP, c, :].rearrange("p (t k f) -> p t k f", k=CORNERS, f=D)
                        msg = prod[:, c * LS:(c + 1) * LS, :]
                        high, mid, low = (parts[:, c, :, i * D:(i + 1) * D] for i in range(3))

                        def one_hot(t):
                            hot_used.up()
                            if (c, t) in ACT_HOT:
                                act_made.up()
                                return
                            made.up()
                            if not first or c >= HOT_LAG[c]:
                                vec.wait_ge(onehot_used, hot_used.at(-HOT_LAG[c] * LS))
                            vec.tensor_scalar(hots[c % 2][t], nodes16[:, :], srcc[:, c, t:t + 1], None, ALU.is_equal)\
                                .then_inc(onehot_ready, 1)

                        vec.wait_ge(slot_in[c], slot_n[c].up(SLOT * LS))
                        vec.tensor_tensor(slot, slot, over(basis[:, bass.ds(t0 + c * LS, LS), :], D), ALU.mult)\
                            .then_inc(vec_done, 1)
                        if c == 0:
                            vec.wait_ge(sources_ready, sources_n.up())
                        one_hot(0)
                        settle()
                        vec.tensor_reduce(msg, slot.rearrange("p t k f -> p t f k"), X_AXIS, ALU.add)\
                            .then_inc(slot_used, 1)
                        slots_n.up()
                        one_hot(1)
                        vec.wait_ge(slot_used, slots_n.at())
                        vec.tensor_copy(high, msg).then_inc(vec_done, 1)
                        one_hot(2)
                        settle()
                        vec.tensor_tensor(msg, msg, high, ALU.subtract).then_inc(vec_done, 1)
                        one_hot(3)
                        settle()
                        vec.tensor_copy(mid, msg).then_inc(vec_done, 1)
                        settle()
                        vec.tensor_tensor(msg, msg, mid, ALU.subtract).then_inc(vec_done, 1)
                        settle()
                        vec.tensor_copy(low, msg).then_inc(parts_ready, 1)
                        one_hot(4)

                slots_n, made, act_made, sources_n = Count(), Count(), Count(), Count()
                before = own.n
                vec.wait_ge(nodes16_made, 1)
                spline_turn(0, True)
                with vec.Fori(0, CH - 1) as turn:
                    per_turn = [(slots_n, SLOTS), (sources_n, 1), (made, L - len(ACT_HOT)),
                                (act_made, len(ACT_HOT)), (hot_used, L), (own, own.n - before)] + \
                        [(c, SLOT * LS) for c in slot_n]
                    for c, per in per_turn:
                        c.enter(turn, per)
                    spline_turn(turn * L + L, False)
                for c, per in per_turn:
                    c.leave(CH - 1)
                vec.wait_ge(onehot_used, T)
                vec.tensor_copy(bigT[0:3 * D, :], ps[0:3 * D, 0:7, :].rearrange("p n c -> p (n c)")[:, 0:N])\
                    .then_inc(vec_for_pe, 1)
                vec.wait_ge(group_copied, group_n.up(2 * len(GROUPS) + J))
                vec.tensor_tensor(X[:, :, :], X[:, :, :], work2[:, :, :], ALU.add).then_inc(vec_done, 1)
                settle()
                layer_norm()

                vec.tensor_tensor(work[:, :, :], X[:, :, :], X[:, :, :], ALU.mult).then_inc(vec_done, 1)
                settle()
                vec.tensor_reduce(per_node(RSTD), work[:, :, :], X_AXIS, ALU.add).then_inc(vec_for_act, 1)
                vec.wait_ge(act_for_vec, act_n.up())
                vec.tensor_scalar(per_node(RN), per_node(RSTD), NORM_EPS, None, ALU.max).then_inc(vec_done, 1)
                settle()
                vec.reciprocal(per_node(RN), per_node(RN)).then_inc(vec_done, 1)
                settle()
                vec.tensor_copy(tabG[:, :, 0:D], X[:, :, :])
                vec.tensor_copy(tabG[:, :, D:HG], over(per_node(RN), 1)).then_inc(vec_for_sync, 1)
                vec.tensor_tensor(scat[0:NP, :, :], X[:, :, :], over(per_node(RN), D), ALU.mult)\
                    .then_inc(vec_for_sync, 1)
                vec.wait_ge(vec_for_sync, 7)
                vec.tensor_tensor(work[:, :, :], scat[0:NP, :, :], scat[0:NP, :, :], ALU.mult).then_inc(vec_done, 1)
                settle()
                vec.tensor_reduce(per_node(TMP), work[:, :, :], X_AXIS, ALU.add).then_inc(vec_done, 1)
                settle()
                vec.tensor_scalar(per_node(SELF), per_node(TMP), scal[:, 1:2], None, ALU.mult)
                begin_pass("agnn", tabG, 7)
                fill_edges(D, 0)

                def agnn_logits(r, t0):
                    ed = edges_d[0:NP, bass.ds(t0 * D, L * D)].rearrange("p (t c) -> p t c", c=D)
                    vec.tensor_tensor(prod[:, :, :], r[:, :, 0:D], ed, ALU.mult).then_inc(vec_done, 1)
                    settle()
                    vec.tensor_reduce(logit[:, 0, :], prod[:, :, :], X_AXIS, ALU.add).then_inc(vec_done, 1)
                    settle()
                    vec.scalar_tensor_tensor(logit[:, 0, :], logit[:, 0, :], scal[:, 1:2], r[:, :, D],
                                             ALU.mult, ALU.mult).then_inc(vec_done, 1)
                    settle()

                softmax_pass("agnn", agnn_logits)
                for m, js in enumerate(BLOCK_OF):
                    block_in(m)
                    vec.tensor_tensor(per_node(TMP, js), agg[0:NP, js, HG], per_node(SOME, js), ALU.mult)
                    vec.tensor_scalar(per_node(MEAN, js), per_node(SOME, js), -1.0, BIG, ALU.add, ALU.mult)\
                        .then_inc(vec_done, 1)
                    settle()
                    vec.tensor_tensor(per_node(TMP, js), per_node(TMP, js), per_node(MEAN, js), ALU.add)\
                        .then_inc(vec_done, 1)
                    settle()
                    vec.tensor_tensor(per_node(MEAN, js), per_node(TMP, js), per_node(SELF, js), ALU.max)\
                        .then_inc(vec_done, 1)
                    settle()
                    vec.tensor_tensor(nodew[:, 0, js], per_node(TMP, js), per_node(MEAN, js), ALU.subtract)
                    vec.tensor_tensor(nodew[:, 1, js], per_node(SELF, js), per_node(MEAN, js), ALU.subtract)\
                        .then_inc(vec_for_act, 1)
                    vec.wait_ge(act_for_vec, act_n.up())
                    vec.tensor_tensor(work[:, js, :], agg[0:NP, js, 0:D], over(nodew[:, 0, js], D), ALU.mult)
                    vec.tensor_tensor(work2[:, js, :], X[:, js, :], over(nodew[:, 1, js], D), ALU.mult)
                    vec.tensor_tensor(per_node(TMP, js), agg[0:NP, js, D], nodew[:, 0, js], ALU.mult)\
                        .then_inc(vec_done, 1)
                    settle()
                    vec.tensor_tensor(work[:, js, :], work[:, js, :], work2[:, js, :], ALU.add)
                    vec.tensor_tensor(per_node(TMP, js), per_node(TMP, js), nodew[:, 1, js], ALU.add)\
                        .then_inc(vec_done, 1)
                    settle()
                    vec.tensor_scalar(per_node(TMP, js), per_node(TMP, js), NORM_EPS, None, ALU.max)\
                        .then_inc(vec_done, 1)
                    settle()
                    vec.reciprocal(per_node(TMP, js), per_node(TMP, js)).then_inc(vec_done, 1)
                    settle()
                    vec.tensor_tensor(work[:, js, :], work[:, js, :], over(per_node(TMP, js), D), ALU.mult)\
                        .then_inc(vec_done, 1)
                    settle()
                    vec.scalar_tensor_tensor(work[:, js, :], work[:, js, :], 0.0, X[:, js, :], ALU.max, ALU.add)\
                        .then_inc(vec_done, 1)
                    settle()
                    vec.tensor_tensor(X[:, js, :], X[:, js, :], work[:, js, :], ALU.add).then_inc(vec_done, 1)
                    settle()
                    layer_norm(vec_for_sync, js)


_INS = ["x", "src", "dst", "edge_attr_2", "L0_gnn_W_gat", "L0_gnn_attn_l", "L0_gnn_attn_r", "L0_gnn_W_ih",
        "L0_gnn_W_hh", "L0_gnn_b_ih", "L0_gnn_b_hh", "L1_gnn_lambda_max", "L1_gnn_cheb_W", "L1_gnn_cheb_b",
        "L1_gnn_src_W", "L1_gnn_src_b", "L1_gnn_dst_W", "L1_gnn_dst_b", "L1_gnn_attn", "L2_gnn_weight",
        "L3_gnn_beta"]


def kernel(**inputs):
    import numpy as np
    import concourse.bacc as bacc
    from concourse import mybir as mb
    from concourse.bass_utils import run_bass_kernel_spmd

    nc = bacc.Bacc("TRN2", target_bir_lowering=False, num_devices=1)
    arrays, args = {}, []
    for name in _INS:
        a = np.ascontiguousarray(inputs[name])
        arrays[f"in_{name}"] = a
        args.append(nc.dram_tensor(f"in_{name}", a.shape, mb.dt.from_np(a.dtype), kind="ExternalInput").ap())
    shape = inputs["x"].shape
    out = nc.dram_tensor("out", shape, mb.dt.float32, kind="ExternalOutput").ap()
    gnn_kernel(nc, *args, out)
    r = run_bass_kernel_spmd(nc, [arrays], core_ids=[0])
    return r.results[0]["out"]
```
